# Optimizing a Trainium2 kernel written in Bass

```python
import numpy as np
import jax
import jax.numpy as jnp

def _softmax(x, axis=-1):
    return jax.nn.softmax(x, axis=axis)

def _gelu(x):
    return jax.nn.gelu(x, approximate=True)

def _silu(x):
    return jax.nn.silu(x)

def _sigmoid(x):
    return jax.nn.sigmoid(x)

def _layernorm(x, axis=-1, eps=1e-05):
    m = jnp.mean(x, axis=axis, keepdims=True)
    v = jnp.var(x, axis=axis, keepdims=True)
    return (x - m) / jnp.sqrt(v + eps)

def _scatter_add(tgt, idx, src, axis=0):
    return tgt.at[idx].add(src)

def _segment_sum(src, seg, n):
    return jax.ops.segment_sum(src, seg, n)
kernel_name = 'mk_adj_resnorm_d4_adj_r2_f63abd'

def setup_inputs(seed: int=0):
    np.random.seed(seed)
    _w = jnp.asarray

    def _rec_inputs():
        import jax
        import jax.numpy as jnp
        _gk = jax.random.key(seed)
        x = -0.000929 + 1 * jax.random.normal(jax.random.fold_in(_gk, 1), (4096, 128), jnp.float32)
        _w = (1.0 + jnp.arange(4096, dtype=jnp.float32)) ** (-0.5)
        _w = _w / _w.mean()
        _pij = jnp.clip(0.00195312 * _w[:, None] * _w[None, :], 0.0, 1.0)
        _a = jax.random.uniform(jax.random.fold_in(_gk, 2), (4096, 4096)) < _pij
        _a = jnp.logical_or(_a, jnp.eye(4096, dtype=bool))
        _af = _a.astype(jnp.float32)
        _af = _af / jnp.maximum(_af.sum(-1, keepdims=True), 1.0)
        adj = _af
        return (x, adj)
    x, adj = _rec_inputs()

    def _L0_gnn_setup():
        import jax, jax.numpy as jnp
        import numpy as np
        from jax import lax
        D_MODEL = 128
        D_STATE = 16
        D_CONV = 4
        EXPAND = 2
        D_INNER = EXPAND * D_MODEL
        DT_RANK = (D_MODEL + 15) // 16
        N = 2048
        EPS = 1e-05

        def _mamba(h, w_in, conv_w, conv_b, w_xp, w_dt, b_dt, A_log, D_skip, w_out):
            L = h.shape[0]
            xz = h @ w_in
            xc, z = (xz[:, :D_INNER], xz[:, D_INNER:])
            xpad = jnp.pad(xc, ((D_CONV - 1, 0), (0, 0)))
            xconv = sum((xpad[k:k + L] * conv_w[:, k] for k in range(D_CONV))) + conv_b
            u = jax.nn.silu(xconv)
            dbc = u @ w_xp
            dt = jax.nn.softplus(dbc[:, :DT_RANK] @ w_dt + b_dt)
            B = dbc[:, DT_RANK:DT_RANK + D_STATE]
            C = dbc[:, DT_RANK + D_STATE:]
            A = -jnp.exp(A_log)
            dA = jnp.exp(dt[:, :, None] * A[None])
            dBu = dt[:, :, None] * B[:, None, :] * u[:, :, None]

            def step(hst, inp):
                dAt, dBut, Ct = inp
                hst = dAt * hst + dBut
                return (hst, hst @ Ct)
            _, ys = lax.scan(step, jnp.zeros((D_INNER, D_STATE), h.dtype), (dA, dBu, C))
            y = ys + u * D_skip
            y = y * jax.nn.silu(z)
            return y @ w_out
        key = jax.random.key(seed)
        ks = jax.random.split(key, 16)
        x = jax.random.normal(ks[0], (N, D_MODEL), dtype=jnp.float32)
        a = jax.random.uniform(ks[1], (N, N), dtype=jnp.float32)
        adj = a / a.sum(axis=1, keepdims=True)
        s = lambda fi, fo: 1.0 / np.sqrt(fi)
        gcn_w = jax.random.uniform(ks[2], (D_MODEL, D_MODEL), jnp.float32, -s(D_MODEL, 0), s(D_MODEL, 0))
        gcn_b = jnp.zeros((D_MODEL,), jnp.float32)
        ln_g = jnp.ones((D_MODEL,), jnp.float32)
        ln_b = jnp.zeros((D_MODEL,), jnp.float32)
        w_in = jax.random.normal(ks[3], (D_MODEL, 2 * D_INNER), jnp.float32) * s(D_MODEL, 0)
        conv_w = jax.random.normal(ks[4], (D_INNER, D_CONV), jnp.float32) * s(D_CONV, 0)
        conv_b = jnp.zeros((D_INNER,), jnp.float32)
        w_xp = jax.random.normal(ks[5], (D_INNER, DT_RANK + 2 * D_STATE), jnp.float32) * s(D_INNER, 0)
        w_dt = jax.random.normal(ks[6], (DT_RANK, D_INNER), jnp.float32) * s(DT_RANK, 0)
        b_dt = jnp.log(jnp.expm1(jnp.exp(jax.random.uniform(ks[7], (D_INNER,), jnp.float32, np.log(0.001), np.log(0.1)))))
        A_log = jnp.log(jnp.broadcast_to(jnp.arange(1, D_STATE + 1, dtype=jnp.float32), (D_INNER, D_STATE)))
        D_skip = jnp.ones((D_INNER,), jnp.float32)
        w_out = jax.random.normal(ks[8], (D_INNER, D_MODEL), jnp.float32) * s(D_INNER, 0)
        return dict(x=x, adj=adj, gcn_w=gcn_w, gcn_b=gcn_b, ln_g=ln_g, ln_b=ln_b, w_in=w_in, conv_w=conv_w, conv_b=conv_b, w_xp=w_xp, w_dt=w_dt, b_dt=b_dt, A_log=A_log, D_skip=D_skip, w_out=w_out)
    _L0_gnn_all = _L0_gnn_setup()
    _L0_gnn_in = {k: v for k, v in _L0_gnn_all.items() if k in ('gcn_w', 'gcn_b', 'ln_g', 'ln_b', 'w_in', 'conv_w', 'conv_b', 'w_xp', 'w_dt', 'b_dt', 'A_log', 'D_skip', 'w_out')}
    del _L0_gnn_all

    def _L1_gnn_setup():
        import jax, jax.numpy as jnp
        import numpy as np
        N, IN_C, OUT_C, HEADS = (4096, 128, 128, 4)
        FPH = OUT_C // HEADS
        LEAKY = 0.2
        key = jax.random.key(seed)
        k1, k2, k3, k4, k5 = jax.random.split(key, 5)
        x = jax.random.normal(k1, (N, IN_C), dtype=jnp.float32)
        u = jax.random.uniform(k2, (N, N), dtype=jnp.float32)
        P_soft = jnp.where(u > 0.5, u, 0.0)
        W = jax.random.normal(k3, (IN_C, OUT_C), dtype=jnp.float32) * (1.0 / np.sqrt(IN_C))
        a_src = jax.random.normal(k4, (HEADS, FPH), dtype=jnp.float32) * 0.1
        a_dst = jax.random.normal(k5, (HEADS, FPH), dtype=jnp.float32) * 0.1
        return {'x': x, 'P_soft': P_soft, 'W': W, 'a_src': a_src, 'a_dst': a_dst}
    _L1_gnn_all = _L1_gnn_setup()
    _L1_gnn_in = {k: v for k, v in _L1_gnn_all.items() if k in ('W', 'a_src', 'a_dst')}
    del _L1_gnn_all

    def _L2_gnn_setup():
        import jax, jax.numpy as jnp
        import numpy as np
        N = 4096
        D_IN = 128
        D_OUT = 128
        key = jax.random.key(seed)
        k1, k2, k3 = jax.random.split(key, 3)
        x = jax.random.normal(k1, (N, D_IN), dtype=jnp.float32)
        adj = jax.random.uniform(k2, (N, N), dtype=jnp.float32)
        W = jax.random.normal(k3, (D_OUT, D_IN), dtype=jnp.float32) * (1.0 / np.sqrt(D_IN))
        return {'x': x, 'adj': adj, 'W': W}
    _L2_gnn_all = _L2_gnn_setup()
    _L2_gnn_in = {k: v for k, v in _L2_gnn_all.items() if k in ('W',)}
    del _L2_gnn_all

    def _L3_gnn_setup():
        import jax, jax.numpy as jnp
        import numpy as np
        MIN_NORM = 1e-15
        BALL_EPS = 1e-05
        C_IN = 1.0
        C_OUT = 1.0

        def _artanh(x):
            x = jnp.clip(x, -1.0 + 1e-07, 1.0 - 1e-07)
            return 0.5 * (jnp.log1p(x) - jnp.log1p(-x))

        def _norm(x):
            return jnp.maximum(jnp.linalg.norm(x, axis=-1, keepdims=True), MIN_NORM)

        def proj(x, c):
            norm = _norm(x)
            maxnorm = (1.0 - BALL_EPS) / jnp.sqrt(c)
            return jnp.where(norm > maxnorm, x / norm * maxnorm, x)

        def expmap0(u, c):
            sc = jnp.sqrt(c)
            un = _norm(u)
            return jnp.tanh(sc * un) * u / (sc * un)

        def logmap0(p, c):
            sc = jnp.sqrt(c)
            pn = _norm(p)
            return _artanh(sc * pn) * p / (sc * pn)

        def mobius_matvec(m, x, c):
            sc = jnp.sqrt(c)
            xn = _norm(x)
            mx = x @ m.T
            mxn = _norm(mx)
            res = jnp.tanh(mxn / xn * _artanh(sc * xn)) * mx / (mxn * sc)
            zero_row = jnp.all(mx == 0, axis=-1, keepdims=True)
            return jnp.where(zero_row, jnp.zeros((), dtype=res.dtype), res)

        def mobius_add(x, y, c):
            x2 = jnp.sum(x * x, axis=-1, keepdims=True)
            y2 = jnp.sum(y * y, axis=-1, keepdims=True)
            xy = jnp.sum(x * y, axis=-1, keepdims=True)
            num = (1.0 + 2.0 * c * xy + c * y2) * x + (1.0 - c * x2) * y
            denom = 1.0 + 2.0 * c * xy + c * c * x2 * y2
            return num / jnp.maximum(denom, MIN_NORM)
        key = jax.random.key(seed)
        k1, k2, k3, k4 = jax.random.split(key, 4)
        N, D_IN, D_OUT = (4096, 128, 128)
        x = proj(0.05 * jax.random.normal(k1, (N, D_IN), dtype=jnp.float32), C_IN)
        adj = jax.random.uniform(k2, (N, N), dtype=jnp.float32)
        adj = adj / jnp.sum(adj, axis=1, keepdims=True)
        bound = np.sqrt(2.0) * np.sqrt(6.0 / (D_IN + D_OUT))
        weight = jax.random.uniform(k3, (D_OUT, D_IN), dtype=jnp.float32, minval=-bound, maxval=bound)
        bias = 0.01 * jax.random.normal(k4, (D_OUT,), dtype=jnp.float32)
        return {'x': x, 'adj': adj, 'weight': weight, 'bias': bias}
    _L3_gnn_all = _L3_gnn_setup()
    _L3_gnn_in = {k: v for k, v in _L3_gnn_all.items() if k in ('weight', 'bias')}
    del _L3_gnn_all
    return {'x': x, 'adj': adj, 'L0_gnn_gcn_w': _L0_gnn_in['gcn_w'], 'L0_gnn_gcn_b': _L0_gnn_in['gcn_b'], 'L0_gnn_ln_g': _L0_gnn_in['ln_g'], 'L0_gnn_ln_b': _L0_gnn_in['ln_b'], 'L0_gnn_w_in': _L0_gnn_in['w_in'], 'L0_gnn_conv_w': _L0_gnn_in['conv_w'], 'L0_gnn_conv_b': _L0_gnn_in['conv_b'], 'L0_gnn_w_xp': _L0_gnn_in['w_xp'], 'L0_gnn_w_dt': _L0_gnn_in['w_dt'], 'L0_gnn_b_dt': _L0_gnn_in['b_dt'], 'L0_gnn_A_log': _L0_gnn_in['A_log'], 'L0_gnn_D_skip': _L0_gnn_in['D_skip'], 'L0_gnn_w_out': _L0_gnn_in['w_out'], 'L1_gnn_W': _L1_gnn_in['W'], 'L1_gnn_a_src': _L1_gnn_in['a_src'], 'L1_gnn_a_dst': _L1_gnn_in['a_dst'], 'L2_gnn_W': _L2_gnn_in['W'], 'L3_gnn_weight': _L3_gnn_in['weight'], 'L3_gnn_bias': _L3_gnn_in['bias']}

def reference(x, adj, L0_gnn_gcn_w, L0_gnn_gcn_b, L0_gnn_ln_g, L0_gnn_ln_b, L0_gnn_w_in, L0_gnn_conv_w, L0_gnn_conv_b, L0_gnn_w_xp, L0_gnn_w_dt, L0_gnn_b_dt, L0_gnn_A_log, L0_gnn_D_skip, L0_gnn_w_out, L1_gnn_W, L1_gnn_a_src, L1_gnn_a_dst, L2_gnn_W, L3_gnn_weight, L3_gnn_bias):
    import jax
    import jax.numpy as jnp

    def _L0_gnn_ref(x, adj, gcn_w, gcn_b, ln_g, ln_b, w_in, conv_w, conv_b, w_xp, w_dt, b_dt, A_log, D_skip, w_out):
        import jax, jax.numpy as jnp
        import numpy as np
        from jax import lax
        D_MODEL = 128
        D_STATE = 16
        D_CONV = 4
        EXPAND = 2
        D_INNER = EXPAND * D_MODEL
        DT_RANK = (D_MODEL + 15) // 16
        N = 2048
        EPS = 1e-05

        def _mamba(h, w_in, conv_w, conv_b, w_xp, w_dt, b_dt, A_log, D_skip, w_out):
            L = h.shape[0]
            xz = h @ w_in
            xc, z = (xz[:, :D_INNER], xz[:, D_INNER:])
            xpad = jnp.pad(xc, ((D_CONV - 1, 0), (0, 0)))
            xconv = sum((xpad[k:k + L] * conv_w[:, k] for k in range(D_CONV))) + conv_b
            u = jax.nn.silu(xconv)
            dbc = u @ w_xp
            dt = jax.nn.softplus(dbc[:, :DT_RANK] @ w_dt + b_dt)
            B = dbc[:, DT_RANK:DT_RANK + D_STATE]
            C = dbc[:, DT_RANK + D_STATE:]
            A = -jnp.exp(A_log)
            dA = jnp.exp(dt[:, :, None] * A[None])
            dBu = dt[:, :, None] * B[:, None, :] * u[:, :, None]

            def step(hst, inp):
                dAt, dBut, Ct = inp
                hst = dAt * hst + dBut
                return (hst, hst @ Ct)
            _, ys = lax.scan(step, jnp.zeros((D_INNER, D_STATE), h.dtype), (dA, dBu, C))
            y = ys + u * D_skip
            y = y * jax.nn.silu(z)
            return y @ w_out
        h = jax.nn.relu(adj @ x @ gcn_w + gcn_b)
        mu = h.mean(-1, keepdims=True)
        var = h.var(-1, keepdims=True)
        h = (h - mu) * lax.rsqrt(var + EPS) * ln_g + ln_b
        return _mamba(h, w_in, conv_w, conv_b, w_xp, w_dt, b_dt, A_log, D_skip, w_out)

    def _L1_gnn_ref(x, P_soft, W, a_src, a_dst):
        import jax, jax.numpy as jnp
        import numpy as np
        N, IN_C, OUT_C, HEADS = (4096, 128, 128, 4)
        FPH = OUT_C // HEADS
        LEAKY = 0.2
        n = x.shape[0]
        h = (x @ W).reshape(n, HEADS, FPH)
        e_src = jnp.einsum('nhf,hf->nh', h, a_src)
        e_dst = jnp.einsum('nhf,hf->nh', h, a_dst)
        e = e_src[:, None, :] + e_dst[None, :, :]
        e = jax.nn.leaky_relu(e, negative_slope=LEAKY)
        mask = (P_soft > 0)[:, :, None]
        e = jnp.where(mask, e, -jnp.inf)
        attn = jax.nn.softmax(e, axis=1)
        attn = attn * P_soft[:, :, None]
        out = jnp.einsum('ijh,jhf->ihf', attn, h)
        return out.reshape(n, -1)

    def _L2_gnn_ref(x, adj, W):
        import jax, jax.numpy as jnp
        import numpy as np
        N = 4096
        D_IN = 128
        D_OUT = 128
        A_hat = adj + jnp.eye(adj.shape[0], dtype=adj.dtype)
        d_inv_sqrt = jnp.sum(A_hat, axis=1) ** (-0.5)
        A_norm = d_inv_sqrt[:, None] * A_hat * d_inv_sqrt[None, :]
        support = x @ W.T
        out = A_norm @ support
        return jax.nn.relu(out)

    def _L3_gnn_ref(x, adj, weight, bias):
        import jax, jax.numpy as jnp
        import numpy as np
        MIN_NORM = 1e-15
        BALL_EPS = 1e-05
        C_IN = 1.0
        C_OUT = 1.0

        def _artanh(x):
            x = jnp.clip(x, -1.0 + 1e-07, 1.0 - 1e-07)
            return 0.5 * (jnp.log1p(x) - jnp.log1p(-x))

        def _norm(x):
            return jnp.maximum(jnp.linalg.norm(x, axis=-1, keepdims=True), MIN_NORM)

        def proj(x, c):
            norm = _norm(x)
            maxnorm = (1.0 - BALL_EPS) / jnp.sqrt(c)
            return jnp.where(norm > maxnorm, x / norm * maxnorm, x)

        def expmap0(u, c):
            sc = jnp.sqrt(c)
            un = _norm(u)
            return jnp.tanh(sc * un) * u / (sc * un)

        def logmap0(p, c):
            sc = jnp.sqrt(c)
            pn = _norm(p)
            return _artanh(sc * pn) * p / (sc * pn)

        def mobius_matvec(m, x, c):
            sc = jnp.sqrt(c)
            xn = _norm(x)
            mx = x @ m.T
            mxn = _norm(mx)
            res = jnp.tanh(mxn / xn * _artanh(sc * xn)) * mx / (mxn * sc)
            zero_row = jnp.all(mx == 0, axis=-1, keepdims=True)
            return jnp.where(zero_row, jnp.zeros((), dtype=res.dtype), res)

        def mobius_add(x, y, c):
            x2 = jnp.sum(x * x, axis=-1, keepdims=True)
            y2 = jnp.sum(y * y, axis=-1, keepdims=True)
            xy = jnp.sum(x * y, axis=-1, keepdims=True)
            num = (1.0 + 2.0 * c * xy + c * y2) * x + (1.0 - c * x2) * y
            denom = 1.0 + 2.0 * c * xy + c * c * x2 * y2
            return num / jnp.maximum(denom, MIN_NORM)
        h = proj(mobius_matvec(weight, x, C_IN), C_IN)
        hyp_bias = proj(expmap0(bias[None, :], C_IN), C_IN)
        h = proj(mobius_add(h, hyp_bias, C_IN), C_IN)
        x_tangent = logmap0(h, C_IN)
        support_t = adj @ x_tangent
        h = proj(expmap0(support_t, C_IN), C_IN)
        xt = jax.nn.relu(logmap0(h, C_IN))
        return proj(expmap0(xt, C_OUT), C_OUT)
    x = _layernorm(x + _L0_gnn_ref(x, adj, L0_gnn_gcn_w, L0_gnn_gcn_b, L0_gnn_ln_g, L0_gnn_ln_b, L0_gnn_w_in, L0_gnn_conv_w, L0_gnn_conv_b, L0_gnn_w_xp, L0_gnn_w_dt, L0_gnn_b_dt, L0_gnn_A_log, L0_gnn_D_skip, L0_gnn_w_out), axis=-1)
    x = _layernorm(x + _L1_gnn_ref(x, adj, L1_gnn_W, L1_gnn_a_src, L1_gnn_a_dst), axis=-1)
    x = _layernorm(x + _L2_gnn_ref(x, adj, L2_gnn_W), axis=-1)
    x = _layernorm(x + _L3_gnn_ref(x, adj, L3_gnn_weight, L3_gnn_bias), axis=-1)
    return x

_drawn_inputs = setup_inputs


def setup_inputs(seed=0):
    import zlib

    import numpy as np

    out = dict(_drawn_inputs(seed))
    spreads = {'L0_gnn_gcn_b': (0.0, 0.1),
     'L0_gnn_ln_g': (1.0, 0.2),
     'L0_gnn_ln_b': (0.0, 0.1),
     'L0_gnn_conv_b': (0.0, 0.1),
     'L0_gnn_D_skip': (1.0, 0.2)}
    factors = {}
    for name, (base, spread) in spreads.items():
        noise = np.random.default_rng([zlib.crc32(name.encode()), seed]).standard_normal(out[name].shape)
        drawn = base * np.exp(spread * noise) if base else spread * noise
        out[name] = jnp.asarray(drawn.astype(out[name].dtype))
    for name, factor in factors.items():
        out[name] = (out[name] * factor).astype(out[name].dtype)
    return out
```

```python
from contextlib import ExitStack

import numpy as np

import concourse.bass as bass
from concourse import mybir

F32 = mybir.dt.float32
BF16 = mybir.dt.bfloat16
FP8 = mybir.dt.float8e4
U8 = mybir.dt.uint8
U32 = mybir.dt.uint32
ALU = mybir.AluOpType
ACT = mybir.ActivationFunctionType
AX_X = mybir.AxisListType.X

P = 128
N = 4096
D = 128
NT = N // P
BANK = 512
EPS = 1e-5

DI = 256
KD = DI // P
S_N = 16
RANK = 8
TAPS = 4
T0 = 512
C0 = N // T0
Q0 = T0 // P
STEPS = KD * S_N
RATE0 = 54
N_DA, N_DBU, N_H, N_CS, N_HC = 3, 3, 4, 3, 4
HC_CREDIT = KD * N_CS
DBU_CREDIT = 2 * KD
Y_LAG = 4

HEADS = 4
F = D // HEADS
T1 = 1024
C1 = N // T1
Q1 = T1 // P
PARTS = 3
N_W, N_S = 2, 2
LEAKY = 0.2
E_MAX = 60.0
RATE2 = 10
RATE3 = 29
R_MAX = np.float32(np.exp(E_MAX))
RATE1 = 44
L1_LN = C0
MIN_SQ = 1e-30
MAX_NORM = 1.0 - 1e-5
ATANH_MAX = 1.0 - 1e-7

RING = 8
LOADS = NT * N // T1


class Link:

    def __init__(self, eng, sem):
        self.eng, self.sem, self.start, self.k, self.origin = eng, sem, 0, 0, 0

    def body(self, c, rate):
        self.origin, self.k, self.rate = self.start + rate * c, 0, rate

    def leave(self, rounds):
        assert self.k == self.rate, f"the rate of {self.sem} is {self.k}"
        self.start += self.rate * rounds
        self.origin, self.k = self.start, 0

    def mark(self, ins):
        ins.then_inc(self.sem, 1)
        self.k += 1
        return self.k

    def wait(self, k=None):
        self.eng.wait_ge(self.sem, self.origin + (self.k if k is None else k))

    def __call__(self, ins):
        self.mark(ins)
        self.wait()

    def straight(self):
        self.start += self.k
        self.origin, self.k = self.start, 0


def build_program(nc, t, out, stop=4):
    adj_t = t["adj_t"]
    ctx = ExitStack()
    with ctx:
        sems = {}

        def sem(name):
            if name not in sems:
                sems[name] = ctx.enter_context(nc.semaphore(name))
            return sems[name]

        def sb(stack, name, shape, dt=F32):
            return stack.enter_context(nc.sbuf_tensor(name, shape, dt))

        ring = sb(ctx, "ring", [P, RING, T1])
        xa = sb(ctx, "xa", [P, NT, D])
        xb = sb(ctx, "xb", [P, NT, D])
        ident = sb(ctx, "ident", [P, P])
        half_neg = sb(ctx, "half_neg", [P, NT])
        half_pos = sb(ctx, "half_pos", [P, NT])
        eps = sb(ctx, "eps", [P, Q1])
        w1 = sb(ctx, "w1", [P, D])
        w1_t = sb(ctx, "w1_t", [P, D])
        a_bd = sb(ctx, "a_bd", [P, 2 * HEADS])
        w2_t = sb(ctx, "w2_t", [P, D])
        w3_t = sb(ctx, "w3_t", [P, D])
        bias3 = sb(ctx, "bias3", [P, D])
        sel = sb(ctx, "sel", [P, 2, P])
        deg = sb(ctx, "deg", [P, NT])
        ln_st = sb(ctx, "ln_st", [P, Q1, 6])
        ln_mv = sb(ctx, "ln_mv", [P, Q1, 2])
        ln_rs = sb(ctx, "ln_rs", [P, Q1])
        ps = ctx.enter_context(nc.psum_tensor("ps", [P, 8, BANK], F32))

        with ExitStack() as l0:
            gcn_w = sb(l0, "gcn_w", [P, D])
            gcn_b = sb(l0, "gcn_b", [P, D])
            ln_g = sb(l0, "ln_g", [P, 1])
            ln_b = sb(l0, "ln_b", [P, 1])
            w_in = sb(l0, "w_in", [P, 2 * DI])
            conv_w = sb(l0, "conv_w", [P, KD, TAPS])
            conv_b = sb(l0, "conv_b", [P, KD])
            w_bc = sb(l0, "w_bc", [P, KD, 3 * 32])
            w_r = sb(l0, "w_r", [P, KD, RANK])
            w_dt = sb(l0, "w_dt", [RANK, DI])
            b_dt = sb(l0, "b_dt", [P, KD])
            a_neg = sb(l0, "a_neg", [P, KD, S_N])
            d_skip = sb(l0, "d_skip", [P, KD])
            w_out = sb(l0, "w_out", [P, KD, D])
            diag_d = sb(l0, "diag_d", [P, KD, P])
            row_is = sb(l0, "row_is", [96, 32])
            pick = sb(l0, "pick", [96, 32, P], BF16)
            ax_t = sb(l0, "ax_t", [P, T0])
            g_act = sb(l0, "g_act", [P, Q0, D])
            h_norm = sb(l0, "h_norm", [P, Q0, D])
            h_t = sb(l0, "h_t", [P, T0])
            xc = sb(l0, "xc", [P, KD, TAPS - 1 + T0])
            conv = sb(l0, "conv", [P, KD, T0])
            u = sb(l0, "u", [P, KD, T0])
            sz = sb(l0, "sz", [P, KD, T0])
            rank_t = sb(l0, "rank_t", [RANK, T0])
            bc1 = sb(l0, "bc1", [96, T0], BF16)
            bc2 = sb(l0, "bc2", [96, T0], BF16)
            bc_parts = sb(l0, "bc_parts", [96, T0], BF16)
            bc_rest = sb(l0, "bc_rest", [96, T0])
            sp_e = sb(l0, "sp_e", [P, KD, T0])
            sp_v = sb(l0, "sp_v", [P, KD, T0])
            dt = sb(l0, "dt", [P, KD, T0])
            du = sb(l0, "du", [P, KD, T0])
            da = sb(l0, "da", [P, N_DA, T0])
            dbu = sb(l0, "dbu", [P, N_DBU, T0])
            hs = sb(l0, "hs", [P, N_H, T0])
            h_last = sb(l0, "h_last", [P, STEPS])
            cs = sb(l0, "cs", [P, N_CS, T0])
            hc = sb(l0, "hc", [P, N_HC, T0])
            yg = sb(l0, "yg", [P, KD, T0])
            xo = sb(l0, "xo", [P, Q0, D])
            ln0_st = sb(l0, "ln0_st", [P, Q0, 6])
            ln0_mv = sb(l0, "ln0_mv", [P, Q0, 2])
            ln0_rs = sb(l0, "ln0_rs", [P, Q0])
            ln1_rs = sb(l0, "ln1_rs", [P, Q0])
            ln1_mv = sb(l0, "ln1_mv", [P, Q0, 2])
            ln1_st = sb(l0, "ln1_st", [P, Q0, 6])

        with ExitStack() as l1:
            x_t = sb(l1, "x_t", [P, N])
            bh = sb(l1, "bh", [P, NT, D])
            stat_s = sb(l1, "stat_s", [P, NT, HEADS, 32], BF16)
            stat_m = sb(l1, "stat_m", [P, NT, HEADS, 32], BF16)
            r_rows = sb(l1, "r_rows", [P, HEADS, T1])
            r_blk = sb(l1, "r_blk", [P, T1])
            w_ring = sb(l1, "w_ring", [P, N_W, HEADS, T1])
            s8 = sb(l1, "s8", [P, N_S, HEADS, T1], FP8)
            m8 = sb(l1, "m8", [P, N_S, T1], U8)
            m1 = sb(l1, "m1", [P, N_S, T1], FP8)
            wa_rep = sb(l1, "wa_rep", [P, HEADS, P])
            a_rep = sb(l1, "a_rep", [P, HEADS, P])
            wa_blk = sb(l1, "wa_blk", [P, HEADS, F])
            w1_cat = sb(l1, "w1_cat", [P, D + HEADS])
            e_dst = sb(l1, "e_dst", [P, NT, HEADS])
            d_max = sb(l1, "d_max", [P, HEADS])
            d_all = sb(l1, "d_all", [P, HEADS])
            e_neg = sb(l1, "e_neg", [P, NT, HEADS])
            bv = sb(l1, "bv", [P, NT, HEADS])
            cv = sb(l1, "cv", [P, NT, HEADS])
            dv = sb(l1, "dv", [P, NT, HEADS])
            neg_c = sb(l1, "neg_c", [P, NT, HEADS])
            r_bias = sb(l1, "r_bias", [P, HEADS])
            r_bias_blk = sb(l1, "r_bias_blk", [P, 1])
            ones = sb(l1, "ones", [P, 32])
            den_raw = sb(l1, "den_raw", [P, T1])
            den = sb(l1, "den", [P, T1])
            sum_raw = sb(l1, "sum_raw", [32, T1])
        with ExitStack() as l2:
            x2_t = sb(l2, "x2_t", [P, N])
            sup = sb(l2, "sup", [P, NT, D])
            dis = sb(l2, "dis", [P, NT])
            acc = sb(l2, "acc", [P, T1])
            xo2 = sb(l2, "xo2", [P, Q1, D])
            big = sb(l2, "big", [P, NT, D])
            sums = sb(l2, "sums", [P, 2 * NT + 1])
            norms = sb(l2, "norms", [P, 2 * NT + 1])
            recips = sb(l2, "recips", [P, 2 * NT + 1])
            dots = sb(l2, "dots", [P, NT])
            sv = [sb(l2, f"sv{i}", [P, NT + 1]) for i in range(8)]
            hyp_bias = sb(l2, "hyp_bias", [P, D])
            rl = sb(l2, "rl", [P, Q1, D])
            sq = sb(l2, "sq", [P, 2, Q1, D])
            fs = sb(l2, "fs", [P, 2, Q1])
            fv = [sb(l2, f"fv{i}", [P, Q1]) for i in range(8)]
            xo3 = sb(l2, "xo3", [P, Q1, D])
        ACC, PREP, TURN = 0, 4, 6

        xo1 = den_raw[:].rearrange("p (q d) -> p q d", q=Q1)

        NUM, DEN, SUM, MISC = 0, 2, 4, 6
        two = lambda bank: ps[:, bank:bank + 2, :].rearrange("p a b -> p (a b)")
        tiles8 = lambda bank: ps[:, bank:bank + 2, :].rearrange("p a (q d) -> p (a q) d", d=D)

        AX, M0, M1, BB, CB, Y = 0, 1, 2, 3, 5, 6
        tiles = lambda bank: ps[:, bank, :].rearrange("p (q d) -> p q d", q=Q0)

        setup_dmas = [
            (ident, t["ident"]), (gcn_w, t["gcn_w"]), (w_in, t["w_in"]),
            (gcn_b, t["gcn_b"].rearrange("(a d) -> a d", a=1).broadcast_to([P, D])),
            (ln_g, t["ln_g"].rearrange("(p a) -> p a", a=1)), (ln_b, t["ln_b"].rearrange("(p a) -> p a", a=1)),
            (conv_w, t["conv_w"].rearrange("(k p) w -> p k w", p=P)),
            (conv_b, t["conv_b"]),
            (w_bc, t["w_bc"].rearrange("(k p) r -> p k r", p=P)),
            (w_r, t["w_r"].rearrange("(k p) r -> p k r", p=P)),
            (w_dt, t["w_dt"]), (b_dt, t["b_dt"]),
            (a_neg, t["a_log"].rearrange("(k p) n -> p k n", p=P)),
            (d_skip, t["d_skip"]),
            (w_out, t["w_out"].rearrange("(k p) m -> p k m", p=P)), (row_is, t["row_is"]),
            (w1, t["w1"]), (w1_t, t["w1_t"]), (a_bd, t["a_bd"]), (w2_t, t["w2_t"]), (w3_t, t["w3_t"]),
            (sel, t["sel"].rearrange("p (two c) -> p two c", two=2)),
            (bias3, t["bias3"].rearrange("(a d) -> a d", a=1).broadcast_to([P, D])),
        ]
        setup_all = 16 * len(setup_dmas)

        block = ctx.enter_context(nc.Block())

        @block.sync
        def _(sp):
            sp.dma_start(xa[:], t["x"].rearrange("(t p) d -> p t d", p=P)).then_inc(sem("x_loaded"), 16)
            adj0 = adj_t.rearrange("(r two p) i -> r p two i", two=2, p=P)

            def load0(c, r):
                slot = r % RING
                sp.dma_start(ring[:, slot, :].rearrange("p (two i) -> p two i", two=2),
                             adj0[r][:, :, bass.ts(c, T0)]).then_inc(sem(f"adj_in{slot}"), 16)

            for r in range(NT // 2):
                if r >= RING:
                    sp.wait_ge(sem("adj_free"), r - RING + 1)
                load0(0, r)
            with sp.Fori(1, C0) as c:
                for r in range(NT // 2):
                    sp.wait_ge(sem("adj_free"), c * (NT // 2) + (r - RING + 1))
                    load0(c, r)
            def load1(layer, c, r):
                sp.wait_ge(sem("adj_free"), layer * LOADS + c * NT + (r - RING + 1))
                sp.dma_start(ring[:, r % RING, :], adj_t[r * P:(r + 1) * P, bass.ts(c, T1)])\
                    .then_inc(sem(f"adj_in{r % RING}"), 16)

            for layer in range(1, stop):
                with sp.Fori(0, C1) as c:
                    for r in range(NT):
                        load1(layer, c, r)
            if stop == 3:
                sp.wait_ge(sem("x3_ready"), C1)
                sp.dma_start(out.rearrange("(t p) d -> p t d", p=P), xb[:]).then_inc(sem("out_done"), 16)
                sp.wait_ge(sem("out_done"), 16)
            if stop == 4:
                rows = out.rearrange("(c q p) d -> c p q d", q=Q1, p=P)
                for c in range(C1):
                    sp.wait_ge(sem("x4_ready"), c + 1)
                    sp.dma_start(rows[c], xa[:, c * Q1:(c + 1) * Q1, :]).then_inc(sem("out_done"), 16)
                sp.wait_ge(sem("out_done"), 16 * C1)
            if stop == 2:
                sp.wait_ge(sem("x2_ready"), C1)
                sp.dma_start(out.rearrange("(t p) d -> p t d", p=P), xa[:]).then_inc(sem("out_done"), 16)
                sp.wait_ge(sem("out_done"), 16)
            if stop == 1:
                sp.wait_ge(sem("x1_ready"), C0)
                sp.dma_start(out.rearrange("(t p) d -> p t d", p=P), xb[:]).then_inc(sem("out_done"), 16)
                sp.wait_ge(sem("out_done"), 16)

        @block.gpsimd
        def _(pool):
            pool.memset(half_neg[:], -0.5).then_inc(sem("halves"), 1)
            pool.memset(half_pos[:], 0.5).then_inc(sem("halves"), 1)
            pool.memset(eps[:], EPS).then_inc(sem("halves"), 1)
            pool.memset(h_last[:], 0.0).then_inc(sem("zeroed"), 1)
            pool.memset(xc[:], 0.0).then_inc(sem("zeroed"), 1)
            pool.wait_ge(sem("halves"), 3)
            link = Link(pool, sem("pool_link"))

            def rstd(rs, mv, q, stats, value, ready):
                pool.wait_ge(stats, value)
                link(pool.tensor_tensor(rs[:, 0:q], mv[:, 0:q, 1], eps[:, 0:q], ALU.add))
                pool.tensor_tensor(rs[:, 0:q], rs[:, 0:q], half_neg[:, 0:q], ALU.pow).then_inc(ready, 1)

            def chunk0(c):
                link.body(c, 2)
                rstd(ln0_rs, ln0_mv, Q0, sem("h_stats"), c + 1, sem("h_rstd"))
                for i in range(STEPS):
                    pool.wait_ge(sem("scanned"), c * STEPS + (N_DA + i + 1))
                    if i % KD == 0:
                        pool.wait_ge(sem("c_rows"), c * S_N + (1 + i // KD + 1))
                    pool.wait_ge(sem("y_summed"), c * STEPS + (i + 1))
                    pool.tensor_tensor(hc[:, i % N_HC, :], hs[:, i % N_H, :], cs[:, i // KD % N_CS, :],
                                       ALU.mult).then_inc(sem("hc_ready"), 1)
                rstd(ln1_rs, ln1_mv, Q0, sem("x1_stats"), c + 1, sem("x1_rstd"))

            pool.sem_inc(sem("hc_ready"), HC_CREDIT)
            with pool.Fori(0, C0) as c:
                chunk0(c)
            link.leave(C0)
            if stop == 1:
                return

            pool.wait_ge(sem("x1_ready"), C0)
            pool.memset(ones[:], 1.0).then_inc(sem("ones_ready"), 1)
            pool.memset(stat_s[:], 0.0).then_inc(sem("stat_zero"), 1)
            pool.memset(stat_m[:], 0.0).then_inc(sem("stat_zero"), 1)
            pool.wait_ge(sem("d_max_ready"), 1)
            pool.partition_all_reduce(d_all[:], d_max[:], P, bass.bass_isa.ReduceOp.max).then_inc(sem("d_all_ready"), 1)

            def norm(c):
                link.body(c, 1)
                rstd(ln_rs, ln_mv, Q1, sem("x2_stats"), c + 1, sem("x2_rstd"))

            with pool.Fori(0, C1) as c:
                norm(c)
            link.leave(C1)
            if stop == 2:
                return

            pool.wait_ge(sem("x2_ready"), C1)
            pool.tensor_scalar(dis[:], deg[:], 1.0, None, ALU.add).then_inc(sem("deg_plus"), 1)
            pool.wait_ge(sem("deg_plus"), 1)
            pool.tensor_tensor(dis[:], dis[:], half_neg[:], ALU.pow).then_inc(sem("dis_ready"), 1)

            def norm2(c):
                link.body(c, 1)
                rstd(ln_rs, ln_mv, Q1, sem("x3_stats"), c + 1, sem("x3_rstd"))

            with pool.Fori(0, C1) as c:
                norm2(c)
            link.leave(C1)
            if stop == 3:
                return

            def norm3(c):
                link.body(c, 1)
                for n in range(2):
                    pool.wait_ge(sem("fs_ready"), c * 2 + (n + 1))
                    pool.tensor_tensor(fv[n][:], fs[:, n, :], half_pos[:, 0:Q1], ALU.pow).then_inc(sem("fn_ready"), 1)
                rstd(ln_rs, ln_mv, Q1, sem("x4_stats"), c + 1, sem("x4_rstd"))

            with pool.Fori(0, C1) as c:
                norm3(c)
            link.leave(C1)

        @block.scalar
        def _(act):
            for dst, src in setup_dmas:
                act.dma_start(dst[:], src).then_inc(sem("setup"), 16)
            act.wait_ge(sem("setup"), setup_all)
            link = Link(act, sem("act_link"))
            link(act.activation(a_neg[:], a_neg[:], ACT.Exp))
            act.mul(a_neg[:], a_neg[:], -1.0).then_inc(sem("a_ready"), 1)
            act.wait_ge(sem("a_ready"), 1)
            act.wait_ge(sem("zeroed"), 2)
            link.straight()

            def chunk0(c):
                link.body(c, 5)
                act.wait_ge(sem("adj_free"), c * (NT // 2) + NT // 2)
                act.copy(ax_t[:], ps[:, AX, :]).then_inc(sem("ax_taken"), 1)
                link(act.copy(xc[:, :, 0:TAPS - 1], xc[:, :, T0:T0 + TAPS - 1]))
                act.wait_ge(sem("h_turned"), c + 1)
                act.activation(h_t[:], ps[:, M1, :], ACT.Identity, bias=ln_b[:, 0:1],
                               scale=ln_g[:, 0:1]).then_inc(sem("h_t_ready"), 1)
                for k in range(KD):
                    act.wait_ge(sem("xz_ready"), c * 4 + (k + 1))
                    act.copy(xc[:, k, TAPS - 1:], ps[:, M0 + k, :]).then_inc(sem("xc_ready"), 1)
                for k in range(KD):
                    act.wait_ge(sem("xz_ready"), c * 4 + (KD + k + 1))
                    act.activation(sz[:, k, :], ps[:, M0 + k, :], ACT.Silu).then_inc(sem("z_ready"), 1)
                for k in range(KD):
                    act.wait_ge(sem("conv_ready"), c * KD + (k + 1))
                    act.activation(u[:, k, :], conv[:, k, :], ACT.Silu,
                                   bias=conv_b[:, k:k + 1]).then_inc(sem("u_ready"), 1)
                act.preload_act_table_set("natural_log_exp_and_others")
                act.wait_ge(sem("rank_ready"), c + 1)
                act.copy(rank_t[:], ps[0:RANK, M1, :]).then_inc(sem("rank_taken"), 1)
                for k in range(KD):
                    act.wait_ge(sem("dt_raw"), c * KD + (k + 1))
                    link.mark(act.activation(sp_v[:, k, :], ps[:, M0 + k, :], ACT.Identity, bias=b_dt[:, k:k + 1]))
                link.wait()
                link(act.activation(sp_e[:], sp_v[:], ACT.Abs))
                link(act.activation(sp_e[:], sp_e[:], ACT.Exp, scale=-1.0))
                act.activation(sp_e[:], sp_e[:], ACT.Ln, bias=1.0).then_inc(sem("sp_ready"), 1)
                for i in range(STEPS):
                    n, k = divmod(i, KD)
                    if i == 0:
                        act.wait_ge(sem("dt_done"), c + 1)
                    act.wait_ge(sem("scanned"), c * STEPS + (i + 1))
                    act.activation(da[:, i % N_DA, :], dt[:, k, :], ACT.Exp,
                                   scale=a_neg[:, k, n:n + 1]).then_inc(sem("da_ready"), 1)
                    if k == 0:
                        act.wait_ge(sem("c_bcast"), c * S_N + (n + 1))
                        act.wait_ge(sem("hc_ready"), c * STEPS + (KD * n + KD))
                        act.copy(cs[:, n % N_CS, :], ps[:, CB, :]).then_inc(sem("c_rows"), 1)

            act.sem_inc(sem("c_rows"), 1)
            with act.Fori(0, C0) as c:
                chunk0(c)
            link.leave(C0)
            if stop == 1:
                return

            act.wait_ge(sem("x1_ready"), C0)
            for g in range(NT // 4):
                act.wait_ge(sem("x1_turned"), g + 1)
                act.copy(x_t[:, g * BANK:(g + 1) * BANK], ps[:, SUM + g % 2, :]).then_inc(sem("x1_t_ready"), 1)
            act.wait_ge(sem("wa_raw"), 2)
            act.copy(wa_rep[:].rearrange("p h m -> p (h m)"), ps[:, MISC + 1, :]).then_inc(sem("wa_ready"), 1)
            act.wait_ge(sem("wa_ready"), 1)
            act.copy(wa_blk[:], wa_rep[:, :, 0:F]).then_inc(sem("wa_ready"), 1)
            for g in range(NT // 2):
                act.wait_ge(sem("h_raw"), g + 1)
                src = ps[:, SUM + g % 2, 0:2 * (D + HEADS)].rearrange("p (a b) -> p a b", a=2)
                act.copy(bh[:, 2 * g:2 * g + 2, :], src[:, :, 0:D])
                act.copy(e_dst[:, 2 * g:2 * g + 2, :], src[:, :, D:]).then_inc(sem("h_taken"), 1)
            act.wait_ge(sem("e_ready"), 1)
            act.activation(bv[:], e_dst[:], ACT.Exp)
            act.activation(cv[:], e_neg[:], ACT.Exp).then_inc(sem("bc_ready"), 1)
            act.wait_ge(sem("r_bias_ready"), 1)

            def chunk1(c):
                for h in range(HEADS + 1):
                    act.wait_ge(sem("s_raw"), c * (HEADS + 1) + (h + 1))
                    dst, bias = (r_rows[:, h, :], r_bias[:, h:h + 1]) if h < HEADS else (r_blk[:], r_bias_blk[:])
                    act.activation(dst, two(MISC), ACT.Exp, bias=bias, scale=1 - LEAKY).then_inc(sem("s_taken"), 1)
                act.wait_ge(sem("r_ready"), c * 2 + 1)
                for j in range(NT):
                    act.wait_ge(sem("den_summed"), c * NT + (j + 1))
                    act.sem_inc(sem("act_settled"), 1)
                    for h in range(HEADS):
                        ins = act.activation(s8[:, j % N_S, h, :], r_rows[:, h, :], ACT.Sign,
                                             bias=neg_c[:, j, h:h + 1], saturate=False)
                    ins.then_inc(sem("sign_ready"), 1)
                act.wait_ge(sem("adj_free"), c * NT + (LOADS + NT))
                act.copy(den_raw[:], two(DEN)).then_inc(sem("den_taken"), 1)
                act.copy(sum_raw[:], ps[0:32, SUM:SUM + 2, :].rearrange("p a b -> p (a b)"))\
                    .then_inc(sem("sum_taken"), 1)

            with act.Fori(0, C1) as c:
                chunk1(c)
            if stop == 2:
                return

            def turn_in(layer, ready):
                act.wait_ge(sem(ready), C1)
                for g in range(NT // 4):
                    act.wait_ge(sem(f"x_turned_{layer}"), g + 1)
                    act.copy(x2_t[:, g * BANK:(g + 1) * BANK], ps[:, PREP + g % 2, :]).then_inc(sem(f"x_t_ready_{layer}"), 1)

            def take_sums(layer, c):
                act.wait_ge(sem("adj_free"), c * NT + (layer * LOADS + NT))
                act.copy(acc[:], two(ACC)).then_inc(sem(f"acc_taken_{layer}"), 1)

            turn_in(2, "x2_ready")
            with act.Fori(0, C1) as c:
                take_sums(2, c)
            if stop == 3:
                return

            turn_in(3, "x3_ready")
            act.sem_inc(sem("sq_ready"), 1)
            act.activation(sup[:], xb[:], ACT.Square).then_inc(sem("squares"), 1)
            for g in range(NT // 4):
                act.wait_ge(sem("mx_raw"), g + 1)
                act.copy(big[:, 4 * g:4 * g + 4, :], tiles(TURN + g % 2)).then_inc(sem("mx_ready"), 1)
            act.wait_ge(sem("mx_ready"), NT // 4)
            act.activation(x2_t[:].rearrange("p (t d) -> p t d", d=D), big[:], ACT.Square).then_inc(sem("squares"), 1)
            act.activation(xo3[:, 0, :], bias3[:], ACT.Square, accum_out=sums[:, 2 * NT:]).then_inc(sem("sums_ready"), 1)
            act.wait_ge(sem("sums_floor"), 1)
            act.activation(norms[:], sums[:], ACT.Sqrt).then_inc(sem("norms_ready"), 1)
            act.preload_act_table_set("natural_log_exp_and_others")
            act.wait_ge(sem("atanh_in"), 1)
            act.activation(sv[1][:], sv[0][:], ACT.Ln, bias=1.0)
            act.activation(sv[2][:], sv[0][:], ACT.Ln, bias=1.0, scale=-1.0).then_inc(sem("atanh_ln"), 1)
            act.wait_ge(sem("tanh_in"), 1)
            act.activation(sv[4][:], sv[3][:], ACT.Exp, scale=-2.0).then_inc(sem("tanh_exp"), 1)
            act.wait_ge(sem("h2_ready"), 1)
            act.activation(x2_t[:].rearrange("p (t d) -> p t d", d=D), big[:], ACT.Square).then_inc(sem("h2_sq"), 1)
            act.wait_ge(sem("h2_floor"), 1)
            act.activation(norms[:, 0:NT], sums[:, 0:NT], ACT.Sqrt).then_inc(sem("h2_norm"), 1)
            act.preload_act_table_set("natural_log_exp_and_others")
            act.wait_ge(sem("h2_atanh_in"), 1)
            act.activation(sv[1][:, 0:NT], sv[0][:, 0:NT], ACT.Ln, bias=1.0)
            act.activation(sv[2][:, 0:NT], sv[0][:, 0:NT], ACT.Ln, bias=1.0, scale=-1.0).then_inc(sem("h2_atanh_ln"), 1)

            def chunk3(c):
                take_sums(3, c)
                act.wait_ge(sem("s_turned"), c + 1)
                act.wait_ge(sem("rl_used"), c + 1)
                act.activation(rl[:], tiles8(TURN), ACT.Relu).then_inc(sem("rl_ready"), 1)
                act.activation(sq[:, 0], tiles8(TURN), ACT.Square).then_inc(sem("sq_ready"), 1)
                act.wait_ge(sem("rl_ready"), c + 1)
                act.activation(sq[:, 1], rl[:], ACT.Square).then_inc(sem("sq_ready"), 1)
                act.wait_ge(sem("fn_ready"), c * 2 + 1)
                act.activation(fv[2][:], fv[0][:], ACT.Exp, scale=-2.0).then_inc(sem("f_exp"), 1)
                act.wait_ge(sem("f_atanh_in"), c + 1)
                act.activation(fv[4][:], fv[3][:], ACT.Ln, bias=1.0)
                act.activation(fv[5][:], fv[3][:], ACT.Ln, bias=1.0, scale=-1.0).then_inc(sem("f_atanh_ln"), 1)
                act.wait_ge(sem("fn_ready"), c * 2 + 2)
                act.activation(fv[2][:], fv[1][:], ACT.Exp, scale=-2.0).then_inc(sem("f_exp"), 1)

            with act.Fori(0, C1) as c:
                chunk3(c)

        @block.vector
        def _(dve):
            link = Link(dve, sem("dve_link"))
            dve.wait_ge(sem("setup"), setup_all)
            for k in range(KD):
                dve.tensor_scalar(diag_d[:, k, :], ident[:], d_skip[:, k:k + 1], None,
                                  ALU.mult).then_inc(sem("consts"), 1)
            dve.tensor_copy(pick[:], row_is[:].unsqueeze(2).broadcast_to([96, 32, P])).then_inc(sem("consts"), 1)
            dve.sem_inc(sem("scanned"), N_DA)
            dve.sem_inc(sem("dbu_ready"), DBU_CREDIT)
            dve.sem_inc(sem("out_taken"), 1)
            dve.wait_ge(sem("zeroed"), 2)
            dve.wait_ge(sem("x_loaded"), 16)

            def stats(st, mv, data, q_n, ready):
                for q in range(q_n):
                    link.mark(dve.bn_stats(st[:, q, :], data[:, q, :]))
                link.wait()
                dve.sem_inc(sem("dve_settled"), 1)
                for q in range(q_n):
                    ins = dve.bn_aggr(mv[:, q, :], st[:, q, :])
                ins.then_inc(ready, 1)

            def normalise(dst, data, mv, rs, q_n, ready):
                for q in range(q_n):
                    ins = dve.tensor_scalar(dst(q), data[:, q, :], mv[:, q, 0:1], rs[:, q:q + 1],
                                            ALU.subtract, ALU.mult)
                ins.then_inc(ready, 1)

            def chunk0(c):
                link.body(c, RATE0)
                dve.wait_ge(sem("g_ready"), c + 1)
                link(dve.tensor_tensor(g_act[:], tiles(M0), gcn_b[:].unsqueeze(1).broadcast_to([P, Q0, D]), ALU.add))
                link(dve.tensor_scalar(g_act[:], g_act[:], 0.0, None, ALU.max))
                stats(ln0_st, ln0_mv, g_act, Q0, sem("h_stats"))
                dve.wait_ge(sem("h_rstd"), c + 1)
                normalise(lambda q: h_norm[:, q, :], g_act, ln0_mv, ln0_rs, Q0, sem("h_norm_ready"))
                at = [0, 0]
                for tap in range(TAPS):
                    for k in range(KD):
                        src, w = xc[:, k, tap:tap + T0], conv_w[:, k, tap:tap + 1]
                        if tap == 0:
                            dve.wait_ge(sem("xc_ready"), c * KD + (k + 1))
                            ins = dve.tensor_scalar(conv[:, k, :], src, w, None, ALU.mult)
                        else:
                            link.wait(at[k])
                            ins = dve.scalar_tensor_tensor(out=conv[:, k, :], in0=src, scalar=w, in1=conv[:, k, :],
                                                           op0=ALU.mult, op1=ALU.add)
                        if tap < TAPS - 1:
                            at[k] = link.mark(ins)
                        else:
                            ins.then_inc(sem("conv_ready"), 1)
                dve.wait_ge(sem("bc_raw"), c + 1)
                raw = ps[0:96, M0, :]
                link.mark(dve.tensor_copy(bc1[:], raw))
                link(dve.tensor_copy(bc_parts[0:32, :], raw[0:32]))
                dve.tensor_tensor(bc_rest[:], raw, bc1[:], ALU.subtract).then_inc(sem("bc_taken"), 1)
                dve.wait_ge(sem("bc_taken"), c + 1)
                link.mark(dve.tensor_copy(bc2[:], bc_rest[:]))
                link(dve.tensor_copy(bc_parts[32:64, :], bc_rest[32:64, :]))
                link(dve.tensor_tensor(bc_rest[64:96, :], bc_rest[64:96, :], bc2[64:96, :], ALU.subtract))
                dve.tensor_copy(bc_parts[64:96, :], bc_rest[64:96, :]).then_inc(sem("bc_split"), 1)
                dve.wait_ge(sem("sp_ready"), c + 1)
                dve.scalar_tensor_tensor(out=dt[:], in0=sp_v[:], scalar=0.0, in1=sp_e[:], op0=ALU.max,
                                         op1=ALU.add).then_inc(sem("dt_done"), 1)
                dve.wait_ge(sem("dt_done"), c + 1)
                dve.wait_ge(sem("u_ready"), c * KD + KD)
                link(dve.tensor_tensor(du[:], dt[:], u[:], ALU.mult))

                def step_dbu(i):
                    n, k = divmod(i, KD)
                    if k == 0:
                        dve.wait_ge(sem("b_bcast"), c * S_N + (n + 1))
                    if i >= N_DBU:
                        dve.wait_ge(sem("scanned"), c * STEPS + (N_DA + i - N_DBU + 1))
                    dve.tensor_tensor(dbu[:, i % N_DBU, :], du[:, k, :], ps[:, BB + n % 2, :],
                                      ALU.mult).then_inc(sem("dbu_ready"), 1)

                def step_keep(i):
                    dve.wait_ge(sem("scanned"), c * STEPS + (N_DA + i + 1))
                    return link.mark(dve.tensor_copy(h_last[:, i:i + 1], hs[:, i % N_H, T0 - 1:T0]))

                kept = [0] * STEPS
                step_dbu(0)
                for i in range(STEPS):
                    if i + 1 < STEPS:
                        step_dbu(i + 1)
                    dve.wait_ge(sem("dbu_ready"), c * STEPS + (DBU_CREDIT + i + 1))
                    dve.wait_ge(sem("da_ready"), c * STEPS + (i + 1))
                    dve.wait_ge(sem("hc_ready"), c * STEPS + (HC_CREDIT - N_H + i + 1))
                    if i >= N_H:
                        link.wait(kept[i - N_H])
                    dve.tensor_tensor_scan(hs[:, i % N_H, :], da[:, i % N_DA, :], dbu[:, i % N_DBU, :],
                                           h_last[:, i:i + 1], ALU.mult, ALU.add).then_inc(sem("scanned"), 1)
                    if i >= 1:
                        kept[i - 1] = step_keep(i - 1)
                kept[STEPS - 1] = step_keep(STEPS - 1)
                link.wait()
                for k in range(KD):
                    dve.wait_ge(sem("y_ready"), c * KD + (k + 1))
                    dve.tensor_tensor(yg[:, k, :], ps[:, Y + k, :], sz[:, k, :], ALU.mult).then_inc(sem("gated"), 1)
                dve.wait_ge(sem("out_ready"), c + 1)
                dve.tensor_tensor(xo[:], tiles(M0), xa[:, bass.ds(c * Q0, Q0), :], ALU.add).then_inc(sem("out_taken"), 1)
                dve.wait_ge(sem("out_taken"), c + 2)
                stats(ln1_st, ln1_mv, xo, Q0, sem("x1_stats"))
                dve.wait_ge(sem("x1_rstd"), c + 1)
                normalise(lambda q: xb[:, bass.ds(c * Q0 + q, 1), :].rearrange("p a d -> p (a d)"),
                          xo, ln1_mv, ln1_rs, Q0, sem("x1_ready"))

            with dve.Fori(0, C0) as c:
                chunk0(c)
            link.leave(C0)
            if stop == 1:
                return

            dve.sem_inc(sem("x_taken"), 1)
            dve.wait_ge(sem("x1_ready"), C0)
            link(dve.tensor_copy(a_rep[:], a_bd[:, HEADS:].unsqueeze(2).broadcast_to([P, HEADS, P])))
            dve.tensor_copy(w1_cat[:, 0:D], w1[:]).then_inc(sem("w1_cat_ready"), 1)
            dve.wait_ge(sem("wa_raw"), 1)
            dve.tensor_copy(w1_cat[:, D:], ps[:, MISC, 0:HEADS]).then_inc(sem("w1_cat_ready"), 1)
            dve.wait_ge(sem("h_taken"), NT // 2)
            dve.tensor_reduce(d_max[:], e_dst[:].rearrange("p t h -> p h t"), AX_X, ALU.max).then_inc(sem("d_max_ready"), 1)
            dve.wait_ge(sem("d_all_ready"), 1)
            link.mark(dve.tensor_tensor(e_dst[:], e_dst[:], d_all[:].unsqueeze(1).broadcast_to([P, NT, HEADS]), ALU.subtract))
            link(dve.tensor_scalar(r_bias[:], d_all[:], 1 - LEAKY, None, ALU.mult))
            for h in range(HEADS):
                rows = slice(F * h, F * (h + 1))
                link.mark(dve.tensor_copy(r_bias_blk[rows, :], r_bias[rows, h:h + 1]))
            dve.tensor_scalar(e_neg[:], e_dst[:], LEAKY - 1, E_MAX, ALU.mult, ALU.min).then_inc(sem("e_ready"), 1)
            dve.wait_ge(sem("bc_ready"), 1)
            link.mark(dve.tensor_tensor(dv[:], bv[:], cv[:], ALU.mult))
            dve.tensor_scalar(neg_c[:], cv[:], -1.0, None, ALU.mult).then_inc(sem("r_bias_ready"), 1)
            bh4 = bh[:].rearrange("p t (h f) -> p (t h) f", f=F)
            dve.tensor_tensor(bh4, bh4, bv[:].rearrange("p t h -> p (t h)").unsqueeze(2)
                              .broadcast_to([P, NT * HEADS, F]), ALU.mult).then_inc(sem("bh_ready"), 1)
            dve.wait_ge(sem("stat_zero"), 2)
            dve.wait_ge(sem("bh_ready"), 1)
            for v, (rest, sign) in enumerate(((bv, 1.0), (dv, -1.0))):
                for part in range(PARTS):
                    col = v * PARTS + part
                    link(dve.tensor_copy(stat_m[:, :, :, col], rest[:]))
                    link.mark(dve.tensor_scalar(stat_s[:, :, :, col], stat_m[:, :, :, col], sign, None, ALU.mult))
                    if part < PARTS - 1:
                        link(dve.tensor_tensor(rest[:], rest[:], stat_m[:, :, :, col], ALU.subtract))
            link.wait()
            dve.tensor_copy(d_max[:], d_all[:]).then_inc(sem("bh_ready"), 1)
            link.straight()

            def chunk1(c):
                link.body(c, RATE1)
                dve.wait_ge(sem("s_taken"), c * (HEADS + 1) + HEADS)
                rows = r_rows[:].rearrange("p h i -> p (h i)")
                dve.tensor_scalar(rows, rows, float(R_MAX), None, ALU.min).then_inc(sem("r_ready"), 1)
                dve.wait_ge(sem("s_taken"), c * (HEADS + 1) + HEADS + 1)
                dve.tensor_scalar(r_blk[:], r_blk[:], float(R_MAX), None, ALU.min).then_inc(sem("r_ready"), 1)
                dve.wait_ge(sem("r_ready"), c * 2 + 2)
                for j in range(NT):
                    adj = ring[:, j % RING, :]
                    sl = j % N_S
                    dve.wait_ge(sem(f"adj_in{j % RING}"), c * (16 * NT // RING) + 16 * (LOADS // RING + j // RING + 1))
                    dve.wait_ge(sem("den_summed"), c * NT + (j + 1))
                    link(dve.tensor_scalar(m8[:, sl, :], adj, 0.0, 255.0, ALU.is_gt, ALU.mult))
                    m8w, s8w = m8[:, sl, :].bitcast(U32), s8[:, sl, :, :].bitcast(U32)
                    dve.tensor_scalar(m1[:, sl, :].bitcast(U32), m8w, 0x38383838, None, ALU.bitwise_and)
                    dve.wait_ge(sem("sign_ready"), c * NT + (j + 1))
                    dve.tensor_tensor(s8w, s8w, m8w.unsqueeze(1).broadcast_to([P, HEADS, T1 // 4]),
                                      ALU.bitwise_and).then_inc(sem("masked"), 1)
                    dve.wait_ge(sem("num_summed"), c * NT + (j + 1))
                    for h in range(HEADS):
                        ins = dve.scalar_tensor_tensor(out=w_ring[:, j % N_W, h, :], in0=r_rows[:, h, :],
                                                       scalar=cv[:, j, h:h + 1], in1=adj, op0=ALU.max, op1=ALU.mult)
                    ins.then_inc(sem("w_ready"), 1)
                dve.wait_ge(sem("p_raw"), c + 1)
                link(dve.tensor_tensor(den[:], r_blk[:], two(MISC), ALU.mult))
                dve.wait_ge(sem("q_raw"), c + 1)
                link(dve.tensor_tensor(den[:], den[:], two(DEN), ALU.add))
                link(dve.reciprocal(den[:], den[:]))
                dve.tensor_tensor(den[:], den[:], two(NUM), ALU.mult).then_inc(sem("o_ready"), 1)
                dve.wait_ge(sem("o_turned"), c + 1)
                link.mark(dve.tensor_copy(deg[:, bass.ds(c * Q1, Q1)],
                                ps[:, SUM, :].rearrange("p (q r) -> p q r", r=64)[:, :, 0]))
                dve.tensor_tensor(xo1, tiles8(MISC), xb[:, bass.ds(c * Q1, Q1), :], ALU.add).then_inc(sem("x_taken"), 1)
                dve.wait_ge(sem("x_taken"), c + 2)
                stats(ln_st, ln_mv, xo1, Q1, sem("x2_stats"))
                dve.wait_ge(sem("x2_rstd"), c + 1)
                normalise(lambda q: xa[:, bass.ds(c * Q1 + q, 1), :].rearrange("p a d -> p (a d)"),
                          xo1, ln_mv, ln_rs, Q1, sem("x2_ready"))

            with dve.Fori(0, C1) as c:
                chunk1(c)
            link.leave(C1)
            if stop == 2:
                return

            dve.sem_inc(sem("turn_taken"), 1)
            dve.wait_ge(sem("x2_ready"), C1)
            dve.wait_ge(sem("dis_ready"), 1)
            for g in range(NT // 4):
                dve.wait_ge(sem("sup_raw"), g + 1)
                dve.tensor_tensor(sup[:, 4 * g:4 * g + 4, :], tiles(TURN + g % 2),
                                  dis[:, 4 * g:4 * g + 4].unsqueeze(2).broadcast_to([P, 4, D]),
                                  ALU.mult).then_inc(sem("sup_ready"), 1)
            dve.wait_ge(sem("sup_ready"), NT // 4)
            link.straight()

            def chunk2(c):
                link.body(c, RATE2)
                rows = bass.ds(c * Q1, Q1)
                dve.wait_ge(sem("s2_turned"), c + 1)
                dve.tensor_tensor(xo2[:], tiles8(TURN), sup[:, rows, :], ALU.add).then_inc(sem("turn_taken"), 1)
                dve.wait_ge(sem("turn_taken"), c + 2)
                link(dve.tensor_tensor(xo2[:], xo2[:], dis[:, rows].unsqueeze(2).broadcast_to([P, Q1, D]), ALU.mult))
                link(dve.scalar_tensor_tensor(out=xo2[:].rearrange("p q d -> p (q d)"), in0=xo2[:].rearrange("p q d -> p (q d)"), scalar=0.0,
                                              in1=xa[:, rows, :].rearrange("p q d -> p (q d)"), op0=ALU.max, op1=ALU.add))
                stats(ln_st, ln_mv, xo2, Q1, sem("x3_stats"))
                dve.wait_ge(sem("x3_rstd"), c + 1)
                normalise(lambda q: xb[:, bass.ds(c * Q1 + q, 1), :].rearrange("p a d -> p (a d)"),
                          xo2, ln_mv, ln_rs, Q1, sem("x3_ready"))
                dve.wait_ge(sem("x3_ready"), c + 1)

            with dve.Fori(0, C1) as c:
                chunk2(c)
            link.leave(C1)
            if stop == 3:
                return

            dve.sem_inc(sem("rl_used"), 1)
            dve.wait_ge(sem("x3_ready"), C1)
            dve.wait_ge(sem("mx_ready"), NT // 4)
            all_rows = [P, NT, D]
            per_row = lambda v: v.unsqueeze(2).broadcast_to(all_rows)
            scratch = x2_t[:].rearrange("p (t d) -> p t d", d=D)
            dve.wait_ge(sem("squares"), 1)
            link(dve.tensor_reduce(sums[:, 0:NT], sup[:], AX_X, ALU.add))
            link(dve.tensor_tensor(sup[:], big[:], bias3[:].unsqueeze(1).broadcast_to(all_rows), ALU.mult))
            link.mark(dve.tensor_reduce(dots[:], sup[:], AX_X, ALU.add))
            dve.wait_ge(sem("squares"), 2)
            link(dve.tensor_reduce(sums[:, NT:2 * NT], scratch, AX_X, ALU.add))
            dve.wait_ge(sem("sums_ready"), 1)
            dve.tensor_scalar(sums[:], sums[:], MIN_SQ, None, ALU.max).then_inc(sem("sums_floor"), 1)
            dve.wait_ge(sem("norms_ready"), 1)
            xn, mxn, bn = norms[:, 0:NT], norms[:, NT:2 * NT], norms[:, 2 * NT:]
            link.mark(dve.reciprocal(recips[:], norms[:]))
            link(dve.memset(sv[0][:, NT:], 0.0))
            dve.tensor_scalar(sv[0][:, 0:NT], xn, ATANH_MAX, None, ALU.min).then_inc(sem("atanh_in"), 1)
            dve.wait_ge(sem("atanh_ln"), 1)
            link(dve.tensor_tensor(sv[3][:], sv[1][:], sv[2][:], ALU.subtract))
            link(dve.scalar_tensor_tensor(out=sv[3][:, 0:NT], in0=sv[3][:, 0:NT], scalar=0.5, in1=mxn,
                                          op0=ALU.mult, op1=ALU.mult))
            link(dve.tensor_tensor(sv[3][:, 0:NT], sv[3][:, 0:NT], recips[:, 0:NT], ALU.mult))
            dve.tensor_copy(sv[3][:, NT:], bn).then_inc(sem("tanh_in"), 1)
            dve.wait_ge(sem("tanh_exp"), 1)

            def tanh_of(e, dst, tmp):
                link.mark(dve.tensor_scalar(dst, e, -1.0, 1.0, ALU.mult, ALU.add))
                link(dve.tensor_scalar(tmp, e, 1.0, None, ALU.add))
                link(dve.reciprocal(tmp, tmp))
                link(dve.tensor_tensor(dst, dst, tmp, ALU.mult))
                link(dve.tensor_scalar(dst, dst, MAX_NORM, None, ALU.min))

            n1 = sv[5]
            tanh_of(sv[4][:], n1[:], sv[6][:])
            link(dve.tensor_tensor(sv[6][:], n1[:], recips[:, NT:], ALU.mult))
            alpha, cb = sv[6][:, 0:NT], sv[6][:, NT:]
            link.mark(dve.tensor_scalar(hyp_bias[:], bias3[:], cb, None, ALU.mult))
            link(dve.tensor_tensor(sv[7][:], n1[:], n1[:], ALU.mult))
            x2, y2 = sv[7][:, 0:NT], sv[7][:, NT:]
            link(dve.tensor_scalar(dots[:], dots[:], cb, 2.0, ALU.mult, ALU.mult))
            link(dve.tensor_tensor(dots[:], dots[:], alpha, ALU.mult))
            link(dve.tensor_scalar(dots[:], dots[:], 1.0, None, ALU.add))
            r_den, cx, cy = sv[4][:, 0:NT], sv[1][:, 0:NT], sv[2][:, 0:NT]
            link(dve.scalar_tensor_tensor(out=r_den, in0=x2, scalar=y2, in1=dots[:], op0=ALU.mult, op1=ALU.add))
            link(dve.tensor_scalar(r_den, r_den, 1e-15, None, ALU.max))
            link(dve.reciprocal(r_den, r_den))
            link(dve.scalar_tensor_tensor(out=cx, in0=dots[:], scalar=y2, in1=r_den, op0=ALU.add, op1=ALU.mult))
            link(dve.tensor_tensor(cx, cx, alpha, ALU.mult))
            link(dve.tensor_scalar(cy, x2, -1.0, 1.0, ALU.mult, ALU.add))
            link(dve.tensor_tensor(cy, cy, r_den, ALU.mult))
            link.mark(dve.tensor_tensor(big[:], big[:], per_row(cx), ALU.mult))
            link(dve.tensor_tensor(scratch, hyp_bias[:].unsqueeze(1).broadcast_to(all_rows), per_row(cy), ALU.mult))
            dve.tensor_tensor(big[:], big[:], scratch, ALU.add).then_inc(sem("h2_ready"), 1)
            dve.wait_ge(sem("h2_sq"), 1)
            link(dve.tensor_reduce(sums[:, 0:NT], scratch, AX_X, ALU.add))
            dve.tensor_scalar(sums[:, 0:NT], sums[:, 0:NT], MIN_SQ, None, ALU.max).then_inc(sem("h2_floor"), 1)
            dve.wait_ge(sem("h2_norm"), 1)
            link.mark(dve.reciprocal(recips[:, 0:NT], xn))
            dve.tensor_scalar(sv[0][:, 0:NT], xn, MAX_NORM, None, ALU.min).then_inc(sem("h2_atanh_in"), 1)
            dve.wait_ge(sem("h2_atanh_ln"), 1)
            link(dve.tensor_tensor(cx, cx, cy, ALU.subtract))
            link(dve.scalar_tensor_tensor(out=cx, in0=cx, scalar=0.5, in1=recips[:, 0:NT], op0=ALU.mult, op1=ALU.mult))
            dve.tensor_tensor(sup[:], big[:], per_row(cx), ALU.mult).then_inc(sem("xt_ready"), 1)
            link.straight()

            def chunk3(c):
                link.body(c, RATE3)
                rows = bass.ds(c * Q1, Q1)
                dve.wait_ge(sem("sq_ready"), c * 2 + 2)
                link(dve.tensor_reduce(fs[:, 0, :], sq[:, 0], AX_X, ALU.add))
                dve.tensor_scalar(fs[:, 0, :], fs[:, 0, :], MIN_SQ, None, ALU.max).then_inc(sem("fs_ready"), 1)
                dve.wait_ge(sem("sq_ready"), c * 2 + 3)
                link(dve.tensor_reduce(fs[:, 1, :], sq[:, 1], AX_X, ALU.add))
                dve.wait_ge(sem("f_exp"), c * 2 + 1)
                tanh_of(fv[2][:], fv[3][:], fv[6][:])
                dve.tensor_copy(fv[7][:], fv[3][:]).then_inc(sem("f_atanh_in"), 1)
                link(dve.reciprocal(fv[0][:], fv[0][:]))
                dve.wait_ge(sem("f_atanh_ln"), c + 1)
                link(dve.tensor_tensor(fv[4][:], fv[4][:], fv[5][:], ALU.subtract))
                k1 = fv[7][:]
                link(dve.scalar_tensor_tensor(out=k1, in0=fv[4][:], scalar=0.5, in1=fv[0][:], op0=ALU.mult, op1=ALU.mult))
                link(dve.tensor_tensor(fv[4][:], k1, k1, ALU.mult))
                link(dve.tensor_tensor(fs[:, 1, :], fs[:, 1, :], fv[4][:], ALU.mult))
                dve.tensor_scalar(fs[:, 1, :], fs[:, 1, :], MIN_SQ, None, ALU.max).then_inc(sem("fs_ready"), 1)
                dve.wait_ge(sem("f_exp"), c * 2 + 2)
                tanh_of(fv[2][:], fv[3][:], fv[6][:])
                link(dve.reciprocal(fv[1][:], fv[1][:]))
                link(dve.tensor_tensor(k1, k1, fv[3][:], ALU.mult))
                link(dve.tensor_tensor(k1, k1, fv[1][:], ALU.mult))
                link(dve.tensor_tensor(rl[:], rl[:], k1.unsqueeze(2).broadcast_to([P, Q1, D]), ALU.mult))
                dve.tensor_tensor(xo3[:], rl[:], xb[:, rows, :], ALU.add).then_inc(sem("rl_used"), 1)
                dve.wait_ge(sem("rl_used"), c + 2)
                stats(ln_st, ln_mv, xo3, Q1, sem("x4_stats"))
                dve.wait_ge(sem("x4_rstd"), c + 1)
                normalise(lambda q: xa[:, bass.ds(c * Q1 + q, 1), :].rearrange("p a d -> p (a d)"),
                          xo3, ln_mv, ln_rs, Q1, sem("x4_ready"))
                dve.wait_ge(sem("x4_ready"), c + 1)

            with dve.Fori(0, C1) as c:
                chunk3(c)
            link.leave(C1)

        @block.tensor
        def _(pe):
            pe.wait_ge(sem("setup"), setup_all)
            pe.wait_ge(sem("consts"), KD + 1)
            pe.wait_ge(sem("x_loaded"), 16)
            pe.sem_inc(sem("y_summed"), N_HC)

            def aggregate(c, j):
                r = j // 2
                if j % 2 == 0:
                    pe.wait_ge(sem(f"adj_in{r % RING}"), c * 32 + 16 * (r // RING + 1))
                ins = pe.matmul(ps[:, AX, :], xa[:, j, :], ring[:, r % RING, j % 2 * T0:(j % 2 + 1) * T0],
                                start=j == 0, stop=j == NT - 1)
                if j % 2 == 1:
                    ins.then_inc(sem("adj_free"), 1)

            def chunk0(c, last):
                pe.wait_ge(sem("ax_taken"), c + 1)
                pe.wait_ge(sem("out_taken"), c + 1)
                for q in range(Q0):
                    ins = pe.matmul(tiles(M0)[:, q, :], ax_t[:, q * P:(q + 1) * P], gcn_w[:], start=True, stop=True)
                ins.then_inc(sem("g_ready"), 1)
                pe.wait_ge(sem("h_norm_ready"), c + 1)
                for q in range(Q0):
                    ins = pe.transpose(tiles(M1)[:, q, :], h_norm[:, q, :], ident[:])
                ins.then_inc(sem("h_turned"), 1)
                pe.wait_ge(sem("h_t_ready"), c + 1)
                for m in range(2 * KD):
                    if m >= KD:
                        pe.wait_ge(sem("xc_ready"), c * KD + (m - KD + 1))
                    pe.matmul(ps[:, M0 + m % KD, :], w_in[:, m * P:(m + 1) * P], h_t[:], start=True,
                              stop=True).then_inc(sem("xz_ready"), 1)
                pe.wait_ge(sem("z_ready"), c * KD + KD)
                pe.wait_ge(sem("u_ready"), c * KD + KD)
                for k in range(KD):
                    ins = pe.matmul(ps[0:96, M0, :], w_bc[:, k, :], u[:, k, :], start=k == 0, stop=k == KD - 1)
                ins.then_inc(sem("bc_raw"), 1)
                for k in range(KD):
                    ins = pe.matmul(ps[0:RANK, M1, :], w_r[:, k, :], u[:, k, :], start=k == 0, stop=k == KD - 1)
                ins.then_inc(sem("rank_ready"), 1)
                pe.wait_ge(sem("rank_taken"), c + 1)
                pe.wait_ge(sem("bc_taken"), c + 1)
                for k in range(KD):
                    pe.matmul(ps[:, M0 + k, :], w_dt[:, k * P:(k + 1) * P], rank_t[:], start=True,
                              stop=True).then_inc(sem("dt_raw"), 1)
                pe.wait_ge(sem("bc_split"), c + 1)

                def sum_y(i):
                    n, k = divmod(i, KD)
                    pe.wait_ge(sem("hc_ready"), c * STEPS + (HC_CREDIT + i + 1))
                    pe.matmul(ps[:, Y + k, :], ident[:], hc[:, i % N_HC, :], start=n == 0,
                              stop=False).then_inc(sem("y_summed"), 1)

                for i in range(STEPS + Y_LAG):
                    n, k = divmod(i, KD)
                    if i < STEPS and k == 0:
                        pe.wait_ge(sem("dbu_ready"), c * STEPS + (KD * n + KD))
                        pe.matmul(ps[:, BB + n % 2, :], pick[:, n, :], bc_parts[:], start=True,
                                  stop=True).then_inc(sem("b_bcast"), 1)
                        pe.wait_ge(sem("c_rows"), c * S_N + (n + 1))
                        pe.matmul(ps[:, CB, :], pick[:, S_N + n, :], bc_parts[:], start=True,
                                  stop=True).then_inc(sem("c_bcast"), 1)
                    if i < STEPS and not last:
                        aggregate(c + 1, i)
                    if i >= Y_LAG:
                        sum_y(i - Y_LAG)
                for k in range(KD):
                    pe.matmul(ps[:, Y + k, :], diag_d[:, k, :], u[:, k, :], start=False,
                              stop=True).then_inc(sem("y_ready"), 1)
                pe.wait_ge(sem("gated"), c * KD + KD)
                for q in range(Q0):
                    for k in range(KD):
                        ins = pe.matmul(tiles(M0)[:, q, :], yg[:, k, q * P:(q + 1) * P], w_out[:, k, :],
                                        start=k == 0, stop=k == KD - 1)
                ins.then_inc(sem("out_ready"), 1)

            for j in range(NT):
                aggregate(0, j)
            with pe.Fori(0, C0 - 1) as c:
                chunk0(c, False)
            chunk0(C0 - 1, True)
            if stop == 1:
                return

            pe.wait_ge(sem("x1_ready"), C0)
            for g in range(NT // 4):
                if g >= 2:
                    pe.wait_ge(sem("x1_t_ready"), g - 1)
                for q in range(4):
                    ins = pe.transpose(ps[:, SUM + g % 2, q * P:(q + 1) * P], xb[:, 4 * g + q, :], ident[:])
                ins.then_inc(sem("x1_turned"), 1)
            pe.wait_ge(sem("w1_cat_ready"), 1)
            pe.matmul(ps[:, MISC, 0:HEADS], w1_t[:], a_bd[:, 0:HEADS], start=True, stop=True).then_inc(sem("wa_raw"), 1)
            pe.matmul(ps[:, MISC + 1, :], w1_t[:], a_rep[:].rearrange("p h m -> p (h m)"), start=True,
                      stop=True).then_inc(sem("wa_raw"), 1)
            pe.wait_ge(sem("w1_cat_ready"), 2)
            pe.wait_ge(sem("x1_t_ready"), NT // 4)
            for g in range(NT // 2):
                if g >= 2:
                    pe.wait_ge(sem("h_taken"), g - 1)
                for q in range(2):
                    j = 2 * g + q
                    ins = pe.matmul(ps[:, SUM + g % 2, q * (D + HEADS):(q + 1) * (D + HEADS)],
                                    x_t[:, j * P:(j + 1) * P], w1_cat[:], start=True, stop=True)
                ins.then_inc(sem("h_raw"), 1)
            pe.wait_ge(sem("h_taken"), NT // 2)
            pe.wait_ge(sem("wa_ready"), 2)
            pe.wait_ge(sem("ones_ready"), 1)
            pe.wait_ge(sem("bh_ready"), 2)
            pe.sem_inc(sem("den_summed"), N_S)
            pe.sem_inc(sem("num_summed"), N_W)

            def chunk1(c):
                pe.wait_ge(sem("x_taken"), c + 1)
                for h in range(HEADS + 1):
                    if h:
                        pe.wait_ge(sem("s_taken"), c * (HEADS + 1) + h)
                    lhs = wa_rep[:, h, :] if h < HEADS else wa_blk[:].rearrange("p h f -> p (h f)")
                    for b in range(2):
                        ins = pe.matmul(ps[:, MISC + b, :], lhs, x_t[:, bass.ds(c * T1 + b * BANK, BANK)],
                                        start=True, stop=True)
                    ins.then_inc(sem("s_raw"), 1)
                for j in range(NT):
                    first, end = j == 0, j == NT - 1
                    pe.wait_ge(sem("masked"), c * NT + (j + 1))
                    pe.sem_inc(sem("pe_settled"), 1)
                    for b in range(2):
                        cols = slice(b * BANK, (b + 1) * BANK)
                        for h in range(HEADS):
                            pe.matmul(ps[F * h:F * (h + 1), DEN + b, :], stat_s[:, j, h, :], s8[:, j % N_S, h, cols],
                                      start=first, stop=False)
                        for h in range(HEADS):
                            ins = pe.matmul(ps[F * h:F * (h + 1), DEN + b, :], stat_m[:, j, h, :], m1[:, j % N_S, cols],
                                            start=False, stop=end)
                    ins.then_inc(sem("den_summed"), 1)
                    pe.wait_ge(sem("w_ready"), c * NT + (j + 1))
                    for b in range(2):
                        cols = slice(b * BANK, (b + 1) * BANK)
                        for h in range(HEADS):
                            ins = pe.matmul(ps[F * h:F * (h + 1), NUM + b, :], bh[:, j, F * h:F * (h + 1)],
                                            w_ring[:, j % N_W, h, cols], start=first, stop=end)
                    ins.then_inc(sem("num_summed"), 1)
                    for b in range(2):
                        ins = pe.matmul(ps[0:32, SUM + b, :], ones[:], ring[:, j % RING, b * BANK:(b + 1) * BANK],
                                        start=first, stop=end)
                    ins.then_inc(sem("adj_free"), 1)
                pe.wait_ge(sem("s_taken"), c * (HEADS + 1) + HEADS + 1)
                pe.wait_ge(sem("den_taken"), c + 1)
                for b in range(2):
                    ins = pe.matmul(ps[:, MISC + b, :], sel[:, 0, :], den_raw[:, b * BANK:(b + 1) * BANK], start=True, stop=True)
                ins.then_inc(sem("p_raw"), 1)
                for b in range(2):
                    ins = pe.matmul(ps[:, DEN + b, :], sel[:, 1, :], den_raw[:, b * BANK:(b + 1) * BANK], start=True, stop=True)
                ins.then_inc(sem("q_raw"), 1)
                pe.wait_ge(sem("sum_taken"), c + 1)
                pe.sem_inc(sem("pe_settled"), 1)
                for q in range(Q1):
                    pe.transpose(ps[:, SUM, q * 64:q * 64 + 32], sum_raw[:, q * P:(q + 1) * P], ident[0:32, 0:32])
                pe.wait_ge(sem("o_ready"), c + 1)
                for q in range(Q1):
                    ins = pe.transpose(tiles8(MISC)[:, q, :], den[:, q * P:(q + 1) * P], ident[:])
                ins.then_inc(sem("o_turned"), 1)

            with pe.Fori(0, C1) as c:
                chunk1(c)
            if stop == 2:
                return

            def turn_in(layer, x, ready):
                pe.wait_ge(sem(ready), C1)
                for g in range(NT // 4):
                    if g >= 2:
                        pe.wait_ge(sem(f"x_t_ready_{layer}"), g - 1)
                    for q in range(4):
                        ins = pe.transpose(ps[:, PREP + g % 2, q * P:(q + 1) * P], x[:, 4 * g + q, :], ident[:])
                    ins.then_inc(sem(f"x_turned_{layer}"), 1)
                pe.wait_ge(sem(f"x_t_ready_{layer}"), NT // 4)

            def by_weight(w, raw, taken):
                for g in range(NT // 4):
                    if g >= 2:
                        pe.wait_ge(sem(taken), g - 1)
                    for q in range(4):
                        ins = pe.matmul(tiles(TURN + g % 2)[:, q, :], x2_t[:, (4 * g + q) * P:(4 * g + q + 1) * P],
                                        w[:], start=True, stop=True)
                    ins.then_inc(sem(raw), 1)

            def aggregate_all(layer, c, turned, free, value):
                for j in range(NT):
                    pe.wait_ge(sem(f"adj_in{j % RING}"),
                               c * (16 * NT // RING) + 16 * (layer * LOADS // RING + j // RING + 1))
                    for b in range(2):
                        ins = pe.matmul(ps[:, ACC + b, :], sup[:, j, :], ring[:, j % RING, b * BANK:(b + 1) * BANK],
                                        start=j == 0, stop=j == NT - 1)
                    ins.then_inc(sem("adj_free"), 1)
                pe.wait_ge(sem(free), value)
                pe.wait_ge(sem(f"acc_taken_{layer}"), c + 1)
                for q in range(Q1):
                    ins = pe.transpose(tiles8(TURN)[:, q, :], acc[:, q * P:(q + 1) * P], ident[:])
                ins.then_inc(sem(turned), 1)

            turn_in(2, xa, "x2_ready")
            by_weight(w2_t, "sup_raw", "sup_ready")
            pe.wait_ge(sem("sup_ready"), NT // 4)

            def chunk2(c):
                aggregate_all(2, c, "s2_turned", "turn_taken", c + 1)

            with pe.Fori(0, C1) as c:
                chunk2(c)
            if stop == 3:
                return

            turn_in(3, xb, "x3_ready")
            by_weight(w3_t, "mx_raw", "mx_ready")
            pe.wait_ge(sem("xt_ready"), 1)

            def chunk3(c):
                aggregate_all(3, c, "s_turned", "sq_ready", c * 2 + 1)

            with pe.Fori(0, C1) as c:
                chunk3(c)


_VECTORS = {"gcn_b": "L0_gnn_gcn_b", "ln_g": "L0_gnn_ln_g", "ln_b": "L0_gnn_ln_b", "gcn_w": "L0_gnn_gcn_w",
            "w_in": "L0_gnn_w_in", "conv_w": "L0_gnn_conv_w", "conv_b": "L0_gnn_conv_b", "w_dt": "L0_gnn_w_dt",
            "b_dt": "L0_gnn_b_dt", "a_log": "L0_gnn_A_log", "d_skip": "L0_gnn_D_skip", "w_out": "L0_gnn_w_out"}


def kernel(**inputs):
    import numpy as np
    import concourse.bacc as bacc
    from concourse.bass_utils import run_bass_kernel_spmd

    arrays = {k: inputs[name] for k, name in _VECTORS.items()}
    for k in ("conv_b", "b_dt", "d_skip"):
        arrays[k] = arrays[k].reshape(KD, P).T
    arrays["x"] = inputs["x"]
    arrays["adj_t"] = inputs["adj"].T
    w_xp = inputs["L0_gnn_w_xp"]
    arrays["w_r"] = w_xp[:, 0:RANK]
    arrays["w_bc"] = np.concatenate([w_xp[:, RANK:]] * PARTS, axis=1)
    arrays["w1"] = inputs["L1_gnn_W"]
    arrays["w1_t"] = inputs["L1_gnn_W"].T
    arrays["w2_t"] = inputs["L2_gnn_W"].T
    arrays["w3_t"] = inputs["L3_gnn_weight"].T
    arrays["bias3"] = inputs["L3_gnn_bias"]
    a_bd = np.zeros((D, 2 * HEADS), np.float32)
    sel = np.zeros((P, 2 * P), np.float32)
    for h in range(HEADS):
        rows = slice(F * h, F * (h + 1))
        a_bd[rows, h] = inputs["L1_gnn_a_dst"][h]
        a_bd[rows, HEADS + h] = inputs["L1_gnn_a_src"][h]
        sel[F * h:F * h + PARTS, rows] = 0.5
        sel[F * h + PARTS:F * h + 2 * PARTS, P + F * h:P + F * (h + 1)] = 0.5
    arrays["a_bd"], arrays["sel"] = a_bd, sel
    arrays["ident"] = np.eye(P, dtype=np.float32)
    arrays["row_is"] = np.tile(np.eye(32, dtype=np.float32), (PARTS, 1))
    arrays = {k: np.ascontiguousarray(a) for k, a in arrays.items()}
    nc = bacc.Bacc("TRN2", target_bir_lowering=False, num_devices=1)
    t = {k: nc.dram_tensor(f"in_{k}", a.shape, mybir.dt.from_np(a.dtype), kind="ExternalInput").ap()
         for k, a in arrays.items()}
    out = nc.dram_tensor("out_x", (N, D), F32, kind="ExternalOutput").ap()
    build_program(nc, t, out)
    r = run_bass_kernel_spmd(nc, [{f"in_{k}": a for k, a in arrays.items()}], core_ids=[0])
    return r.results[0]["out_x"]
```

```python
from contextlib import ExitStack

import numpy as np

import concourse.bass as bass
from concourse import mybir

F32 = mybir.dt.float32
BF16 = mybir.dt.bfloat16
FP8 = mybir.dt.float8e4
U8 = mybir.dt.uint8
U32 = mybir.dt.uint32
ALU = mybir.AluOpType
ACT = mybir.ActivationFunctionType
AX_X = mybir.AxisListType.X

P = 128
N = 4096
D = 128
NT = N // P
BANK = 512
EPS = 1e-5

DI = 256
KD = DI // P
S_N = 16
RANK = 8
TAPS = 4
T0 = 512
C0 = N // T0
Q0 = T0 // P
STEPS = KD * S_N
RATE0 = 112
ACT_RATE0 = 5
N_DA, N_DBU, N_H, N_CS = 4, 4, 4, 4
HC_CREDIT = KD * N_CS
DBU_CREDIT = 2 * KD
PAIR_CREDIT = KD + 1
PAIRS = STEPS // 2
N_PAIR = 8
Y_LAG = 7
AT_GCN, AT_G_STATS, AT_G_RSTD, AT_G_NORM = 1, 2, 2, 6
AT_TURN, AT_H_T, AT_XC, AT_XC_OUT, AT_Z, AT_CONV, AT_SILU = 8, 9, 11, 12, 13, 14, 18
AT_BC, AT_BC_SPLIT, AT_DT_RAW, AT_SOFTPLUS, AT_DT = 20, 21, 24, 25, 29
AT_GATE, AT_OUT, AT_X1_STATS, AT_X1_RSTD, AT_X1 = 7, 8, 10, 10, 14


def at(chunk, rate, k):
    pair, offset = chunk
    return pair * (2 * rate) + (offset * rate + k)

HEADS = 4
F = D // HEADS
T1 = 1024
C1 = N // T1
Q1 = T1 // P
PARTS = 3
N_W, N_V, N_S = 2, 4, 4
DVE_HEADS = 2
R_ORDER = (2, 3, 0, 1)
RELU_CREDIT = 1
NUM_CREDIT = 8
DEG = 2 * PARTS
MASKED = 8
SUMS_AT = 0
TURN_AT = 4
ATTEND_AT = 6
RSTD_AT = 7
FINISH_AT = 9
PREFILL_AT = NT - 6
LEAKY = 0.2
E_MAX = 60.0
RATE2 = 12
RATE3 = 18
R_MAX = np.float32(np.exp(E_MAX))
RATE1 = 97
L1_LN = C0
MIN_SQ = 1e-30
MAX_NORM = float(np.float32(1.0 - 1e-5))
ATANH_MAX = 1.0 - 1e-7
LEAST_GAP = 1.0 - MAX_NORM ** 2
ATANH_OF_MAX = float(np.arctanh(MAX_NORM))
FLAT_SQ = 1e-7

X_PARTS = 4
RING = 8
LOADS = NT * N // T1


FIRST = (0, 0)
LOOPS0 = (C0 - 3) // 2
AFTER = [(LOOPS0, offset) for offset in range(1, C0 - 2 * LOOPS0)]


def act_masks(j):
    return j % 2 == 0


def in_loop(pair):
    return [(pair, 1), (pair, 2)]


def neighbour(chunk, distance):
    return chunk[0], chunk[1] + distance


def has_next(chunk):
    return not isinstance(chunk[0], int) or chunk != AFTER[-1]


def has_previous(chunk):
    return chunk[1] > 0


class Link:

    def __init__(self, eng, sem):
        self.eng, self.sem, self.start, self.k, self.origin = eng, sem, 0, 0, 0

    def body(self, c, rate):
        self.origin, self.k, self.rate = self.start + rate * c, 0, rate

    def leave(self, rounds):
        assert self.k == self.rate, f"the rate of {self.sem} is {self.k}"
        self.start += self.rate * rounds
        self.origin, self.k = self.start, 0

    def mark(self, ins):
        ins.then_inc(self.sem, 1)
        self.k += 1
        return self.k

    def wait(self, k=None):
        self.eng.wait_ge(self.sem, self.origin + (self.k if k is None else k))

    def __call__(self, ins):
        self.mark(ins)
        self.wait()

    def straight(self):
        self.start += self.k
        self.origin, self.k = self.start, 0


def build_program(nc, t, out, stop=4):
    adj_t = t["adj_t"]
    ctx = ExitStack()
    with ctx:
        sems = {}

        def sem(name):
            if name not in sems:
                sems[name] = ctx.enter_context(nc.semaphore(name))
            return sems[name]

        def sb(stack, name, shape, dt=F32):
            return stack.enter_context(nc.sbuf_tensor(name, shape, dt))

        ring = sb(ctx, "ring", [P, RING, T1])
        xa = sb(ctx, "xa", [P, NT, D])
        xb = sb(ctx, "xb", [P, NT, D])
        ident = sb(ctx, "ident", [P, P])
        half_neg = sb(ctx, "half_neg", [P, NT])
        half_pos = sb(ctx, "half_pos", [P, 2 * Q1])
        eps = sb(ctx, "eps", [P, Q1])
        w1_cat = sb(ctx, "w1_cat", [P, D + 2 * HEADS])
        w1_t = sb(ctx, "w1_t", [P, D])
        a_bd = sb(ctx, "a_bd", [P, 2 * HEADS])
        w2_t = sb(ctx, "w2_t", [P, D])
        w3_t = sb(ctx, "w3_t", [P, D])
        w3 = sb(ctx, "w3", [P, D])
        bias3 = sb(ctx, "bias3", [P, D])
        bias3_col = sb(ctx, "bias3_col", [P, 1])
        deg = sb(ctx, "deg", [P, NT])
        ln_st = sb(ctx, "ln_st", [P, Q1, 6])
        ln_mv = sb(ctx, "ln_mv", [P, Q1, 2])
        ln_rs = sb(ctx, "ln_rs", [P, Q1])
        ps = ctx.enter_context(nc.psum_tensor("ps", [P, 8, BANK], F32))

        with ExitStack() as l0:
            gcn_w = sb(l0, "gcn_w", [P, D])
            gcn_b = sb(l0, "gcn_b", [P, D])
            ln_g = sb(l0, "ln_g", [P, 1])
            ln_b = sb(l0, "ln_b", [P, 1])
            w_in = sb(l0, "w_in", [P, 2 * DI])
            conv_w = sb(l0, "conv_w", [P, KD, TAPS])
            conv_b = sb(l0, "conv_b", [P, KD])
            w_bc = sb(l0, "w_bc", [P, KD, 3 * 32])
            w_r = sb(l0, "w_r", [P, KD, RANK])
            w_dt = sb(l0, "w_dt", [RANK, DI])
            b_dt = sb(l0, "b_dt", [P, KD])
            a_neg = sb(l0, "a_neg", [P, KD, S_N])
            d_skip = sb(l0, "d_skip", [P, KD])
            w_out = sb(l0, "w_out", [P, KD, D])
            row_is = sb(l0, "row_is", [96, 32])
            pick = sb(l0, "pick", [96, 32, P], BF16)
            ax_t = sb(l0, "ax_t", [P, T0])
            g_act = sb(l0, "g_act", [P, Q0, D])
            h_norm = sb(l0, "h_norm", [P, Q0, D])
            xc = sb(l0, "xc", [P, KD, TAPS - 1 + T0])
            conv = sb(l0, "conv", [P, KD, T0])
            u = sb(l0, "u", [P, 2, KD, T0])
            sz = sb(l0, "sz", [P, 2, KD, T0])
            rank_t = sb(l0, "rank_t", [RANK, T0])
            bc1 = sb(l0, "bc1", [96, T0], BF16)
            bc2 = sb(l0, "bc2", [96, T0], BF16)
            bc_parts = sb(l0, "bc_parts", [96, 2, T0], BF16)
            bc_rest = sb(l0, "bc_rest", [96, T0])
            sp_e = sb(l0, "sp_e", [P, KD, T0])
            sp_v = sb(l0, "sp_v", [P, KD, T0])
            dt = sb(l0, "dt", [P, 2, KD, T0])
            du = sb(l0, "du", [P, 2, KD, T0])
            da = sb(l0, "da", [P, N_DA, T0])
            dbu = sb(l0, "dbu", [P, N_DBU, T0])
            hs = sb(l0, "hs", [P, N_H, T0])
            h_last = sb(l0, "h_last", [P, STEPS])
            cs = sb(l0, "cs", [P, N_CS, T0])
            hc = sb(l0, "hc", [P, N_PAIR, T0])
            hc_odd = sb(l0, "hc_odd", [P, 2, KD, T0])
            yg = sb(l0, "yg", [P, KD, T0])
            xo = sb(l0, "xo", [P, Q0, D])
            ln0_st = sb(l0, "ln0_st", [P, Q0, 6])
            ln0_mv = sb(l0, "ln0_mv", [P, Q0, 2])
            ln0_rs = sb(l0, "ln0_rs", [P, Q0])
            ln1_rs = sb(l0, "ln1_rs", [P, Q0])
            ln1_mv = sb(l0, "ln1_mv", [P, Q0, 2])
            ln1_st = sb(l0, "ln1_st", [P, Q0, 6])

        with ExitStack() as l1:
            v_ring = sb(l1, "v_ring", [P, N_V, HEADS - DVE_HEADS, T1])
            x_t = v_ring[:, 0:2].rearrange("p v h i -> p (v h i)")
            bh = sb(l1, "bh", [P, NT, D])
            stat_s = sb(l1, "stat_s", [P, NT, HEADS, 32], BF16)
            stat_m = sb(l1, "stat_m", [P, NT, 32], BF16)
            r_rows = sb(l1, "r_rows", [P, HEADS, T1])
            w_ring = sb(l1, "w_ring", [P, N_W, DVE_HEADS, T1])
            s8 = sb(l1, "s8", [P, N_S, HEADS, T1], FP8)
            m1 = sb(l1, "m1", [P, N_S, T1], FP8)
            dh = sb(l1, "dh", [P, NT, (HEADS - DVE_HEADS) * F])
            e_all = sb(l1, "e_all", [P, NT, 2 * HEADS])
            d_max = sb(l1, "d_max", [P, HEADS])
            d_all = sb(l1, "d_all", [P, HEADS])
            dv = e_all[:, :, 0:HEADS]
            r_now = e_all[:, 0:Q1, HEADS:]
            e_neg = sb(l1, "e_neg", [P, NT, HEADS])
            neg_c = e_neg
            bv = sb(l1, "bv", [P, NT, HEADS])
            cv = sb(l1, "cv", [P, NT, HEADS])
            r_nat = sb(l1, "r_nat", [P, NT + Q1, HEADS])
            deg_col = sb(l1, "deg_col", [P, F])
            den_raw = sb(l1, "den_raw", [P, T1])
            num_raw = sb(l1, "num_raw", [P, T1])
            den_p = sb(l1, "den_p", [P, Q1, HEADS])
            den_q = sb(l1, "den_q", [P, Q1, HEADS])
            den_m = sb(l1, "den_m", [P, Q1, HEADS])
            xo1 = sb(l1, "xo1", [P, Q1, D])
        with ExitStack() as l2:
            x2_t = sb(l2, "x2_t", [P, N])
            sup = sb(l2, "sup", [P, NT, D])
            dis = sb(l2, "dis", [P, NT])
            acc = sb(l2, "acc", [P, T1])
            xo2 = sb(l2, "xo2", [P, Q1, D])
            big = sb(l2, "big", [P, NT, D])
            sums = sb(l2, "sums", [P, 2 * NT + 1])
            norms = sb(l2, "norms", [P, 2 * NT + 1])
            recips = sb(l2, "recips", [P, 2 * NT + 1])
            dots = sb(l2, "dots", [P, NT])
            w3b = sb(l2, "w3b", [P, 1])
            ln_plus, ln_minus, arg, tanh_e, tanh, gap, sq_norm, tmp = [
                sb(l2, name, [P, NT + 1]) for name in
                ("ln_plus", "ln_minus", "arg", "tanh_e", "tanh", "gap", "sq_norm", "tmp")]
            clipped, r_den, cx, cy, gap2, norm2, ln_norm2, by_norm2, clip2, ln_plus2, ln_gap2 = [
                sb(l2, name, [P, NT]) for name in
                ("clipped", "r_den", "cx", "cy", "gap2", "norm2", "ln_norm2", "by_norm2", "clip2", "ln_plus2", "ln_gap2")]
            hyp_bias = sb(l2, "hyp_bias", [P, D])
            bias_part = sb(l2, "bias_part", [P, 4, D])
            rl = sb(l2, "rl", [P, Q1, D])
            sq = sb(l2, "sq", [P, 2, Q1, D])
            f_sq, f_norm, f_recip = [sb(l2, name, [P, 2, Q1]) for name in ("f_sq", "f_norm", "f_recip")]
            f_k, f_arg, f_tanh = [sb(l2, name, [P, Q1]) for name in ("f_k", "f_arg", "f_tanh")]
            xo3 = sb(l2, "xo3", [P, Q1, D])
        ACC, PREP, TURN = 0, 4, 6

        NUM, DEN, NAT, RAW = 0, 2, 4, 6
        two = lambda bank: ps[:, bank:bank + 2, :].rearrange("p a b -> p (a b)")
        tiles8 = lambda bank: ps[:, bank:bank + 2, :].rearrange("p a (q d) -> p (a q) d", d=D)

        AX, M0, M1, BB, CB, Y = 0, 1, 2, 3, 5, 6
        tiles = lambda bank: ps[:, bank, :].rearrange("p (q d) -> p q d", q=Q0)

        setup_dmas = [
            (ident, t["ident"]), (gcn_w, t["gcn_w"]), (w_in, t["w_in"]),
            (gcn_b, t["gcn_b"].rearrange("(a d) -> a d", a=1).broadcast_to([P, D])),
            (ln_g, t["ln_g"].rearrange("(p a) -> p a", a=1)), (ln_b, t["ln_b"].rearrange("(p a) -> p a", a=1)),
            (conv_w, t["conv_w"].rearrange("(k p) w -> p k w", p=P)),
            (conv_b, t["conv_b"]),
            (w_bc, t["w_bc"].rearrange("(k p) r -> p k r", p=P)),
            (w_r, t["w_r"].rearrange("(k p) r -> p k r", p=P)),
            (w_dt, t["w_dt"]), (b_dt, t["b_dt"]),
            (a_neg, t["a_log"].rearrange("(k p) n -> p k n", p=P)),
            (d_skip, t["d_skip"]),
            (w_out, t["w_out"].rearrange("(k p) m -> p k m", p=P)), (row_is, t["row_is"]),
            (w1_t, t["w1_t"]), (a_bd, t["a_bd"]), (w2_t, t["w2_t"]), (w3_t, t["w3_t"]),
            (w3, t["w3"]), (bias3_col, t["bias3"].rearrange("(p a) -> p a", a=1)),
            (bias3, t["bias3"].rearrange("(a d) -> a d", a=1).broadcast_to([P, D])),
        ]
        setup_all = 16 * (len(setup_dmas) + 1)

        block = ctx.enter_context(nc.Block())

        @block.sync
        def _(sp):
            x_rows = t["x"].rearrange("(t p) d -> p t d", p=P)

            def load_x(part):
                rows = slice(part * NT // X_PARTS, (part + 1) * NT // X_PARTS)
                sp.dma_start(xa[:, rows, :], x_rows[:, rows, :]).then_inc(sem(f"x_in{part}"), 16)

            adj0 = adj_t.rearrange("(r two p) i -> r p two i", two=2, p=P)

            def load0(c, r):
                slot = r % RING
                sp.dma_start(ring[:, slot, :].rearrange("p (two i) -> p two i", two=2),
                             adj0[r][:, :, bass.ts(c, T0)]).then_inc(sem(f"adj_in{slot}"), 16)

            for r in range(NT // 2):
                if r < X_PARTS:
                    load_x(r)
                if r >= RING:
                    sp.wait_ge(sem("adj_free"), r - RING + 1)
                load0(0, r)
            with sp.Fori(1, C0) as c:
                for r in range(NT // 2):
                    sp.wait_ge(sem("adj_free"), c * (NT // 2) + (r - RING + 1))
                    load0(c, r)
            def load1(layer, c, r):
                if layer == 1:
                    sp.wait_ge(sem("num_summed"), c * NT + (NUM_CREDIT + r - RING + 1))
                else:
                    sp.wait_ge(sem("adj_free"), c * NT + ((layer - 1) * LOADS + r - RING + 1))
                sp.dma_start(ring[:, r % RING, :], adj_t[r * P:(r + 1) * P, bass.ts(c, T1)])\
                    .then_inc(sem(f"adj_in{r % RING}"), 16)

            for layer in range(1, stop):
                if layer == 1:
                    sp.wait_ge(sem("adj_free"), LOADS)
                elif layer == 2:
                    sp.wait_ge(sem("num_summed"), LOADS + NUM_CREDIT)
                with sp.Fori(0, C1) as c:
                    for r in range(NT):
                        load1(layer, c, r)
            if stop == 3:
                sp.wait_ge(sem("x3_ready"), C1)
                sp.dma_start(out.rearrange("(t p) d -> p t d", p=P), xb[:]).then_inc(sem("out_done"), 16)
                sp.wait_ge(sem("out_done"), 16)
            if stop == 4:
                rows = out.rearrange("(c q p) d -> c p q d", q=Q1, p=P)
                for c in range(C1):
                    sp.wait_ge(sem("x4_ready"), c + 1)
                    sp.dma_start(rows[c], xa[:, c * Q1:(c + 1) * Q1, :]).then_inc(sem("out_done"), 16)
                sp.wait_ge(sem("out_done"), 16 * C1)
            if stop == 2:
                sp.wait_ge(sem("x2_ready"), C1)
                sp.dma_start(out.rearrange("(t p) d -> p t d", p=P), xa[:]).then_inc(sem("out_done"), 16)
                sp.wait_ge(sem("out_done"), 16)
            if stop == 1:
                sp.wait_ge(sem("x1_ready"), C0)
                sp.dma_start(out.rearrange("(t p) d -> p t d", p=P), xb[:]).then_inc(sem("out_done"), 16)
                sp.wait_ge(sem("out_done"), 16)

        @block.gpsimd
        def _(pool):
            pool.memset(half_neg[:], -0.5).then_inc(sem("halves"), 1)
            pool.memset(half_pos[:], 0.5).then_inc(sem("halves"), 1)
            pool.memset(eps[:], EPS).then_inc(sem("halves"), 1)
            pool.memset(h_last[:], 0.0).then_inc(sem("zeroed"), 1)
            pool.memset(xc[:], 0.0).then_inc(sem("zeroed"), 1)
            pool.wait_ge(sem("halves"), 3)
            link = Link(pool, sem("pool_link"))

            def rstd(rs, mv, q, stats, value, ready):
                pool.wait_ge(stats, value)
                link(pool.tensor_tensor(rs[:, 0:q], mv[:, 0:q, 1], eps[:, 0:q], ALU.add))
                pool.tensor_tensor(rs[:, 0:q], rs[:, 0:q], half_neg[:, 0:q], ALU.pow).then_inc(ready, 1)

            def prepare(n, i):
                if i == AT_G_RSTD:
                    rstd(ln0_rs, ln0_mv, Q0, sem("h_stats"), at(n, 1, 1), sem("h_rstd"))

            def finish0(c):
                rstd(ln1_rs, ln1_mv, Q0, sem("x1_stats"), at(c, 1, 1), sem("x1_rstd"))

            def chunk0(c):
                for i in range(STEPS):
                    n, k = divmod(i, KD)
                    m = n // 2 * KD + k
                    if has_next(c):
                        prepare(neighbour(c, 1), i)
                    if i == AT_X1_RSTD and has_previous(c):
                        finish0(neighbour(c, -1))
                    pool.wait_ge(sem("scanned"), at(c, STEPS, N_DA + i + 1))
                    if k == 0:
                        pool.wait_ge(sem("c_rows"), at(c, S_N, n + 2))
                    if n % 2 == 0:
                        pool.wait_ge(sem("y_summed"), at(c, PAIRS, m + 1))
                        pool.tensor_tensor(hc[:, m % N_PAIR, :], hs[:, i % N_H, :], cs[:, n % N_CS, :],
                                           ALU.mult).then_inc(sem("hc_ready"), 1)
                    else:
                        odd = n // 2 % 2
                        if k == 0:
                            pool.wait_ge(sem("pair_ready"), at(c, PAIRS, m + 1))
                        pool.tensor_tensor(hc_odd[:, odd, k, :], hs[:, i % N_H, :], cs[:, n % N_CS, :],
                                           ALU.mult).then_inc(sem("hc_ready"), 1)
                        if k == KD - 1:
                            for kk in range(KD):
                                mm = m - k + kk
                                pool.wait_ge(sem("hc_ready"), at(c, STEPS, HC_CREDIT + i + 1 - k + kk))
                                pool.tensor_tensor(hc[:, mm % N_PAIR, :], hc[:, mm % N_PAIR, :], hc_odd[:, odd, kk, :],
                                                   ALU.add).then_inc(sem("pair_ready"), 1)

            for i in range(STEPS):
                prepare((0, 0), i)
            link.straight()
            pool.sem_inc(sem("hc_ready"), HC_CREDIT)
            pool.sem_inc(sem("pair_ready"), PAIR_CREDIT)
            chunk0(FIRST)
            link.straight()
            with pool.Fori(0, LOOPS0) as pair:
                link.body(pair, 4)
                for c in in_loop(pair):
                    chunk0(c)
            link.leave(LOOPS0)
            for c in AFTER:
                chunk0(c)
            finish0(AFTER[-1])
            link.straight()
            if stop == 1:
                return

            pool.wait_ge(sem("x1_ready"), C0)
            pool.memset(deg_col[:], 0.0).then_inc(sem("stat_zero"), 1)
            pool.memset(r_nat[:], 1.0).then_inc(sem("stat_zero"), 1)
            pool.memset(stat_s[:], 0.0).then_inc(sem("stat_zero"), 1)
            pool.memset(stat_m[:], 0.0).then_inc(sem("stat_zero"), 1)
            pool.wait_ge(sem("stat_zero"), 4)
            pool.memset(deg_col[:, DEG:DEG + 1], 1.0).then_inc(sem("stat_zero"), 1)
            pool.wait_ge(sem("d_max_ready"), 1)
            pool.partition_all_reduce(d_all[:], d_max[:], P, bass.bass_isa.ReduceOp.max).then_inc(sem("d_all_ready"), 1)

            def finish1(c):
                rstd(ln_rs, ln_mv, Q1, sem("x2_stats"), c + 1, sem("x2_rstd"))

            def chunk1(c, first):
                if not first:
                    link.body(c - 1, 1)
                for j in range(NT):
                    adj = ring[:, j % RING, :].unsqueeze(1).broadcast_to([P, HEADS - DVE_HEADS, T1])
                    pool.wait_ge(sem(f"adj_in{j % RING}"), c * (16 * NT // RING) + 16 * (LOADS // RING + j // RING + 1))
                    pool.wait_ge(sem("relu_ready"), c * NT + (j + 1 + RELU_CREDIT))
                    pool.tensor_tensor(v_ring[:, j % N_V], v_ring[:, j % N_V], adj, ALU.mult).then_inc(sem("v_ready"), 1)
                    if j == RSTD_AT and not first:
                        finish1(c - 1)

            chunk1(0, True)
            with pool.Fori(1, C1) as c:
                chunk1(c, False)
            link.leave(C1 - 1)
            finish1(C1 - 1)
            link.straight()
            if stop == 2:
                return

            pool.wait_ge(sem("x2_ready"), C1)
            pool.tensor_scalar(dis[:], deg[:], 1.0, None, ALU.add).then_inc(sem("deg_plus"), 1)
            pool.wait_ge(sem("deg_plus"), 1)
            pool.tensor_tensor(dis[:], dis[:], half_neg[:], ALU.pow).then_inc(sem("dis_ready"), 1)

            def norm2(c):
                link.body(c, 1)
                rstd(ln_rs, ln_mv, Q1, sem("x3_stats"), c + 1, sem("x3_rstd"))

            with pool.Fori(0, C1) as c:
                norm2(c)
            link.leave(C1)
            if stop == 3:
                return

            def norm3(c):
                link.body(c, 1)
                pool.wait_ge(sem("f_sq_ready"), c + 1)
                pool.tensor_tensor(f_norm[:].rearrange("p a q -> p (a q)"), f_sq[:].rearrange("p a q -> p (a q)"),
                                   half_pos[:, 0:2 * Q1], ALU.pow).then_inc(sem("f_norm_ready"), 1)
                rstd(ln_rs, ln_mv, Q1, sem("x4_stats"), c + 1, sem("x4_rstd"))

            with pool.Fori(0, C1) as c:
                norm3(c)
            link.leave(C1)

        @block.scalar
        def _(act):
            for dst, src in setup_dmas:
                act.dma_start(dst[:], src).then_inc(sem("setup"), 16)
            act.dma_start(w1_cat[:, 0:D], t["w1"]).then_inc(sem("setup"), 16)
            act.wait_ge(sem("setup"), setup_all)
            link = Link(act, sem("act_link"))
            link(act.activation(a_neg[:], a_neg[:], ACT.Exp))
            act.mul(a_neg[:], a_neg[:], -1.0).then_inc(sem("a_ready"), 1)
            act.wait_ge(sem("a_ready"), 1)
            act.wait_ge(sem("zeroed"), 2)
            link.straight()

            def take_ax(n):
                act.wait_ge(sem("adj_free"), at(n, NT // 2, NT // 2))
                act.copy(ax_t[:], ps[:, AX, :]).then_inc(sem("ax_taken"), 1)

            def prepare(n, i, first=False):
                half = n[1] % 2
                if i == AT_H_T:
                    if not first:
                        act.wait_ge(sem("conv_ready"), at(n, KD, 0))
                    link.mark(act.copy(xc[:, :, 0:TAPS - 1], xc[:, :, T0:T0 + TAPS - 1]))
                    act.wait_ge(sem("h_turned"), at(n, 1, 1))
                    act.activation(ax_t[:], ps[:, M0, :], ACT.Identity, bias=ln_b[:, 0:1],
                                   scale=ln_g[:, 0:1]).then_inc(sem("h_t_ready"), 1)
                    link.wait()
                if i == AT_XC_OUT:
                    for k in range(KD):
                        act.wait_ge(sem("xz_ready"), at(n, 4, k + 1))
                        act.copy(xc[:, k, TAPS - 1:], ps[:, M0 + k, :]).then_inc(sem("xc_ready"), 1)
                if i == AT_SILU:
                    for k in range(KD):
                        act.wait_ge(sem("xz_ready"), at(n, 4, KD + k + 1))
                        act.activation(sz[:, half, k, :], ps[:, M0 + k, :], ACT.Silu).then_inc(sem("z_ready"), 1)
                    for k in range(KD):
                        act.wait_ge(sem("conv_ready"), at(n, KD, k + 1))
                        act.activation(u[:, half, k, :], conv[:, k, :], ACT.Silu,
                                       bias=conv_b[:, k:k + 1]).then_inc(sem("u_ready"), 1)
                    act.preload_act_table_set("natural_log_exp_and_others")
                if i == AT_BC + 1:
                    act.wait_ge(sem("rank_ready"), at(n, 1, 1))
                    act.copy(rank_t[:], ps[0:RANK, M1, :]).then_inc(sem("rank_taken"), 1)
                if i == AT_SOFTPLUS:
                    for k in range(KD):
                        act.wait_ge(sem("dt_raw"), at(n, KD, k + 1))
                        link.mark(act.activation(sp_v[:, k, :], ps[:, M0 + k, :], ACT.Identity, bias=b_dt[:, k:k + 1]))
                    link.wait()
                    link.mark(act.activation(sp_e[:], sp_v[:], ACT.Abs))
                if i == AT_SOFTPLUS + 1:
                    link.wait()
                    link.mark(act.activation(sp_e[:], sp_e[:], ACT.Exp, scale=-1.0))
                if i == AT_SOFTPLUS + 2:
                    link.wait()
                    act.activation(sp_e[:], sp_e[:], ACT.Ln, bias=1.0).then_inc(sem("sp_ready"), 1)

            def chunk0(c):
                half = c[1] % 2
                if has_next(c):
                    take_ax(neighbour(c, 1))
                for i in range(STEPS):
                    n, k = divmod(i, KD)
                    if i == 0:
                        act.wait_ge(sem("dt_done"), at(c, 1, 1))
                    act.wait_ge(sem("scanned"), at(c, STEPS, i + 1))
                    act.activation(da[:, i % N_DA, :], dt[:, half, k, :], ACT.Exp,
                                   scale=a_neg[:, k, n:n + 1]).then_inc(sem("da_ready"), 1)
                    if k == 0:
                        act.wait_ge(sem("c_bcast"), at(c, S_N, n + 1))
                        act.wait_ge(sem("hc_ready"), at(c, STEPS, KD * n + KD))
                        act.copy(cs[:, n % N_CS, :], ps[:, CB, :]).then_inc(sem("c_rows"), 1)
                    if has_next(c):
                        prepare(neighbour(c, 1), i)

            take_ax((0, 0))
            for i in range(STEPS):
                prepare((0, 0), i, first=True)
            link.straight()
            act.sem_inc(sem("c_rows"), 1)
            chunk0(FIRST)
            link.straight()
            with act.Fori(0, LOOPS0) as pair:
                link.body(pair, 2 * ACT_RATE0)
                for c in in_loop(pair):
                    chunk0(c)
            link.leave(LOOPS0)
            for c in AFTER:
                chunk0(c)
            link.straight()
            if stop == 1:
                return

            act.wait_ge(sem("x1_ready"), C0)
            for g in range(NT // 4):
                act.wait_ge(sem("x1_turned"), g + 1)
                act.copy(x_t[:, g * BANK:(g + 1) * BANK], ps[:, NAT + g % 2, :]).then_inc(sem("x1_t_ready"), 1)
            for g in range(NT // 2):
                act.wait_ge(sem("h_raw"), g + 1)
                src = ps[:, NAT + g % 2, 0:2 * (D + 2 * HEADS)].rearrange("p (a b) -> p a b", a=2)
                act.copy(bh[:, 2 * g:2 * g + 2, :], src[:, :, 0:D])
                act.copy(e_all[:, 2 * g:2 * g + 2, :], src[:, :, D:]).then_inc(sem("h_taken"), 1)
            act.wait_ge(sem("e_ready"), 1)
            act.wait_ge(sem("stat_zero"), 4)
            act.activation(bv[:], e_all[:, :, 0:HEADS], ACT.Exp)
            act.activation(cv[:], e_neg[:], ACT.Exp)
            act.activation(r_nat[:, 0:NT, :], e_all[:, :, HEADS:], ACT.Exp, scale=1 - LEAKY).then_inc(sem("bc_ready"), 1)
            act.wait_ge(sem("neg_c_ready"), 1)
            act.sem_inc(sem("relu_ready"), RELU_CREDIT)
            act.sem_inc(sem("sign_ready"), 1)

            def take_r(c, ahead, heads):
                act.wait_ge(sem("relu_ready"), c * NT + (ahead * NT + RELU_CREDIT))
                for h in heads:
                    act.wait_ge(sem("r_raw"), c * HEADS + (ahead * HEADS + R_ORDER.index(h) + 1))
                    if h == 1:
                        act.wait_ge(sem("w_ready"), c * NT + (ahead * NT + 1))
                    act.copy(r_rows[:, h, :], two(RAW if h % 2 else NAT)).then_inc(sem("r_taken"), 1)


            def take_sums1(c):
                act.wait_ge(sem("den_summed"), c * NT + (NT + N_S))
                act.copy(den_raw[:], two(DEN)).then_inc(sem("sums_taken"), 1)
                act.copy(num_raw[:], two(NUM)).then_inc(sem("sums_taken"), 1)

            def signs(c, j):
                act.wait_ge(sem("v_ready"), c * NT + (j + 1))
                act.wait_ge(sem("den_summed"), c * NT + (j + 1))
                act.sem_inc(sem("act_settled"), 1)
                act.activation(s8[:, j % N_S, DVE_HEADS:, :], v_ring[:, j % N_V], ACT.Sign,
                               saturate=False).then_inc(sem("sign_ready"), 1)

            def chunk1(c, first):
                for j in range(NT):
                    if act_masks(j):
                        act.wait_ge(sem(f"adj_in{j % RING}"), c * (16 * NT // RING) + 16 * (LOADS // RING + j // RING + 1))
                        act.wait_ge(sem("den_summed"), c * NT + (j + 1))
                        act.sem_inc(sem("act_settled"), 1)
                        act.activation(m1[:, j % N_S, :], ring[:, j % RING, :], ACT.Sign,
                                       saturate=False).then_inc(sem("mask_ready"), 1)
                    act.wait_ge(sem("num_summed"), c * NT + (NUM_CREDIT - N_V + j + 1))
                    if j < N_V:
                        act.wait_ge(sem("sign_ready"), c * NT + 1)
                    for h in range(DVE_HEADS, HEADS):
                        ins = act.activation(v_ring[:, j % N_V, h - DVE_HEADS, :], r_rows[:, h, :], ACT.Relu,
                                             bias=neg_c[:, j, h:h + 1])
                    ins.then_inc(sem("relu_ready"), 1)
                    if j >= 1:
                        signs(c, j - 1)
                    if j == SUMS_AT and not first:
                        take_sums1(c - 1)
                take_r(c, 1, (2, 3))
                signs(c, NT - 1)
                take_r(c, 1, (1,))
                act.wait_ge(sem("r_taken"), c * 3 + 6)

            take_r(0, 0, (2, 3, 1))
            act.wait_ge(sem("r_taken"), 3)
            chunk1(0, True)
            with act.Fori(1, C1) as c:
                chunk1(c, False)
            take_sums1(C1 - 1)
            if stop == 2:
                return

            def take_mx(g):
                act.wait_ge(sem("mx_raw"), g + 1)
                act.wait_ge(sem("mx_summed"), g + 1)
                act.copy(big[:, 4 * g:4 * g + 4, :], tiles(TURN + g % 2)).then_inc(sem("mx_copied"), 1)
                act.activation(sq[:, g % 2, 0:4, :], tiles(TURN + g % 2), ACT.Square).then_inc(sem("mx_ready"), 1)

            def turn_in(layer, with_mx=False):
                for g in range(NT // 4):
                    act.wait_ge(sem(f"x_turned_{layer}"), g + 1)
                    act.copy(x2_t[:, g * BANK:(g + 1) * BANK], ps[:, PREP + g % 2, :]).then_inc(sem(f"x_t_ready_{layer}"), 1)
                    if with_mx and g >= 1:
                        take_mx(g - 1)
                if with_mx:
                    take_mx(NT // 4 - 1)

            def take_sums(layer, c):
                act.wait_ge(sem("adj_free"), c * NT + ((layer - 1) * LOADS + NT))
                act.copy(acc[:], two(ACC)).then_inc(sem(f"acc_taken_{layer}"), 1)

            turn_in(2)
            with act.Fori(0, C1) as c:
                take_sums(2, c)
            if stop == 3:
                return

            act.wait_ge(sem("w3b_raw"), 1)
            act.copy(w3b[:], ps[:, ACC + 1, 0:1]).then_inc(sem("w3b_ready"), 1)
            turn_in(3, with_mx=True)
            act.activation(xo3[:, 0, :], bias3[:], ACT.Square, accum_out=sums[:, 2 * NT:]).then_inc(sem("sums_ready"), 1)
            act.preload_act_table_set("natural_log_exp_and_others")
            act.wait_ge(sem("sums_floor"), 1)
            act.activation(norms[:], sums[:], ACT.Ln).then_inc(sem("norms_ln"), 1)
            act.wait_ge(sem("norms_ln"), 1)
            act.activation(norms[:], norms[:], ACT.Exp, scale=0.5).then_inc(sem("norms_ready"), 1)
            act.wait_ge(sem("clipped_ready"), 1)
            act.activation(ln_plus[:, 0:NT], clipped[:], ACT.Ln, bias=1.0)
            act.activation(ln_minus[:, 0:NT], clipped[:], ACT.Ln, bias=1.0, scale=-1.0).then_inc(sem("atanh_ln"), 1)
            act.wait_ge(sem("tanh_in"), 1)
            act.activation(tanh_e[:], arg[:], ACT.Exp, scale=-2.0).then_inc(sem("tanh_exp"), 1)
            act.wait_ge(sem("norm2_sq"), 1)
            act.activation(ln_norm2[:], norm2[:], ACT.Ln).then_inc(sem("norm2_ln"), 1)
            act.wait_ge(sem("norm2_ln"), 1)
            act.activation(norm2[:], ln_norm2[:], ACT.Exp, scale=0.5)
            act.activation(by_norm2[:], ln_norm2[:], ACT.Exp, scale=-0.5)
            act.activation(ln_gap2[:], gap2[:], ACT.Ln).then_inc(sem("norm2_ready"), 1)
            act.wait_ge(sem("clip2_ready"), 1)
            act.activation(ln_plus2[:], clip2[:], ACT.Ln, bias=1.0).then_inc(sem("atanh2_ln"), 1)

            def chunk3(c):
                take_sums(3, c)
                act.wait_ge(sem("s_turned"), c + 1)
                act.wait_ge(sem("rl_used"), c + 1)
                act.activation(rl[:], tiles8(TURN), ACT.Relu).then_inc(sem("rl_ready"), 1)
                act.activation(sq[:, 0], tiles8(TURN), ACT.Square).then_inc(sem("turn3_taken"), 1)
                act.wait_ge(sem("rl_ready"), c + 1)
                act.activation(sq[:, 1], rl[:], ACT.Square).then_inc(sem("sq_ready"), 1)
                act.wait_ge(sem("f_arg_ready"), c + 1)
                act.activation(f_tanh[:], f_arg[:], ACT.Exp, scale=-2.0).then_inc(sem("f_exp"), 1)

            act.sem_inc(sem("turn3_taken"), 1)
            with act.Fori(0, C1) as c:
                chunk3(c)

        @block.vector
        def _(dve):
            link = Link(dve, sem("dve_link"))
            dve.wait_ge(sem("setup"), setup_all)
            dve.tensor_copy(pick[:], row_is[:].unsqueeze(2).broadcast_to([96, 32, P])).then_inc(sem("consts"), 1)
            dve.sem_inc(sem("scanned"), N_DA)
            dve.sem_inc(sem("dbu_ready"), DBU_CREDIT)
            dve.sem_inc(sem("out_taken"), 2)
            dve.wait_ge(sem("zeroed"), 2)
            for part in range(X_PARTS):
                dve.wait_ge(sem(f"x_in{part}"), 16)

            def stats(st, mv, data, q_n, ready):
                for q in range(q_n):
                    link.mark(dve.bn_stats(st[:, q, :], data[:, q, :]))
                link.wait()
                dve.sem_inc(sem("dve_settled"), 1)
                for q in range(q_n):
                    ins = dve.bn_aggr(mv[:, q, :], st[:, q, :])
                ins.then_inc(ready, 1)

            def normalise(dst, data, mv, rs, q_n, ready):
                for q in range(q_n):
                    ins = dve.tensor_scalar(dst(q), data[:, q, :], mv[:, q, 0:1], rs[:, q:q + 1],
                                            ALU.subtract, ALU.mult)
                ins.then_inc(ready, 1)

            conv_at = [0, 0]

            def prepare(n, i):
                half = n[1] % 2
                if i == AT_G_STATS:
                    dve.wait_ge(sem("g_ready"), at(n, 1, 1))
                    link(dve.tensor_tensor(g_act[:], tiles(M1), gcn_b[:].unsqueeze(1).broadcast_to([P, Q0, D]), ALU.add))
                    link(dve.tensor_scalar(g_act[:], g_act[:], 0.0, None, ALU.max))
                    stats(ln0_st, ln0_mv, g_act, Q0, sem("h_stats"))
                if i == AT_G_NORM:
                    dve.wait_ge(sem("h_rstd"), at(n, 1, 1))
                    normalise(lambda q: h_norm[:, q, :], g_act, ln0_mv, ln0_rs, Q0, sem("h_norm_ready"))
                if AT_CONV <= i < AT_CONV + TAPS:
                    tap = i - AT_CONV
                    for k in range(KD):
                        src, w = xc[:, k, tap:tap + T0], conv_w[:, k, tap:tap + 1]
                        if tap == 0:
                            dve.wait_ge(sem("xc_ready"), at(n, KD, k + 1))
                            ins = dve.tensor_scalar(conv[:, k, :], src, w, None, ALU.mult)
                        else:
                            link.wait(conv_at[k])
                            ins = dve.scalar_tensor_tensor(out=conv[:, k, :], in0=src, scalar=w, in1=conv[:, k, :],
                                                           op0=ALU.mult, op1=ALU.add)
                        if tap < TAPS - 1:
                            conv_at[k] = link.mark(ins)
                        else:
                            ins.then_inc(sem("conv_ready"), 1)
                if i == AT_BC_SPLIT:
                    dve.wait_ge(sem("bc_raw"), at(n, 1, 1))
                    raw = ps[0:96, M0, :]
                    link.mark(dve.tensor_copy(bc1[:], raw))
                    link(dve.tensor_copy(bc_parts[0:32, half, :], raw[0:32]))
                    dve.tensor_tensor(bc_rest[:], raw, bc1[:], ALU.subtract).then_inc(sem("bc_taken"), 1)
                if i == AT_BC_SPLIT + 1:
                    dve.wait_ge(sem("bc_taken"), at(n, 1, 1))
                    link.mark(dve.tensor_copy(bc2[:], bc_rest[:]))
                    link(dve.tensor_copy(bc_parts[32:64, half, :], bc_rest[32:64, :]))
                    link(dve.tensor_tensor(bc_rest[64:96, :], bc_rest[64:96, :], bc2[64:96, :], ALU.subtract))
                    dve.tensor_copy(bc_parts[64:96, half, :], bc_rest[64:96, :]).then_inc(sem("bc_split"), 1)
                if i == AT_DT:
                    dve.wait_ge(sem("sp_ready"), at(n, 1, 1))
                    dve.scalar_tensor_tensor(out=dt[:, half], in0=sp_v[:], scalar=0.0, in1=sp_e[:], op0=ALU.max,
                                             op1=ALU.add).then_inc(sem("dt_done"), 1)
                if i == AT_DT + 1:
                    dve.wait_ge(sem("dt_done"), at(n, 1, 1))
                    dve.wait_ge(sem("u_ready"), at(n, KD, KD))
                    link(dve.tensor_tensor(du[:, half], dt[:, half], u[:, half], ALU.mult))

            def finish0(c, i):
                half = c[1] % 2
                if i == AT_GATE:
                    for k in range(KD):
                        dve.wait_ge(sem("y_summed"), at(c, PAIRS, N_PAIR + PAIRS - KD + k + 1))
                        link(dve.scalar_tensor_tensor(out=yg[:, k, :], in0=u[:, half, k, :], scalar=d_skip[:, k:k + 1],
                                                      in1=ps[:, Y + k, :], op0=ALU.mult, op1=ALU.add))
                        dve.tensor_tensor(yg[:, k, :], yg[:, k, :], sz[:, half, k, :], ALU.mult).then_inc(sem("gated"), 1)
                rows = at(c, Q0, 0)
                if i == AT_X1_STATS:
                    dve.wait_ge(sem("out_ready"), at(c, 1, 1))
                    dve.tensor_tensor(xo[:], tiles(M1), xa[:, bass.ds(rows, Q0), :], ALU.add).then_inc(sem("out_taken"), 1)
                    dve.wait_ge(sem("out_taken"), at(c, 1, 3))
                    stats(ln1_st, ln1_mv, xo, Q0, sem("x1_stats"))
                if i == AT_X1:
                    dve.wait_ge(sem("x1_rstd"), at(c, 1, 1))
                    normalise(lambda q: xb[:, bass.ds(rows + q, 1), :].rearrange("p a d -> p (a d)"),
                              xo, ln1_mv, ln1_rs, Q0, sem("x1_ready"))

            def chunk0(c):
                half = c[1] % 2

                def step_dbu(i):
                    n, k = divmod(i, KD)
                    if k == 0:
                        dve.wait_ge(sem("b_bcast"), at(c, S_N, n + 1))
                    if i >= N_DBU:
                        dve.wait_ge(sem("scanned"), at(c, STEPS, N_DA + i - N_DBU + 1))
                    dve.tensor_tensor(dbu[:, i % N_DBU, :], du[:, half, k, :], ps[:, BB + n % 2, :],
                                      ALU.mult).then_inc(sem("dbu_ready"), 1)

                def step_keep(i):
                    dve.wait_ge(sem("scanned"), at(c, STEPS, N_DA + i + 1))
                    return link.mark(dve.tensor_copy(h_last[:, i:i + 1], hs[:, i % N_H, T0 - 1:T0]))

                kept = [0] * STEPS
                step_dbu(0)
                for i in range(STEPS):
                    if i + 1 < STEPS:
                        step_dbu(i + 1)
                    dve.wait_ge(sem("dbu_ready"), at(c, STEPS, DBU_CREDIT + i + 1))
                    dve.wait_ge(sem("da_ready"), at(c, STEPS, i + 1))
                    dve.wait_ge(sem("hc_ready"), at(c, STEPS, HC_CREDIT - N_H + i + 1))
                    if i >= N_H:
                        link.wait(kept[i - N_H])
                    dve.tensor_tensor_scan(hs[:, i % N_H, :], da[:, i % N_DA, :], dbu[:, i % N_DBU, :],
                                           h_last[:, i:i + 1], ALU.mult, ALU.add).then_inc(sem("scanned"), 1)
                    if i >= 1:
                        kept[i - 1] = step_keep(i - 1)
                    if has_next(c):
                        prepare(neighbour(c, 1), i)
                    if has_previous(c):
                        finish0(neighbour(c, -1), i)
                kept[STEPS - 1] = step_keep(STEPS - 1)
                link.wait()

            for i in range(STEPS):
                prepare((0, 0), i)
            link.straight()
            chunk0(FIRST)
            link.straight()
            with dve.Fori(0, LOOPS0) as pair:
                link.body(pair, RATE0)
                for c in in_loop(pair):
                    chunk0(c)
            link.leave(LOOPS0)
            for c in AFTER:
                chunk0(c)
            for i in range(STEPS):
                finish0(AFTER[-1], i)
            link.straight()
            if stop == 1:
                return

            dve.sem_inc(sem("x_taken"), 1)
            dve.wait_ge(sem("x1_ready"), C0)
            dve.wait_ge(sem("wa_raw"), 1)
            dve.tensor_copy(w1_cat[:, D:], ps[:, RAW, 0:2 * HEADS]).then_inc(sem("w1_cat_ready"), 1)
            dve.wait_ge(sem("h_taken"), NT // 2)
            e_dst, e_src = e_all[:, :, 0:HEADS], e_all[:, :, HEADS:]
            dve.tensor_reduce(d_max[:], e_dst.rearrange("p t h -> p h t"), AX_X, ALU.max).then_inc(sem("d_max_ready"), 1)
            dve.wait_ge(sem("d_all_ready"), 1)
            d_wide = d_all[:].unsqueeze(1).broadcast_to([P, NT, HEADS])
            link.mark(dve.tensor_tensor(e_src, e_src, d_wide, ALU.add))
            link(dve.tensor_tensor(e_dst, e_dst, d_wide, ALU.subtract))
            dve.tensor_scalar(e_neg[:], e_dst, LEAKY - 1, E_MAX, ALU.mult, ALU.min).then_inc(sem("e_ready"), 1)
            dve.wait_ge(sem("bc_ready"), 1)
            link.mark(dve.tensor_scalar(r_nat[:, 0:NT, :], r_nat[:, 0:NT, :], float(R_MAX), None, ALU.min))
            link.mark(dve.tensor_tensor(dv, bv[:], cv[:], ALU.mult))
            dve.tensor_scalar(neg_c[:], cv[:], -1.0, None, ALU.mult).then_inc(sem("neg_c_ready"), 1)
            link.wait()
            dve.tensor_copy(r_now, r_nat[:, 0:Q1, :]).then_inc(sem("r_now_ready"), 1)
            own = slice(DVE_HEADS * F, D)
            wide = lambda v, n: v.unsqueeze(3).broadcast_to([P, NT, n, F])
            link(dve.tensor_tensor(dh[:].rearrange("p t (h f) -> p t h f", f=F),
                                   bh[:, :, own].rearrange("p t (h f) -> p t h f", f=F),
                                   wide(dv[:, :, DVE_HEADS:], HEADS - DVE_HEADS), ALU.mult))
            bh4 = bh[:].rearrange("p t (h f) -> p t h f", f=F)
            link(dve.tensor_tensor(bh4, bh4, wide(bv[:], HEADS), ALU.mult))
            dve.wait_ge(sem("stat_zero"), 5)
            masked = stat_m[:, :, MASKED:MASKED + HEADS * PARTS].rearrange("p t (h a) -> p t h a", a=PARTS)
            for part in range(PARTS):
                for rest, into in ((bv[:], stat_s[:, :, :, part]), (dv, masked[:, :, :, part])):
                    link(dve.tensor_copy(into, rest))
                    if part < PARTS - 1:
                        link(dve.tensor_tensor(rest, rest, into, ALU.subtract))
                link.mark(dve.tensor_scalar(stat_s[:, :, :, PARTS + part], masked[:, :, :, part], -1.0, None, ALU.mult))
            link.wait()
            dve.sem_inc(sem("bh_ready"), 1)
            dve.sem_inc(sem("w_ready"), 1)
            link.straight()

            def attend(c):
                rows = bass.ds(c * Q1, Q1)
                dve.wait_ge(sem("den_turned"), c + 1)
                sums = tiles8(NAT).rearrange("p q (h f) -> p q h f", f=F)
                link.mark(dve.tensor_copy(deg[:, rows], sums[:, :, 0, DEG]))
                link.mark(dve.tensor_reduce(den_p[:], sums[:, :, :, 0:PARTS], AX_X, ALU.add))
                link.mark(dve.tensor_reduce(den_q[:], sums[:, :, :, PARTS:2 * PARTS], AX_X, ALU.add))
                for b in range(2):
                    half = slice(b * Q1 // 2, (b + 1) * Q1 // 2)
                    ins = dve.tensor_reduce(den_m[:, half, :], sums[:, half, b, MASKED:MASKED + HEADS * PARTS]
                                            .rearrange("p q (h a) -> p q h a", a=PARTS), AX_X, ALU.add)
                ins.then_inc(sem("den_used"), 1)
                dve.wait_ge(sem("den_used"), c + 1)
                link(dve.tensor_tensor(den_q[:], den_q[:], den_m[:], ALU.add))
                link(dve.tensor_tensor(den_p[:], den_p[:], r_nat[:, rows, :], ALU.mult))
                link(dve.tensor_tensor(den_p[:], den_p[:], den_q[:], ALU.add))
                link(dve.reciprocal(den_p[:], den_p[:]))
                dve.wait_ge(sem("num_turned"), c + 1)
                dve.tensor_tensor(xo1[:].rearrange("p q (h f) -> p (q h) f", f=F),
                                  tiles8(RAW).rearrange("p q (h f) -> p (q h) f", f=F),
                                  den_p[:].rearrange("p q h -> p (q h)").unsqueeze(2).broadcast_to([P, Q1 * HEADS, F]),
                                  ALU.mult).then_inc(sem("x_taken"), 1)
                dve.wait_ge(sem("x_taken"), c + 2)
                link(dve.tensor_tensor(xo1[:], xo1[:], xb[:, rows, :], ALU.add))
                stats(ln_st, ln_mv, xo1, Q1, sem("x2_stats"))

            def finish1(c):
                dve.wait_ge(sem("x2_rstd"), c + 1)
                normalise(lambda q: xa[:, bass.ds(c * Q1 + q, 1), :].rearrange("p a d -> p (a d)"),
                          xo1, ln_mv, ln_rs, Q1, sem("x2_ready"))

            def chunk1(c, first):
                if not first:
                    link.body(c - 1, RATE1)
                dve.wait_ge(sem("r_raw"), c * HEADS + (R_ORDER.index(0) + 1))
                dve.wait_ge(sem("w_ready"), c * NT + 1)
                link(dve.tensor_copy(r_rows[:, 0, :], two(NAT)))
                dve.wait_ge(sem("r_taken"), c * 3 + 3)
                for j in range(NT):
                    adj = ring[:, j % RING, :]
                    sl = j % N_S
                    dve.wait_ge(sem(f"adj_in{j % RING}"), c * (16 * NT // RING) + 16 * (LOADS // RING + j // RING + 1))
                    dve.wait_ge(sem("den_summed"), c * NT + (j + 1))
                    dve.sem_inc(sem("dve_settled"), 1)
                    if not act_masks(j):
                        link.mark(dve.tensor_scalar(m1[:, sl, :], adj, 0.0, None, ALU.is_gt, saturate=False))
                    for h in range(DVE_HEADS):
                        ins = dve.tensor_scalar(s8[:, sl, h, :], r_rows[:, h, :], cv[:, j, h:h + 1], None,
                                                ALU.is_gt, saturate=False)
                        link.mark(ins)
                    dve.wait_ge(sem("num_summed"), c * NT + (NUM_CREDIT - N_W + j + 1))
                    for h in range(DVE_HEADS):
                        ins = dve.scalar_tensor_tensor(out=w_ring[:, j % N_W, h, :], in0=r_rows[:, h, :],
                                                       scalar=cv[:, j, h:h + 1], in1=adj, op0=ALU.max, op1=ALU.mult)
                    ins.then_inc(sem("w_ready"), 1)
                    link.wait()
                    if act_masks(j):
                        dve.wait_ge(sem("mask_ready"), c * (NT // 2) + (j // 2 + 1))
                    s8w = s8[:, sl, 0:DVE_HEADS, :].bitcast(U32)
                    dve.tensor_tensor(s8w, s8w, m1[:, sl, :].bitcast(U32).unsqueeze(1)
                                      .broadcast_to([P, DVE_HEADS, T1 // 4]), ALU.bitwise_and).then_inc(sem("masked"), 1)
                    if j == ATTEND_AT and not first:
                        attend(c - 1)
                    if j == FINISH_AT and not first:
                        finish1(c - 1)
                    if j == PREFILL_AT - 2:
                        dve.wait_ge(sem("r_raw"), c * HEADS + HEADS)
                        dve.tensor_copy(r_now, r_nat[:, bass.ds(c * Q1 + Q1, Q1), :]).then_inc(sem("r_now_ready"), 1)

            chunk1(0, True)
            link.straight()
            with dve.Fori(1, C1) as c:
                chunk1(c, False)
            link.leave(C1 - 1)
            attend(C1 - 1)
            finish1(C1 - 1)
            link.straight()
            if stop == 2:
                return

            dve.sem_inc(sem("turn_taken"), 1)
            dve.wait_ge(sem("x2_ready"), C1)
            dve.wait_ge(sem("dis_ready"), 1)
            for g in range(NT // 4):
                dve.wait_ge(sem("sup_raw"), g + 1)
                dve.tensor_tensor(sup[:, 4 * g:4 * g + 4, :], tiles(TURN + g % 2),
                                  dis[:, 4 * g:4 * g + 4].unsqueeze(2).broadcast_to([P, 4, D]),
                                  ALU.mult).then_inc(sem("sup_ready"), 1)
            dve.wait_ge(sem("sup_ready"), NT // 4)
            dve.sem_inc(sem("mx_summed"), 2)
            link.straight()

            def chunk2(c):
                link.body(c, RATE2)
                rows = bass.ds(c * Q1, Q1)
                dve.wait_ge(sem("s2_turned"), c + 1)
                dve.tensor_tensor(xo2[:], tiles8(TURN), sup[:, rows, :], ALU.add).then_inc(sem("turn_taken"), 1)
                dve.wait_ge(sem("turn_taken"), c + 2)
                link(dve.tensor_tensor(xo2[:], xo2[:], dis[:, rows].unsqueeze(2).broadcast_to([P, Q1, D]), ALU.mult))
                link(dve.scalar_tensor_tensor(out=xo2[:].rearrange("p q d -> p (q d)"), in0=xo2[:].rearrange("p q d -> p (q d)"), scalar=0.0,
                                              in1=xa[:, rows, :].rearrange("p q d -> p (q d)"), op0=ALU.max, op1=ALU.add))
                stats(ln_st, ln_mv, xo2, Q1, sem("x3_stats"))
                dve.wait_ge(sem("x3_rstd"), c + 1)
                normalise(lambda q: xb[:, bass.ds(c * Q1 + q, 1), :].rearrange("p a d -> p (a d)"),
                          xo2, ln_mv, ln_rs, Q1, sem("x3_ready"))
                dve.wait_ge(sem("x3_ready"), c + 1)
                link(dve.tensor_tensor(rl[:], xb[:, rows, :], xb[:, rows, :], ALU.mult))
                link(dve.tensor_reduce(sums[:, rows], rl[:], AX_X, ALU.add))

            with dve.Fori(0, C1) as c:
                chunk2(c)
            link.leave(C1)
            if stop == 3:
                return

            dve.sem_inc(sem("rl_used"), 1)
            per_row = lambda v: v.unsqueeze(2).broadcast_to([P, 4, D])
            link.mark(dve.memset(arg[:], 0.0))
            for g in range(NT // 4):
                dve.wait_ge(sem("mx_ready"), g + 1)
                dve.tensor_reduce(sums[:, NT + 4 * g:NT + 4 * g + 4], sq[:, g % 2, 0:4, :], AX_X,
                                  ALU.add).then_inc(sem("mx_summed"), 1)
            dve.wait_ge(sem("dots_raw"), NT // 4)
            link.mark(dve.tensor_copy(dots[:], ps[:, ACC, 0:NT]))
            dve.wait_ge(sem("mx_summed"), NT // 4 + 2)
            dve.wait_ge(sem("sums_ready"), 1)
            dve.tensor_scalar(sums[:], sums[:], MIN_SQ, None, ALU.max).then_inc(sem("sums_floor"), 1)
            dve.wait_ge(sem("norms_ready"), 1)
            xn, mxn, bn = norms[:, 0:NT], norms[:, NT:2 * NT], norms[:, 2 * NT:]
            link.mark(dve.reciprocal(recips[:], norms[:]))
            dve.tensor_scalar(clipped[:], xn, ATANH_MAX, None, ALU.min).then_inc(sem("clipped_ready"), 1)
            link.wait()
            link.mark(dve.tensor_copy(arg[:, NT:], bn))
            link(dve.tensor_tensor(tmp[:, 0:NT], mxn, recips[:, 0:NT], ALU.mult))
            dve.wait_ge(sem("atanh_ln"), 1)
            link(dve.tensor_tensor(arg[:, 0:NT], ln_plus[:, 0:NT], ln_minus[:, 0:NT], ALU.subtract))
            dve.scalar_tensor_tensor(out=arg[:, 0:NT], in0=arg[:, 0:NT], scalar=0.5, in1=tmp[:, 0:NT],
                                     op0=ALU.mult, op1=ALU.mult).then_inc(sem("tanh_in"), 1)
            dve.wait_ge(sem("tanh_exp"), 1)
            link.mark(dve.tensor_scalar(tanh[:], tanh_e[:], -1.0, 1.0, ALU.mult, ALU.add))
            link(dve.tensor_scalar(tmp[:], tanh_e[:], 1.0, None, ALU.add))
            link(dve.reciprocal(tmp[:], tmp[:]))
            link.mark(dve.tensor_tensor(tanh[:], tanh[:], tmp[:], ALU.mult))
            link.mark(dve.tensor_tensor(gap[:], tanh_e[:], tmp[:], ALU.mult))
            link.wait()
            link.mark(dve.tensor_scalar(tanh[:], tanh[:], MAX_NORM, None, ALU.min))
            link(dve.scalar_tensor_tensor(out=gap[:], in0=gap[:], scalar=4.0, in1=tmp[:], op0=ALU.mult, op1=ALU.mult))
            link.mark(dve.tensor_scalar(gap[:], gap[:], LEAST_GAP, None, ALU.max))
            link.mark(dve.tensor_tensor(sq_norm[:], tanh[:], tanh[:], ALU.mult))
            link(dve.tensor_tensor(tmp[:], tanh[:], recips[:, NT:], ALU.mult))
            alpha, cb = tmp[:, 0:NT], tmp[:, NT:]
            x_sq, y_sq = sq_norm[:, 0:NT], sq_norm[:, NT:]
            link.mark(dve.tensor_scalar(hyp_bias[:], bias3[:], cb, None, ALU.mult))
            link(dve.tensor_scalar(dots[:], dots[:], cb, 2.0, ALU.mult, ALU.mult))
            link(dve.tensor_tensor(dots[:], dots[:], alpha, ALU.mult))
            link(dve.tensor_scalar(dots[:], dots[:], 1.0, None, ALU.add))
            link(dve.scalar_tensor_tensor(out=r_den[:], in0=x_sq, scalar=y_sq, in1=dots[:], op0=ALU.mult, op1=ALU.add))
            link(dve.tensor_scalar(r_den[:], r_den[:], 1e-15, None, ALU.max))
            link(dve.reciprocal(r_den[:], r_den[:]))
            link.mark(dve.scalar_tensor_tensor(out=cx[:], in0=dots[:], scalar=y_sq, in1=r_den[:], op0=ALU.add, op1=ALU.mult))
            link(dve.tensor_tensor(cy[:], gap[:, 0:NT], r_den[:], ALU.mult))
            link(dve.tensor_scalar(gap2[:], cy[:], gap[:, NT:], None, ALU.mult))
            link(dve.tensor_scalar(norm2[:], gap2[:], -1.0, 1.0, ALU.mult, ALU.add))
            link.mark(dve.tensor_scalar(gap2[:], gap2[:], LEAST_GAP, None, ALU.max))
            link.mark(dve.tensor_tensor(cx[:], cx[:], alpha, ALU.mult))
            link.wait()
            dve.tensor_scalar(norm2[:], norm2[:], FLAT_SQ, None, ALU.max).then_inc(sem("norm2_sq"), 1)
            dve.wait_ge(sem("norm2_ready"), 1)
            dve.tensor_scalar(clip2[:], norm2[:], MAX_NORM, None, ALU.min).then_inc(sem("clip2_ready"), 1)
            dve.wait_ge(sem("atanh2_ln"), 1)
            link(dve.scalar_tensor_tensor(out=ln_plus2[:], in0=ln_gap2[:], scalar=-0.5, in1=ln_plus2[:],
                                          op0=ALU.mult, op1=ALU.add))
            link(dve.tensor_tensor(ln_plus2[:], ln_plus2[:], by_norm2[:], ALU.mult))
            link.mark(dve.tensor_tensor(cx[:], cx[:], ln_plus2[:], ALU.mult))
            link(dve.tensor_tensor(cy[:], cy[:], ln_plus2[:], ALU.mult))
            for g in range(NT // 4):
                tile4 = slice(4 * g, 4 * g + 4)
                link.mark(dve.tensor_tensor(sup[:, tile4, :], big[:, tile4, :], per_row(cx[:, tile4]), ALU.mult))
                link(dve.tensor_tensor(bias_part[:], hyp_bias[:].unsqueeze(1).broadcast_to([P, 4, D]),
                                       per_row(cy[:, tile4]), ALU.mult))
                dve.tensor_tensor(sup[:, tile4, :], sup[:, tile4, :], bias_part[:], ALU.add).then_inc(sem("xt_ready"), 1)
                dve.wait_ge(sem("xt_ready"), g + 1)
            link.straight()

            def chunk3(c):
                link.body(c, RATE3)
                rows = bass.ds(c * Q1, Q1)
                dve.wait_ge(sem("sq_ready"), c + 1)
                link(dve.tensor_reduce(f_sq[:], sq[:], AX_X, ALU.add))
                dve.tensor_scalar(f_sq[:], f_sq[:], MIN_SQ, None, ALU.max).then_inc(sem("f_sq_ready"), 1)
                dve.wait_ge(sem("f_norm_ready"), c + 1)
                link.mark(dve.tensor_scalar(f_k[:], f_norm[:, 0, :], ATANH_OF_MAX, None, ALU.min))
                link(dve.reciprocal(f_recip[:], f_norm[:]))
                link(dve.tensor_tensor(f_k[:], f_k[:], f_recip[:, 0, :], ALU.mult))
                dve.tensor_tensor(f_arg[:], f_k[:], f_norm[:, 1, :], ALU.mult).then_inc(sem("f_arg_ready"), 1)
                dve.wait_ge(sem("f_exp"), c + 1)
                link.mark(dve.tensor_scalar(f_k[:], f_tanh[:], 1.0, None, ALU.add))
                link(dve.tensor_scalar(f_tanh[:], f_tanh[:], -1.0, 1.0, ALU.mult, ALU.add))
                link(dve.reciprocal(f_k[:], f_k[:]))
                link(dve.tensor_tensor(f_tanh[:], f_tanh[:], f_k[:], ALU.mult))
                link(dve.scalar_tensor_tensor(out=f_tanh[:], in0=f_tanh[:], scalar=MAX_NORM, in1=f_recip[:, 1, :],
                                              op0=ALU.min, op1=ALU.mult))
                link(dve.tensor_tensor(xo3[:], rl[:], f_tanh[:].unsqueeze(2).broadcast_to([P, Q1, D]), ALU.mult))
                dve.tensor_tensor(xo3[:], xo3[:], xb[:, rows, :], ALU.add).then_inc(sem("rl_used"), 1)
                dve.wait_ge(sem("rl_used"), c + 2)
                stats(ln_st, ln_mv, xo3, Q1, sem("x4_stats"))
                dve.wait_ge(sem("x4_rstd"), c + 1)
                normalise(lambda q: xa[:, bass.ds(c * Q1 + q, 1), :].rearrange("p a d -> p (a d)"),
                          xo3, ln_mv, ln_rs, Q1, sem("x4_ready"))
                dve.wait_ge(sem("x4_ready"), c + 1)

            with dve.Fori(0, C1) as c:
                chunk3(c)
            link.leave(C1)

        @block.tensor
        def _(pe):
            pe.sem_inc(sem("y_summed"), N_PAIR)

            def aggregate(c, j):
                r = j // 2
                if j % 2 == 0:
                    pe.wait_ge(sem(f"adj_in{r % RING}"), at(c, 16 * NT // 2 // RING, 16 * (r // RING + 1)))
                ins = pe.matmul(ps[:, AX, :], xa[:, j, :], ring[:, r % RING, j % 2 * T0:(j % 2 + 1) * T0],
                                start=j == 0, stop=j == NT - 1)
                if j % 2 == 1:
                    ins.then_inc(sem("adj_free"), 1)

            def prepare(n, i):
                half = n[1] % 2
                if i == AT_GCN:
                    pe.wait_ge(sem("ax_taken"), at(n, 1, 1))
                    for q in range(Q0):
                        ins = pe.matmul(tiles(M1)[:, q, :], ax_t[:, q * P:(q + 1) * P], gcn_w[:], start=True, stop=True)
                    ins.then_inc(sem("g_ready"), 1)
                if i == AT_TURN:
                    pe.wait_ge(sem("h_norm_ready"), at(n, 1, 1))
                    for q in range(Q0):
                        ins = pe.transpose(tiles(M0)[:, q, :], h_norm[:, q, :], ident[:])
                    ins.then_inc(sem("h_turned"), 1)
                if i in (AT_XC, AT_Z):
                    for k in range(KD):
                        m = k if i == AT_XC else KD + k
                        if i == AT_XC:
                            pe.wait_ge(sem("h_t_ready"), at(n, 1, 1))
                            pe.wait_ge(sem("out_taken"), at(n, 1, 1))
                        else:
                            pe.wait_ge(sem("xc_ready"), at(n, KD, k + 1))
                        pe.matmul(ps[:, M0 + k, :], w_in[:, m * P:(m + 1) * P], ax_t[:], start=True,
                                  stop=True).then_inc(sem("xz_ready"), 1)
                if i == AT_BC:
                    pe.wait_ge(sem("z_ready"), at(n, KD, KD))
                    pe.wait_ge(sem("u_ready"), at(n, KD, KD))
                    for k in range(KD):
                        ins = pe.matmul(ps[0:RANK, M1, :], w_r[:, k, :], u[:, half, k, :], start=k == 0, stop=k == KD - 1)
                    ins.then_inc(sem("rank_ready"), 1)
                    for k in range(KD):
                        ins = pe.matmul(ps[0:96, M0, :], w_bc[:, k, :], u[:, half, k, :], start=k == 0, stop=k == KD - 1)
                    ins.then_inc(sem("bc_raw"), 1)
                if i == AT_DT_RAW:
                    pe.wait_ge(sem("rank_taken"), at(n, 1, 1))
                    pe.wait_ge(sem("bc_taken"), at(n, 1, 1))
                    for k in range(KD):
                        pe.matmul(ps[:, M0 + k, :], w_dt[:, k * P:(k + 1) * P], rank_t[:], start=True,
                                  stop=True).then_inc(sem("dt_raw"), 1)

            def finish0(c):
                pe.wait_ge(sem("gated"), at(c, KD, KD))
                for q in range(Q0):
                    for k in range(KD):
                        ins = pe.matmul(tiles(M1)[:, q, :], yg[:, k, q * P:(q + 1) * P], w_out[:, k, :],
                                        start=k == 0, stop=k == KD - 1)
                ins.then_inc(sem("out_ready"), 1)

            def b_row(c, n):
                pe.wait_ge(sem("dbu_ready"), at(c, STEPS, KD * n + KD))
                pe.matmul(ps[:, BB + n % 2, :], pick[:, n % S_N, :], bc_parts[:, (c[1] + n // S_N) % 2, :], start=True,
                          stop=True).then_inc(sem("b_bcast"), 1)

            def c_row(c, n):
                pe.wait_ge(sem("c_rows"), at(c, S_N, n + 1))
                pe.matmul(ps[:, CB, :], pick[:, S_N + n % S_N, :], bc_parts[:, (c[1] + n // S_N) % 2, :], start=True,
                          stop=True).then_inc(sem("c_bcast"), 1)

            def sum_y(c, i):
                n, k = divmod(i, KD)
                m = n // 2 * KD + k
                if n % 2 == 1:
                    pe.wait_ge(sem("pair_ready"), at(c, PAIRS, PAIR_CREDIT + m + 1))
                    ins = pe.matmul(ps[:, Y + k, :], ident[:], hc[:, m % N_PAIR, :], start=n == 1, stop=n == S_N - 1)
                    ins.then_inc(sem("y_summed"), 1)

            def chunk0(c):
                for i in range(STEPS):
                    n, k = divmod(i, KD)
                    if n + 1 < S_N or has_next(c):
                        if k == 0:
                            b_row(c, n + 1)
                        else:
                            c_row(c, n + 1)
                    if has_next(c) and has_next(neighbour(c, 1)):
                        if i == 0:
                            pe.wait_ge(sem("ax_taken"), at(c, 1, 2))
                        aggregate(neighbour(c, 2), i)
                    if has_next(c):
                        prepare(neighbour(c, 1), i)
                    if i == STEPS - 3 and has_next(c):
                        pe.wait_ge(sem("bc_split"), at(c, 1, 2))
                    if i == AT_OUT and has_previous(c):
                        finish0(neighbour(c, -1))
                    if i >= Y_LAG:
                        sum_y(c, i - Y_LAG)
                    elif has_previous(c):
                        sum_y(neighbour(c, -1), STEPS - Y_LAG + i)

            for j in range(NT):
                if j % (NT // X_PARTS) == 0:
                    pe.wait_ge(sem(f"x_in{j * X_PARTS // NT}"), 16)
                aggregate((0, 0), j)
            pe.wait_ge(sem("setup"), setup_all)
            pe.wait_ge(sem("consts"), 1)
            pe.wait_ge(sem("ax_taken"), 1)
            for i in range(STEPS):
                prepare((0, 0), i)
                aggregate((0, 1), i)
            pe.wait_ge(sem("bc_split"), 1)
            b_row((0, 0), 0)
            c_row((0, 0), 0)
            chunk0(FIRST)
            with pe.Fori(0, LOOPS0) as pair:
                for c in in_loop(pair):
                    chunk0(c)
            for c in AFTER:
                chunk0(c)
            for i in range(STEPS - Y_LAG, STEPS):
                sum_y(AFTER[-1], i)
            finish0(AFTER[-1])
            if stop == 1:
                return

            pe.wait_ge(sem("x1_ready"), C0)
            for g in range(NT // 4):
                if g >= 2:
                    pe.wait_ge(sem("x1_t_ready"), g - 1)
                for q in range(4):
                    ins = pe.transpose(ps[:, NAT + g % 2, q * P:(q + 1) * P], xb[:, 4 * g + q, :], ident[:])
                ins.then_inc(sem("x1_turned"), 1)
            pe.matmul(ps[:, RAW, 0:2 * HEADS], w1_t[:], a_bd[:], start=True, stop=True).then_inc(sem("wa_raw"), 1)
            pe.wait_ge(sem("w1_cat_ready"), 1)
            pe.wait_ge(sem("x1_t_ready"), NT // 4)
            cols = D + 2 * HEADS
            for g in range(NT // 2):
                if g >= 2:
                    pe.wait_ge(sem("h_taken"), g - 1)
                for q in range(2):
                    j = 2 * g + q
                    ins = pe.matmul(ps[:, NAT + g % 2, q * cols:(q + 1) * cols], x_t[:, j * P:(j + 1) * P],
                                    w1_cat[:], start=True, stop=True)
                ins.then_inc(sem("h_raw"), 1)
            pe.wait_ge(sem("h_taken"), NT // 2)
            pe.sem_inc(sem("den_summed"), N_S)
            pe.sem_inc(sem("num_summed"), NUM_CREDIT)

            def fill(h):
                for q in range(Q1):
                    ins = pe.matmul(tiles8(RAW if h % 2 else NAT)[:, q, :], r_now[:, q, h:h + 1].broadcast_to([P, P]),
                                    ident[:], start=True, stop=True)
                ins.then_inc(sem("r_raw"), 1)

            def turn1(c):
                for q in range(Q1):
                    ins = pe.transpose(tiles8(NAT)[:, q, :], den_raw[:, q * P:(q + 1) * P], ident[:])
                ins.then_inc(sem("den_turned"), 1)
                for q in range(Q1):
                    ins = pe.transpose(tiles8(RAW)[:, q, :], num_raw[:, q * P:(q + 1) * P], ident[:])
                ins.then_inc(sem("num_turned"), 1)

            def chunk1(c, first):
                if not first:
                    pe.wait_ge(sem("sums_taken"), c * 2)
                for j in range(NT):
                    start, end = j == 0, j == NT - 1
                    pe.wait_ge(sem(f"adj_in{j % RING}"), c * (16 * NT // RING) + 16 * (LOADS // RING + j // RING + 1))
                    for b in range(2):
                        adj = ring[:, j % RING, b * BANK:(b + 1) * BANK]
                        for h in range(DVE_HEADS, HEADS):
                            pe.matmul(ps[F * h:F * (h + 1), NUM + b, :], dh[:, j, F * (h - DVE_HEADS):F * (h - DVE_HEADS + 1)],
                                      adj, start=start, stop=False)
                        pe.matmul(ps[0:F, DEN + b, :], deg_col[:], adj, start=start, stop=False)
                    if end:
                        pe.wait_ge(sem("r_taken"), c * 3 + 4)
                        fill(0)
                        pe.wait_ge(sem("r_taken"), c * 3 + 5)
                        fill(1)
                    pe.wait_ge(sem("w_ready"), c * NT + (j + 2))
                    pe.wait_ge(sem("v_ready"), c * NT + (j + 1))
                    for b in range(2):
                        cols = slice(b * BANK, (b + 1) * BANK)
                        for h in range(HEADS):
                            moving = w_ring[:, j % N_W, h, cols] if h < DVE_HEADS else v_ring[:, j % N_V, h - DVE_HEADS, cols]
                            ins = pe.matmul(ps[F * h:F * (h + 1), NUM + b, :], bh[:, j, F * h:F * (h + 1)],
                                            moving, start=start and h < DVE_HEADS, stop=end)
                    ins.then_inc(sem("num_summed"), 1)
                    pe.wait_ge(sem("masked"), c * NT + (j + 1))
                    pe.wait_ge(sem("sign_ready"), c * NT + (j + 2))
                    pe.sem_inc(sem("pe_settled"), 1)
                    for b in range(2):
                        cols = slice(b * BANK, (b + 1) * BANK)
                        order = (0, 1, 2, 3) if b == 0 else (1, 2, 3, 0)
                        for h in order:
                            pe.matmul(ps[F * h:F * (h + 1), DEN + b, :], stat_s[:, j, h, :], s8[:, j % N_S, h, cols],
                                      start=start and h > 0, stop=end and h != b)
                        ins = pe.matmul(ps[F * b:F * (b + 1), DEN + b, :], stat_m[:, j, :], m1[:, j % N_S, cols],
                                        start=False, stop=end)
                    ins.then_inc(sem("den_summed"), 1)
                    if j == TURN_AT and not first:
                        turn1(c - 1)
                    if j == PREFILL_AT:
                        pe.wait_ge(sem("r_now_ready"), c + 2)
                        if not first:
                            pe.wait_ge(sem("den_used"), c)
                            pe.wait_ge(sem("x_taken"), c + 1)
                        fill(2)
                        fill(3)

            pe.wait_ge(sem("r_now_ready"), 1)
            fill(2)
            fill(3)
            pe.wait_ge(sem("r_taken"), 1)
            fill(0)
            pe.wait_ge(sem("r_taken"), 2)
            fill(1)
            pe.wait_ge(sem("bh_ready"), 1)
            chunk1(0, True)
            with pe.Fori(1, C1) as c:
                chunk1(c, False)
            pe.wait_ge(sem("sums_taken"), 2 * C1)
            pe.wait_ge(sem("r_taken"), 3 * C1 + 3)
            turn1(C1 - 1)
            if stop == 2:
                return

            def prepare(layer, x, ready, w, raw, taken):
                def turn(g):
                    pe.wait_ge(sem(ready), g * 4 // Q1 + 1)
                    if g >= 2:
                        pe.wait_ge(sem(f"x_t_ready_{layer}"), g - 1)
                    for q in range(4):
                        ins = pe.transpose(ps[:, PREP + g % 2, q * P:(q + 1) * P], x[:, 4 * g + q, :], ident[:])
                    ins.then_inc(sem(f"x_turned_{layer}"), 1)

                def product(g):
                    pe.wait_ge(sem(f"x_t_ready_{layer}"), g + 1)
                    if g >= 2:
                        pe.wait_ge(sem(taken), g - 1)
                    for q in range(4):
                        ins = pe.matmul(tiles(TURN + g % 2)[:, q, :], x2_t[:, (4 * g + q) * P:(4 * g + q + 1) * P],
                                        w[:], start=True, stop=True)
                    ins.then_inc(sem(raw), 1)

                turn(0)
                for g in range(NT // 4):
                    if g + 1 < NT // 4:
                        turn(g + 1)
                    product(g)
                    if layer == 3:
                        for j in range(4 * g, 4 * g + 4):
                            ins = pe.matmul(ps[:, ACC, j:j + 1], x2_t[:, j * P:(j + 1) * P], w3b[:], start=True, stop=True)
                        ins.then_inc(sem("dots_raw"), 1)

            def aggregate_all(layer, c, ready, turned, free, value):
                for j in range(NT):
                    pe.wait_ge(sem(f"adj_in{j % RING}"),
                               c * (16 * NT // RING) + 16 * (layer * LOADS // RING + j // RING + 1))
                    if j % 4 == 0:
                        pe.wait_ge(sem(ready), j // 4 + 1)
                    for b in range(2):
                        ins = pe.matmul(ps[:, ACC + b, :], sup[:, j, :], ring[:, j % RING, b * BANK:(b + 1) * BANK],
                                        start=j == 0, stop=j == NT - 1)
                    ins.then_inc(sem("adj_free"), 1)
                pe.wait_ge(sem(free), value)
                pe.wait_ge(sem(f"acc_taken_{layer}"), c + 1)
                for q in range(Q1):
                    ins = pe.transpose(tiles8(TURN)[:, q, :], acc[:, q * P:(q + 1) * P], ident[:])
                ins.then_inc(sem(turned), 1)

            pe.wait_ge(sem("den_used"), C1)
            pe.wait_ge(sem("x_taken"), C1 + 1)
            prepare(2, xa, "x2_ready", w2_t, "sup_raw", "sup_ready")

            def chunk2(c):
                aggregate_all(2, c, "sup_ready", "s2_turned", "turn_taken", c + 1)

            with pe.Fori(0, C1) as c:
                chunk2(c)
            if stop == 3:
                return

            pe.wait_ge(sem("turn_taken"), C1 + 1)
            pe.matmul(ps[:, ACC + 1, 0:1], w3[:], bias3_col[:], start=True, stop=True).then_inc(sem("w3b_raw"), 1)
            pe.wait_ge(sem("w3b_ready"), 1)
            prepare(3, xb, "x3_ready", w3_t, "mx_raw", "mx_ready")

            def chunk3(c):
                aggregate_all(3, c, "xt_ready", "s_turned", "turn3_taken", c + 1)

            with pe.Fori(0, C1) as c:
                chunk3(c)


_VECTORS = {"gcn_b": "L0_gnn_gcn_b", "ln_g": "L0_gnn_ln_g", "ln_b": "L0_gnn_ln_b", "gcn_w": "L0_gnn_gcn_w",
            "w_in": "L0_gnn_w_in", "conv_w": "L0_gnn_conv_w", "conv_b": "L0_gnn_conv_b", "w_dt": "L0_gnn_w_dt",
            "b_dt": "L0_gnn_b_dt", "a_log": "L0_gnn_A_log", "d_skip": "L0_gnn_D_skip", "w_out": "L0_gnn_w_out"}


def kernel(**inputs):
    import numpy as np
    import concourse.bacc as bacc
    from concourse.bass_utils import run_bass_kernel_spmd

    arrays = {k: inputs[name] for k, name in _VECTORS.items()}
    for k in ("conv_b", "b_dt", "d_skip"):
        arrays[k] = arrays[k].reshape(KD, P).T
    arrays["x"] = inputs["x"]
    arrays["adj_t"] = inputs["adj"].T
    w_xp = inputs["L0_gnn_w_xp"]
    arrays["w_r"] = w_xp[:, 0:RANK]
    arrays["w_bc"] = np.concatenate([w_xp[:, RANK:]] * PARTS, axis=1)
    arrays["w1"] = inputs["L1_gnn_W"]
    arrays["w1_t"] = inputs["L1_gnn_W"].T
    arrays["w2_t"] = inputs["L2_gnn_W"].T
    arrays["w3"] = inputs["L3_gnn_weight"]
    arrays["w3_t"] = inputs["L3_gnn_weight"].T
    arrays["bias3"] = inputs["L3_gnn_bias"]
    a_bd = np.zeros((D, 2 * HEADS), np.float32)
    for h in range(HEADS):
        rows = slice(F * h, F * (h + 1))
        a_bd[rows, h] = inputs["L1_gnn_a_dst"][h]
        a_bd[rows, HEADS + h] = inputs["L1_gnn_a_src"][h]
    arrays["a_bd"] = a_bd
    arrays["ident"] = np.eye(P, dtype=np.float32)
    arrays["row_is"] = np.tile(np.eye(32, dtype=np.float32), (PARTS, 1))
    arrays = {k: np.ascontiguousarray(a) for k, a in arrays.items()}
    nc = bacc.Bacc("TRN2", target_bir_lowering=False, num_devices=1)
    t = {k: nc.dram_tensor(f"in_{k}", a.shape, mybir.dt.from_np(a.dtype), kind="ExternalInput").ap()
         for k, a in arrays.items()}
    out = nc.dram_tensor("out_x", (N, D), F32, kind="ExternalOutput").ap()
    build_program(nc, t, out)
    r = run_bass_kernel_spmd(nc, [{f"in_{k}": a for k, a in arrays.items()}], core_ids=[0])
    return r.results[0]["out_x"]
```

```python
from contextlib import ExitStack

import numpy as np

import concourse.bass as bass
from concourse import mybir

F32 = mybir.dt.float32
FP22 = mybir.dt.float32r
BF16 = mybir.dt.bfloat16
FP8 = mybir.dt.float8e4
U32 = mybir.dt.uint32
ALU = mybir.AluOpType
ACT = mybir.ActivationFunctionType
AX_X = mybir.AxisListType.X

P = 128
N = 4096
D = 128
NT = N // P
BANK = 512
EPS = 1e-5

RING = 8
X_PARTS = 4

DI = 256
KD = DI // P
S_N = 16
RANK = 8
TAPS = 4
T0 = 512
C0 = N // T0
Q0 = T0 // P
STEPS = KD * S_N
PAIRS = STEPS // 2
N_DA, N_DBU, N_H, N_CS, N_PAIR = 4, 4, 4, 4, 8
Y_LAG = 7
HC_CREDIT = KD * N_CS
DBU_CREDIT = 2 * KD
PAIR_CREDIT = KD + 1
AT_GCN, AT_G_STATS, AT_G_RSTD, AT_G_NORM = 1, 2, 2, 6
AT_TURN, AT_H_T, AT_XC, AT_XC_OUT, AT_Z, AT_CONV, AT_SILU = 8, 9, 11, 12, 13, 14, 18
AT_BC, AT_BC_SPLIT, AT_DT_RAW, AT_SOFTPLUS, AT_DT = 20, 22, 25, 26, 30
AT_GATE, AT_OUT, AT_X1_STATS, AT_X1_RSTD, AT_X1 = 7, 8, 10, 10, 14

HEADS = 4
F = D // HEADS
T1 = 1024
C1 = N // T1
Q1 = T1 // P
LOADS = NT * N // T1
LEAKY = 0.2
E_MAX = 60.0
R_MAX = np.float32(np.exp(E_MAX))
DVE_HEADS = 2
PARTS = 3
N_W, N_V, N_S = 2, 4, 4
R_ORDER = (2, 3, 0, 1)
RELU_CREDIT = 1
NUM_CREDIT = RING
DEG = 2 * PARTS
MASKED = 8
SUMS_AT, TURN_AT, ATTEND_AT, RSTD_AT, FINISH_AT = 0, 4, 6, 7, 9
PREFILL_AT = NT - 6
N_SPLIT = 4
SUMS2_AT, TURN2_AT = 1, 2
AT2_ADD, AT2_STATS, AT2_RSTD, AT2_NORM, AT2_SQUARES = 5, 7, 8, 11, 14
AT3_SQUARES, AT3_SUMS, AT3_ROOT, AT3_ARG, AT3_EXP = 4, 7, 8, 12, 13
AT3_ADD, AT3_STATS, AT3_RSTD, AT3_NORM = 15, 17, 18, 21
MIN_SQ = 1e-30
MAX_NORM = float(np.float32(1.0 - 1e-5))
ATANH_MAX = 1.0 - 1e-7
LEAST_GAP = 1.0 - MAX_NORM ** 2
ATANH_OF_MAX = float(np.arctanh(MAX_NORM))
FLAT_SQ = 1e-7

RATE0, RATE1, RATE2, RATE3 = 108, 97, 12, 18
ACT_RATE0, POOL_RATE0 = 10, 4

FIRST = (0, 0)
LOOPS0 = (C0 - 3) // 2
AFTER = [(LOOPS0, offset) for offset in range(1, C0 - 2 * LOOPS0)]


def in_loop(pair):
    return [(pair, 1), (pair, 2)]


def at(chunk, rate, k):
    pair, offset = chunk
    return pair * (2 * rate) + (offset * rate + k)


def neighbour(chunk, distance):
    return chunk[0], chunk[1] + distance


def has_next(chunk):
    return not isinstance(chunk[0], int) or chunk != AFTER[-1]


def has_previous(chunk):
    return chunk[1] > 0


def act_masks(j):
    return j % 2 == 0


def pool_splits(j):
    return j % 4 == 3


def low_count(layer, c, tile, distance=0):
    tile += distance
    on_pool = pool_splits(tile)
    rate = NT // 4 if on_pool else NT - NT // 4
    credit = RING // 4 if on_pool else RING - RING // 4
    index = tile // 4 + 1 if on_pool else tile // 4 * 3 + tile % 4 + 1
    return "pool_low_ready" if on_pool else "low_ready", c * rate + ((layer - 2) * C1 * rate + index + credit)


class Link:

    def __init__(self, eng, sem):
        self.eng, self.sem, self.start, self.k, self.origin = eng, sem, 0, 0, 0

    def body(self, c, rate):
        self.origin, self.k, self.rate = self.start + rate * c, 0, rate

    def leave(self, rounds):
        assert self.k == self.rate, f"the rate of {self.sem} is {self.k}"
        self.start += self.rate * rounds
        self.origin, self.k = self.start, 0

    def mark(self, ins):
        ins.then_inc(self.sem, 1)
        self.k += 1
        return self.k

    def wait(self, k=None):
        self.eng.wait_ge(self.sem, self.origin + (self.k if k is None else k))

    def __call__(self, ins):
        self.mark(ins)
        self.wait()

    def straight(self):
        self.start += self.k
        self.origin, self.k = self.start, 0


def build_program(nc, t, out):
    adj_t = t["adj_t"]
    ctx = ExitStack()
    with ctx:
        sems = {}

        def sem(name):
            if name not in sems:
                sems[name] = ctx.enter_context(nc.semaphore(name))
            return sems[name]

        def sb(stack, name, shape, dt=F32):
            return stack.enter_context(nc.sbuf_tensor(name, shape, dt))

        ring = sb(ctx, "ring", [P, RING, T1])
        xa = sb(ctx, "xa", [P, NT, D])
        xb = sb(ctx, "xb", [P, NT, D])
        ident = sb(ctx, "ident", [P, P])
        half_neg = sb(ctx, "half_neg", [P, NT])
        half_pos = sb(ctx, "half_pos", [P, 2 * Q1])
        eps = sb(ctx, "eps", [P, Q1])
        w1_cat = sb(ctx, "w1_cat", [P, D + 2 * HEADS])
        w1_t = sb(ctx, "w1_t", [P, D])
        a_bd = sb(ctx, "a_bd", [P, 2 * HEADS])
        w2_t = sb(ctx, "w2_t", [P, D])
        w3_t = sb(ctx, "w3_t", [P, D])
        w3 = sb(ctx, "w3", [P, D])
        bias3 = sb(ctx, "bias3", [P, D])
        bias3_col = sb(ctx, "bias3_col", [P, 1])
        deg = sb(ctx, "deg", [P, NT])
        ln_st = sb(ctx, "ln_st", [P, Q1, 6])
        ln_mv = sb(ctx, "ln_mv", [P, Q1, 2])
        ln_rs = sb(ctx, "ln_rs", [P, Q1])
        ps = ctx.enter_context(nc.psum_tensor("ps", [P, 8, BANK], F32))

        with ExitStack() as l0:
            gcn_w = sb(l0, "gcn_w", [P, D])
            gcn_b = sb(l0, "gcn_b", [P, D])
            ln_g = sb(l0, "ln_g", [P, 1])
            ln_b = sb(l0, "ln_b", [P, 1])
            w_in = sb(l0, "w_in", [P, 2 * DI])
            conv_w = sb(l0, "conv_w", [P, KD, TAPS])
            conv_b = sb(l0, "conv_b", [P, KD])
            w_bc = sb(l0, "w_bc", [P, KD, 3 * 32])
            w_r = sb(l0, "w_r", [P, KD, RANK])
            w_dt = sb(l0, "w_dt", [RANK, DI])
            b_dt = sb(l0, "b_dt", [P, KD])
            a_neg = sb(l0, "a_neg", [P, KD, S_N])
            d_skip = sb(l0, "d_skip", [P, KD])
            w_out = sb(l0, "w_out", [P, KD, D])
            row_is = sb(l0, "row_is", [96, 32])
            pick = sb(l0, "pick", [96, 32, P], BF16)
            ax_t = sb(l0, "ax_t", [P, T0])
            g_act = sb(l0, "g_act", [P, Q0, D])
            h_norm = sb(l0, "h_norm", [P, Q0, D])
            xc = sb(l0, "xc", [P, KD, TAPS - 1 + T0])
            conv = sb(l0, "conv", [P, KD, T0])
            u = sb(l0, "u", [P, 2, KD, T0])
            sz = sb(l0, "sz", [P, 2, KD, T0])
            rank_t = sb(l0, "rank_t", [RANK, T0])
            bc1 = sb(l0, "bc1", [96, T0], BF16)
            bc2 = sb(l0, "bc2", [96, T0], BF16)
            bc_parts = sb(l0, "bc_parts", [96, 2, T0], BF16)
            bc_rest = sb(l0, "bc_rest", [96, T0])
            sp_e = sb(l0, "sp_e", [P, KD, T0])
            sp_v = sb(l0, "sp_v", [P, KD, T0])
            dt = sb(l0, "dt", [P, 2, KD, T0])
            du = sb(l0, "du", [P, 2, KD, T0])
            da = sb(l0, "da", [P, N_DA, T0])
            dbu = sb(l0, "dbu", [P, N_DBU, T0])
            hs = sb(l0, "hs", [P, N_H, T0])
            h_last = sb(l0, "h_last", [P, STEPS])
            cs = sb(l0, "cs", [P, N_CS, T0])
            hc = sb(l0, "hc", [P, N_PAIR, T0])
            hc_odd = sb(l0, "hc_odd", [P, 2, KD, T0])
            yg = sb(l0, "yg", [P, KD, T0])
            xo = sb(l0, "xo", [P, Q0, D])
            ln0_st = sb(l0, "ln0_st", [P, Q0, 6])
            ln0_mv = sb(l0, "ln0_mv", [P, Q0, 2])
            ln0_rs = sb(l0, "ln0_rs", [P, Q0])
            ln1_rs = sb(l0, "ln1_rs", [P, Q0])
            ln1_mv = sb(l0, "ln1_mv", [P, Q0, 2])
            ln1_st = sb(l0, "ln1_st", [P, Q0, 6])

        with ExitStack() as l1:
            v_ring = sb(l1, "v_ring", [P, N_V, HEADS - DVE_HEADS, T1])
            x_t = v_ring[:, 0:2].rearrange("p v h i -> p (v h i)")
            bh = sb(l1, "bh", [P, NT, D])
            stat_s = sb(l1, "stat_s", [P, NT, HEADS, 32], BF16)
            stat_m = sb(l1, "stat_m", [P, NT, 32], BF16)
            r_rows = sb(l1, "r_rows", [P, HEADS, T1])
            w_ring = sb(l1, "w_ring", [P, N_W, DVE_HEADS, T1])
            s8 = sb(l1, "s8", [P, N_S, HEADS, T1], FP8)
            m1 = sb(l1, "m1", [P, N_S, T1], FP8)
            dh = sb(l1, "dh", [P, NT, (HEADS - DVE_HEADS) * F])
            e_all = sb(l1, "e_all", [P, NT, 2 * HEADS])
            d_max = sb(l1, "d_max", [P, HEADS])
            d_all = sb(l1, "d_all", [P, HEADS])
            dv = e_all[:, :, 0:HEADS]
            r_now = e_all[:, 0:Q1, HEADS:]
            e_neg = sb(l1, "e_neg", [P, NT, HEADS])
            neg_c = e_neg
            bv = sb(l1, "bv", [P, NT, HEADS])
            cv = sb(l1, "cv", [P, NT, HEADS])
            r_nat = sb(l1, "r_nat", [P, NT + Q1, HEADS])
            deg_col = sb(l1, "deg_col", [P, F])
            den_raw = sb(l1, "den_raw", [P, T1])
            num_raw = sb(l1, "num_raw", [P, T1])
            den_p = sb(l1, "den_p", [P, Q1, HEADS])
            den_q = sb(l1, "den_q", [P, Q1, HEADS])
            den_m = sb(l1, "den_m", [P, Q1, HEADS])
            xo1 = sb(l1, "xo1", [P, Q1, D])
        with ExitStack() as l2:
            x2_t = sb(l2, "x2_t", [P, N])
            sup = sb(l2, "sup", [P, NT, D])
            dis = sb(l2, "dis", [P, NT])
            acc = sb(l2, "acc", [P, T1])
            xo2 = sb(l2, "xo2", [P, Q1, D])
            sup_h = sb(l2, "sup_h", [P, NT, D], FP22)
            sup_l = sb(l2, "sup_l", [P, NT, D], FP22)
            adj_h = sb(l2, "adj_h", [P, N_SPLIT, T1], FP22)
            adj_l = sb(l2, "adj_l", [P, N_SPLIT, T1], FP22)
            sums = sb(l2, "sums", [P, 2 * NT + 1])
            norms = sb(l2, "norms", [P, 2 * NT + 1])
            recips = sb(l2, "recips", [P, 2 * NT + 1])
            dots = sb(l2, "dots", [P, NT])
            w3b = sb(l2, "w3b", [P, 1])
            ln_plus, ln_minus, arg, tanh_e, tanh, gap, sq_norm, tmp = [
                sb(l2, name, [P, NT + 1]) for name in
                ("ln_plus", "ln_minus", "arg", "tanh_e", "tanh", "gap", "sq_norm", "tmp")]
            clipped, r_den, cx, cy, gap2, norm2, ln_norm2, by_norm2, clip2, ln_plus2, ln_gap2 = [
                sb(l2, name, [P, NT]) for name in
                ("clipped", "r_den", "cx", "cy", "gap2", "norm2", "ln_norm2", "by_norm2", "clip2", "ln_plus2", "ln_gap2")]
            hyp_bias = sb(l2, "hyp_bias", [P, D])
            bias_part = sb(l2, "bias_part", [P, 4, D])
            rl = sb(l2, "rl", [P, Q1, D])
            sq = sb(l2, "sq", [P, 2, Q1, D])
            f_sq, f_norm, f_recip = [sb(l2, name, [P, 2, Q1]) for name in ("f_sq", "f_norm", "f_recip")]
            f_k, f_arg, f_tanh = [sb(l2, name, [P, Q1]) for name in ("f_k", "f_arg", "f_tanh")]
            xo3 = sb(l2, "xo3", [P, Q1, D])
        ACC, PREP, TURN = 0, 4, 6

        NUM, DEN, NAT, RAW = 0, 2, 4, 6
        two = lambda bank: ps[:, bank:bank + 2, :].rearrange("p a b -> p (a b)")
        tiles8 = lambda bank: ps[:, bank:bank + 2, :].rearrange("p a (q d) -> p (a q) d", d=D)

        AX, M0, M1, BB, CB, Y = 0, 1, 2, 3, 5, 6
        tiles = lambda bank: ps[:, bank, :].rearrange("p (q d) -> p q d", q=Q0)

        setup_dmas = [
            (ident, t["ident"]), (gcn_w, t["gcn_w"]), (w_in, t["w_in"]),
            (gcn_b, t["gcn_b"].rearrange("(a d) -> a d", a=1).broadcast_to([P, D])),
            (ln_g, t["ln_g"].rearrange("(p a) -> p a", a=1)), (ln_b, t["ln_b"].rearrange("(p a) -> p a", a=1)),
            (conv_w, t["conv_w"].rearrange("(k p) w -> p k w", p=P)),
            (conv_b, t["conv_b"]),
            (w_bc, t["w_bc"].rearrange("(k p) r -> p k r", p=P)),
            (w_r, t["w_r"].rearrange("(k p) r -> p k r", p=P)),
            (w_dt, t["w_dt"]), (b_dt, t["b_dt"]),
            (a_neg, t["a_log"].rearrange("(k p) n -> p k n", p=P)),
            (d_skip, t["d_skip"]),
            (w_out, t["w_out"].rearrange("(k p) m -> p k m", p=P)), (row_is, t["row_is"]),
            (w1_t, t["w1_t"]), (a_bd, t["a_bd"]), (w2_t, t["w2_t"]), (w3_t, t["w3_t"]),
            (w3, t["w3"]), (bias3_col, t["bias3"].rearrange("(p a) -> p a", a=1)),
            (bias3, t["bias3"].rearrange("(a d) -> a d", a=1).broadcast_to([P, D])),
        ]
        setup_all = 16 * (len(setup_dmas) + 1)

        block = ctx.enter_context(nc.Block())

        @block.sync
        def _(sp):
            x_rows = t["x"].rearrange("(t p) d -> p t d", p=P)

            def load_x(part):
                rows = slice(part * NT // X_PARTS, (part + 1) * NT // X_PARTS)
                sp.dma_start(xa[:, rows, :], x_rows[:, rows, :]).then_inc(sem(f"x_in{part}"), 16)

            adj0 = adj_t.rearrange("(r two p) i -> r p two i", two=2, p=P)

            def load0(c, r):
                slot = r % RING
                sp.dma_start(ring[:, slot, :].rearrange("p (two i) -> p two i", two=2),
                             adj0[r][:, :, bass.ts(c, T0)]).then_inc(sem(f"adj_in{slot}"), 16)

            for r in range(NT // 2):
                if r < X_PARTS:
                    load_x(r)
                if r >= RING:
                    sp.wait_ge(sem("adj_free"), r - RING + 1)
                load0(0, r)
            with sp.Fori(1, C0) as c:
                for r in range(NT // 2):
                    sp.wait_ge(sem("adj_free"), c * (NT // 2) + (r - RING + 1))
                    load0(c, r)
            def load1(layer, c, r):
                if layer == 1:
                    sp.wait_ge(sem("num_summed"), c * NT + (NUM_CREDIT + r - RING + 1))
                else:
                    name, value = low_count(layer, c, r, -RING)
                    sp.wait_ge(sem(name), value)
                sp.dma_start(ring[:, r % RING, :], adj_t[r * P:(r + 1) * P, bass.ts(c, T1)])\
                    .then_inc(sem(f"adj_in{r % RING}"), 16)

            for layer in (1, 2, 3):
                if layer == 1:
                    sp.wait_ge(sem("adj_free"), LOADS)
                elif layer == 2:
                    sp.wait_ge(sem("num_summed"), LOADS + NUM_CREDIT)
                with sp.Fori(0, C1) as c:
                    for r in range(NT):
                        load1(layer, c, r)
            rows = out.rearrange("(c q p) d -> c p q d", q=Q1, p=P)
            for c in range(C1):
                sp.wait_ge(sem("x4_ready"), c + 1)
                sp.dma_start(rows[c], xa[:, c * Q1:(c + 1) * Q1, :]).then_inc(sem("out_done"), 16)
            sp.wait_ge(sem("out_done"), 16 * C1)

        @block.gpsimd
        def _(pool):
            pool.memset(half_neg[:], -0.5).then_inc(sem("halves"), 1)
            pool.memset(half_pos[:], 0.5).then_inc(sem("halves"), 1)
            pool.memset(eps[:], EPS).then_inc(sem("halves"), 1)
            pool.memset(h_last[:], 0.0).then_inc(sem("zeroed"), 1)
            pool.memset(xc[:], 0.0).then_inc(sem("zeroed"), 1)
            pool.wait_ge(sem("halves"), 3)
            link = Link(pool, sem("pool_link"))

            def rstd(rs, mv, q, stats, value, ready):
                pool.wait_ge(stats, value)
                link(pool.tensor_tensor(rs[:, 0:q], mv[:, 0:q, 1], eps[:, 0:q], ALU.add))
                pool.tensor_tensor(rs[:, 0:q], rs[:, 0:q], half_neg[:, 0:q], ALU.pow).then_inc(ready, 1)

            def prepare(n, i):
                if i == AT_G_RSTD:
                    rstd(ln0_rs, ln0_mv, Q0, sem("h_stats"), at(n, 1, 1), sem("h_rstd"))

            def finish0(c):
                rstd(ln1_rs, ln1_mv, Q0, sem("x1_stats"), at(c, 1, 1), sem("x1_rstd"))

            def chunk0(c):
                for i in range(STEPS):
                    n, k = divmod(i, KD)
                    m = n // 2 * KD + k
                    if has_next(c):
                        prepare(neighbour(c, 1), i)
                    if i == AT_X1_RSTD and has_previous(c):
                        finish0(neighbour(c, -1))
                    pool.wait_ge(sem("scanned"), at(c, STEPS, N_DA + i + 1))
                    if k == 0:
                        pool.wait_ge(sem("c_rows"), at(c, S_N, n + 2))
                    if n % 2 == 0:
                        pool.wait_ge(sem("y_summed"), at(c, PAIRS, m + 1))
                        pool.tensor_tensor(hc[:, m % N_PAIR, :], hs[:, i % N_H, :], cs[:, n % N_CS, :],
                                           ALU.mult).then_inc(sem("hc_ready"), 1)
                    else:
                        odd = n // 2 % 2
                        if k == 0:
                            pool.wait_ge(sem("pair_ready"), at(c, PAIRS, m + 1))
                        pool.tensor_tensor(hc_odd[:, odd, k, :], hs[:, i % N_H, :], cs[:, n % N_CS, :],
                                           ALU.mult).then_inc(sem("hc_ready"), 1)
                        if k == KD - 1:
                            for kk in range(KD):
                                mm = m - k + kk
                                pool.wait_ge(sem("hc_ready"), at(c, STEPS, HC_CREDIT + i + 1 - k + kk))
                                pool.tensor_tensor(hc[:, mm % N_PAIR, :], hc[:, mm % N_PAIR, :], hc_odd[:, odd, kk, :],
                                                   ALU.add).then_inc(sem("pair_ready"), 1)

            for i in range(STEPS):
                prepare((0, 0), i)
            link.straight()
            pool.sem_inc(sem("hc_ready"), HC_CREDIT)
            pool.sem_inc(sem("pair_ready"), PAIR_CREDIT)
            chunk0(FIRST)
            link.straight()
            with pool.Fori(0, LOOPS0) as pair:
                link.body(pair, POOL_RATE0)
                for c in in_loop(pair):
                    chunk0(c)
            link.leave(LOOPS0)
            for c in AFTER:
                chunk0(c)
            finish0(AFTER[-1])
            link.straight()

            pool.wait_ge(sem("x1_ready"), C0)
            pool.memset(deg_col[:], 0.0).then_inc(sem("stat_zero"), 1)
            pool.memset(r_nat[:], 1.0).then_inc(sem("stat_zero"), 1)
            pool.memset(stat_s[:], 0.0).then_inc(sem("stat_zero"), 1)
            pool.memset(stat_m[:], 0.0).then_inc(sem("stat_zero"), 1)
            pool.wait_ge(sem("stat_zero"), 4)
            pool.memset(deg_col[:, DEG:DEG + 1], 1.0).then_inc(sem("stat_zero"), 1)
            pool.wait_ge(sem("d_max_ready"), 1)
            pool.partition_all_reduce(d_all[:], d_max[:], P, bass.bass_isa.ReduceOp.max).then_inc(sem("d_all_ready"), 1)

            def finish1(c):
                rstd(ln_rs, ln_mv, Q1, sem("x2_stats"), c + 1, sem("x2_rstd"))

            def chunk1(c, first):
                if not first:
                    link.body(c - 1, 1)
                for j in range(NT):
                    adj = ring[:, j % RING, :].unsqueeze(1).broadcast_to([P, HEADS - DVE_HEADS, T1])
                    pool.wait_ge(sem(f"adj_in{j % RING}"), c * (16 * NT // RING) + 16 * (LOADS // RING + j // RING + 1))
                    pool.wait_ge(sem("relu_ready"), c * NT + (j + 1 + RELU_CREDIT))
                    pool.tensor_tensor(v_ring[:, j % N_V], v_ring[:, j % N_V], adj, ALU.mult).then_inc(sem("v_ready"), 1)
                    if j == RSTD_AT and not first:
                        finish1(c - 1)

            chunk1(0, True)
            with pool.Fori(1, C1) as c:
                chunk1(c, False)
            link.leave(C1 - 1)
            finish1(C1 - 1)
            link.straight()

            pool.wait_ge(sem("x2_ready"), C1)
            pool.tensor_scalar(dis[:], deg[:], 1.0, None, ALU.add).then_inc(sem("deg_plus"), 1)
            pool.wait_ge(sem("deg_plus"), 1)
            pool.tensor_tensor(dis[:], dis[:], half_neg[:], ALU.pow).then_inc(sem("dis_ready"), 1)

            pool.sem_inc(sem("pool_low_ready"), RING // 4)

            def split_low(layer, c, j):
                if pool_splits(j):
                    pool.wait_ge(sem("high_ready"), c * NT + ((layer - 2) * LOADS + j + 1))
                    pool.tensor_tensor(adj_l[:, j % N_SPLIT, :], ring[:, j % RING, :], adj_h[:, j % N_SPLIT, :].bitcast(F32),
                                       ALU.subtract).then_inc(sem("pool_low_ready"), 1)

            def finish2(c, j):
                if j == AT2_RSTD:
                    rstd(ln_rs, ln_mv, Q1, sem("x3_stats"), c + 1, sem("x3_rstd"))

            def layer_loop(layer, finish):
                for j in range(NT):
                    split_low(layer, 0, j)
                with pool.Fori(1, C1) as c:
                    link.body(c - 1, 1)
                    for j in range(NT):
                        split_low(layer, c, j)
                        finish(c - 1, j)
                link.leave(C1 - 1)
                for j in range(NT):
                    finish(C1 - 1, j)
                link.straight()

            layer_loop(2, finish2)

            def finish3(c, j):
                if j == AT3_ROOT:
                    pool.wait_ge(sem("f_sq_ready"), c + 1)
                    pool.tensor_tensor(f_norm[:].rearrange("p a q -> p (a q)"), f_sq[:].rearrange("p a q -> p (a q)"),
                                       half_pos[:, 0:2 * Q1], ALU.pow).then_inc(sem("f_norm_ready"), 1)
                if j == AT3_RSTD:
                    rstd(ln_rs, ln_mv, Q1, sem("x4_stats"), c + 1, sem("x4_rstd"))

            layer_loop(3, finish3)

        @block.scalar
        def _(act):
            for dst, src in setup_dmas:
                act.dma_start(dst[:], src).then_inc(sem("setup"), 16)
            act.dma_start(w1_cat[:, 0:D], t["w1"]).then_inc(sem("setup"), 16)
            act.wait_ge(sem("setup"), setup_all)
            link = Link(act, sem("act_link"))
            link(act.activation(a_neg[:], a_neg[:], ACT.Exp))
            act.mul(a_neg[:], a_neg[:], -1.0).then_inc(sem("a_ready"), 1)
            act.wait_ge(sem("a_ready"), 1)
            act.wait_ge(sem("zeroed"), 2)
            link.straight()

            def take_ax(n):
                act.wait_ge(sem("adj_free"), at(n, NT // 2, NT // 2))
                act.copy(ax_t[:], ps[:, AX, :]).then_inc(sem("ax_taken"), 1)

            def prepare(n, i, first=False):
                half = n[1] % 2
                if i == AT_H_T:
                    if not first:
                        act.wait_ge(sem("conv_ready"), at(n, KD, 0))
                    link.mark(act.copy(xc[:, :, 0:TAPS - 1], xc[:, :, T0:T0 + TAPS - 1]))
                    act.wait_ge(sem("h_turned"), at(n, 1, 1))
                    act.activation(ax_t[:], ps[:, M0, :], ACT.Identity, bias=ln_b[:, 0:1],
                                   scale=ln_g[:, 0:1]).then_inc(sem("h_t_ready"), 1)
                    link.wait()
                if i == AT_XC_OUT:
                    for k in range(KD):
                        act.wait_ge(sem("xz_ready"), at(n, 4, k + 1))
                        act.copy(xc[:, k, TAPS - 1:], ps[:, M0 + k, :]).then_inc(sem("xc_ready"), 1)
                if i == AT_SILU:
                    for k in range(KD):
                        act.wait_ge(sem("xz_ready"), at(n, 4, KD + k + 1))
                        act.activation(sz[:, half, k, :], ps[:, M0 + k, :], ACT.Silu).then_inc(sem("z_ready"), 1)
                    for k in range(KD):
                        act.wait_ge(sem("conv_ready"), at(n, KD, k + 1))
                        act.activation(u[:, half, k, :], conv[:, k, :], ACT.Silu,
                                       bias=conv_b[:, k:k + 1]).then_inc(sem("u_ready"), 1)
                    act.preload_act_table_set("natural_log_exp_and_others")
                if i == AT_BC + 1:
                    act.wait_ge(sem("rank_ready"), at(n, 1, 1))
                    act.copy(rank_t[:], ps[0:RANK, M1, :]).then_inc(sem("rank_taken"), 1)
                    act.wait_ge(sem("bc_raw"), at(n, 1, 1))
                    act.copy(bc1[:], ps[0:96, M0, :])
                    act.copy(bc_parts[0:32, half, :], ps[0:32, M0, :]).then_inc(sem("bc1_ready"), 1)
                if i == AT_SOFTPLUS:
                    for k in range(KD):
                        act.wait_ge(sem("dt_raw"), at(n, KD, k + 1))
                        link.mark(act.activation(sp_v[:, k, :], ps[:, M0 + k, :], ACT.Identity, bias=b_dt[:, k:k + 1]))
                    link.wait()
                    link.mark(act.activation(sp_e[:], sp_v[:], ACT.Abs))
                if i == AT_SOFTPLUS + 1:
                    link.wait()
                    link.mark(act.activation(sp_e[:], sp_e[:], ACT.Exp, scale=-1.0))
                if i == AT_SOFTPLUS + 2:
                    link.wait()
                    act.activation(sp_e[:], sp_e[:], ACT.Ln, bias=1.0).then_inc(sem("sp_ready"), 1)

            def chunk0(c):
                half = c[1] % 2
                if has_next(c):
                    take_ax(neighbour(c, 1))
                for i in range(STEPS):
                    n, k = divmod(i, KD)
                    if i == 0:
                        act.wait_ge(sem("dt_done"), at(c, 1, 1))
                    act.wait_ge(sem("scanned"), at(c, STEPS, i + 1))
                    act.activation(da[:, i % N_DA, :], dt[:, half, k, :], ACT.Exp,
                                   scale=a_neg[:, k, n:n + 1]).then_inc(sem("da_ready"), 1)
                    if k == 0:
                        act.wait_ge(sem("c_bcast"), at(c, S_N, n + 1))
                        act.wait_ge(sem("hc_ready"), at(c, STEPS, KD * n + KD))
                        act.copy(cs[:, n % N_CS, :], ps[:, CB, :]).then_inc(sem("c_rows"), 1)
                    if has_next(c):
                        prepare(neighbour(c, 1), i)

            take_ax((0, 0))
            for i in range(STEPS):
                prepare((0, 0), i, first=True)
            link.straight()
            act.sem_inc(sem("c_rows"), 1)
            chunk0(FIRST)
            link.straight()
            with act.Fori(0, LOOPS0) as pair:
                link.body(pair, ACT_RATE0)
                for c in in_loop(pair):
                    chunk0(c)
            link.leave(LOOPS0)
            for c in AFTER:
                chunk0(c)
            link.straight()

            for g in range(NT // 4):
                act.wait_ge(sem("x1_turned"), g + 1)
                act.copy(x_t[:, g * BANK:(g + 1) * BANK], ps[:, NAT + g % 2, :]).then_inc(sem("x1_t_ready"), 1)
            for g in range(NT // 2):
                act.wait_ge(sem("h_raw"), g + 1)
                src = ps[:, NAT + g % 2, 0:2 * (D + 2 * HEADS)].rearrange("p (a b) -> p a b", a=2)
                act.copy(bh[:, 2 * g:2 * g + 2, :], src[:, :, 0:D])
                act.copy(e_all[:, 2 * g:2 * g + 2, :], src[:, :, D:]).then_inc(sem("h_taken"), 1)
            act.wait_ge(sem("e_ready"), 1)
            act.wait_ge(sem("stat_zero"), 4)
            act.activation(bv[:], e_all[:, :, 0:HEADS], ACT.Exp)
            act.activation(cv[:], e_neg[:], ACT.Exp)
            act.activation(r_nat[:, 0:NT, :], e_all[:, :, HEADS:], ACT.Exp, scale=1 - LEAKY).then_inc(sem("bc_ready"), 1)
            act.wait_ge(sem("neg_c_ready"), 1)
            act.sem_inc(sem("relu_ready"), RELU_CREDIT)
            act.sem_inc(sem("sign_ready"), 1)

            def take_r(c, ahead, heads):
                if 1 not in heads:
                    act.wait_ge(sem("relu_ready"), c * NT + (ahead * NT + RELU_CREDIT))
                for h in heads:
                    act.wait_ge(sem("r_raw"), c * HEADS + (ahead * HEADS + R_ORDER.index(h) + 1))
                    if h == 1:
                        act.wait_ge(sem("w_ready"), c * NT + (ahead * NT + 1))
                    act.copy(r_rows[:, h, :], two(RAW if h % 2 else NAT)).then_inc(sem("r_taken"), 1)


            def take_sums1(c):
                act.wait_ge(sem("den_summed"), c * NT + (NT + N_S))
                act.copy(den_raw[:], two(DEN)).then_inc(sem("sums_taken"), 1)
                act.copy(num_raw[:], two(NUM)).then_inc(sem("sums_taken"), 1)

            def signs(c, j):
                act.wait_ge(sem("v_ready"), c * NT + (j + 1))
                act.wait_ge(sem("den_summed"), c * NT + (j + 1))
                act.sem_inc(sem("act_settled"), 1)
                act.activation(s8[:, j % N_S, DVE_HEADS:, :], v_ring[:, j % N_V], ACT.Sign,
                               saturate=False).then_inc(sem("sign_ready"), 1)

            def chunk1(c, first):
                act.wait_ge(sem("r_taken"), c * 3 + 2)
                for j in range(NT):
                    if act_masks(j):
                        act.wait_ge(sem(f"adj_in{j % RING}"), c * (16 * NT // RING) + 16 * (LOADS // RING + j // RING + 1))
                        act.wait_ge(sem("den_summed"), c * NT + (j + 1))
                        act.sem_inc(sem("act_settled"), 1)
                        act.activation(m1[:, j % N_S, :], ring[:, j % RING, :], ACT.Sign,
                                       saturate=False).then_inc(sem("mask_ready"), 1)
                    act.wait_ge(sem("num_summed"), c * NT + (NUM_CREDIT - N_V + j + 1))
                    if j < N_V:
                        act.wait_ge(sem("sign_ready"), c * NT + 1)
                    for h in range(DVE_HEADS, HEADS):
                        ins = act.activation(v_ring[:, j % N_V, h - DVE_HEADS, :], r_rows[:, h, :], ACT.Relu,
                                             bias=neg_c[:, j, h:h + 1])
                    ins.then_inc(sem("relu_ready"), 1)
                    if j == 0:
                        take_r(c, 0, (1,))
                    if j >= 1:
                        signs(c, j - 1)
                    if j == SUMS_AT and not first:
                        take_sums1(c - 1)
                take_r(c, 1, (2, 3))
                signs(c, NT - 1)

            take_r(0, 0, (2, 3))
            chunk1(0, True)
            with act.Fori(1, C1) as c:
                chunk1(c, False)
            take_sums1(C1 - 1)

            def take_mx(g):
                act.wait_ge(sem("mx_raw"), g + 1)
                act.wait_ge(sem("mx_summed"), g + 1)
                act.copy(sup[:, 4 * g:4 * g + 4, :], tiles(TURN + g % 2))
                act.activation(sq[:, g % 2, 0:4, :], tiles(TURN + g % 2), ACT.Square).then_inc(sem("mx_ready"), 1)

            def turn_in(layer, with_mx=False):
                for g in range(NT // 4):
                    act.wait_ge(sem(f"x_turned_{layer}"), g + 1)
                    act.copy(x2_t[:, g * BANK:(g + 1) * BANK], ps[:, PREP + g % 2, :]).then_inc(sem(f"x_t_ready_{layer}"), 1)
                    if with_mx and g >= 1:
                        take_mx(g - 1)
                if with_mx:
                    take_mx(NT // 4 - 1)

            def take_sums(layer, c):
                act.wait_ge(sem("split_used"), c * NT + ((layer - 2) * LOADS + NT + N_SPLIT))
                act.copy(acc[:], two(ACC)).then_inc(sem(f"acc_taken_{layer}"), 1)

            def split_high(layer, c, j):
                act.wait_ge(sem(f"adj_in{j % RING}"),
                            c * (16 * NT // RING) + 16 * (layer * LOADS // RING + j // RING + 1))
                act.wait_ge(sem("split_used"), c * NT + ((layer - 2) * LOADS + j + 1))
                act.copy(adj_h[:, j % N_SPLIT, :], ring[:, j % RING, :]).then_inc(sem("high_ready"), 1)

            def layer_loop(layer, finish):
                for j in range(NT):
                    split_high(layer, 0, j)
                with act.Fori(1, C1) as c:
                    for j in range(NT):
                        split_high(layer, c, j)
                        if j == SUMS2_AT:
                            take_sums(layer, c - 1)
                        finish(c - 1, j)
                take_sums(layer, C1 - 1)
                for j in range(NT):
                    finish(C1 - 1, j)

            turn_in(2)
            layer_loop(2, lambda c, j: None)

            act.wait_ge(sem("w3b_raw"), 1)
            act.copy(w3b[:], ps[:, ACC + 1, 0:1]).then_inc(sem("w3b_ready"), 1)
            turn_in(3, with_mx=True)
            act.activation(xo3[:, 0, :], bias3[:], ACT.Square, accum_out=sums[:, 2 * NT:]).then_inc(sem("sums_ready"), 1)
            act.preload_act_table_set("natural_log_exp_and_others")
            act.wait_ge(sem("sums_floor"), 1)
            act.activation(norms[:], sums[:], ACT.Ln).then_inc(sem("norms_ln"), 1)
            act.wait_ge(sem("norms_ln"), 1)
            act.activation(norms[:], norms[:], ACT.Exp, scale=0.5).then_inc(sem("norms_ready"), 1)
            act.wait_ge(sem("clipped_ready"), 1)
            act.activation(ln_plus[:, 0:NT], clipped[:], ACT.Ln, bias=1.0)
            act.activation(ln_minus[:, 0:NT], clipped[:], ACT.Ln, bias=1.0, scale=-1.0).then_inc(sem("atanh_ln"), 1)
            act.wait_ge(sem("tanh_in"), 1)
            act.activation(tanh_e[:], arg[:], ACT.Exp, scale=-2.0).then_inc(sem("tanh_exp"), 1)
            act.wait_ge(sem("norm2_sq"), 1)
            act.activation(ln_norm2[:], norm2[:], ACT.Ln).then_inc(sem("norm2_ln"), 1)
            act.wait_ge(sem("norm2_ln"), 1)
            act.activation(norm2[:], ln_norm2[:], ACT.Exp, scale=0.5)
            act.activation(by_norm2[:], ln_norm2[:], ACT.Exp, scale=-0.5)
            act.activation(ln_gap2[:], gap2[:], ACT.Ln).then_inc(sem("norm2_ready"), 1)
            act.wait_ge(sem("clip2_ready"), 1)
            act.activation(ln_plus2[:], clip2[:], ACT.Ln, bias=1.0).then_inc(sem("atanh2_ln"), 1)

            def finish3(c, j):
                if j == AT3_SQUARES:
                    act.wait_ge(sem("s_turned"), c + 1)
                    act.wait_ge(sem("rl_used"), c + 1)
                    act.activation(rl[:], tiles8(TURN), ACT.Relu).then_inc(sem("rl_ready"), 1)
                    act.activation(sq[:, 0], tiles8(TURN), ACT.Square).then_inc(sem("turn3_taken"), 1)
                    act.wait_ge(sem("rl_ready"), c + 1)
                    act.activation(sq[:, 1], rl[:], ACT.Square).then_inc(sem("sq_ready"), 1)
                if j == AT3_EXP:
                    act.wait_ge(sem("f_arg_ready"), c + 1)
                    act.activation(f_tanh[:], f_arg[:], ACT.Exp, scale=-2.0).then_inc(sem("f_exp"), 1)

            act.sem_inc(sem("turn3_taken"), 1)
            layer_loop(3, finish3)

        @block.vector
        def _(dve):
            link = Link(dve, sem("dve_link"))
            dve.wait_ge(sem("setup"), setup_all)
            dve.tensor_copy(pick[:], row_is[:].unsqueeze(2).broadcast_to([96, 32, P])).then_inc(sem("consts"), 1)
            dve.sem_inc(sem("scanned"), N_DA)
            dve.sem_inc(sem("dbu_ready"), DBU_CREDIT)
            dve.sem_inc(sem("out_taken"), 2)
            dve.wait_ge(sem("zeroed"), 2)
            for part in range(X_PARTS):
                dve.wait_ge(sem(f"x_in{part}"), 16)

            def stats(st, mv, data, q_n, ready):
                for q in range(q_n):
                    link.mark(dve.bn_stats(st[:, q, :], data[:, q, :]))
                link.wait()
                dve.sem_inc(sem("dve_settled"), 1)
                for q in range(q_n):
                    ins = dve.bn_aggr(mv[:, q, :], st[:, q, :])
                ins.then_inc(ready, 1)

            def normalise(dst, data, mv, rs, q_n, ready):
                for q in range(q_n):
                    ins = dve.tensor_scalar(dst(q), data[:, q, :], mv[:, q, 0:1], rs[:, q:q + 1],
                                            ALU.subtract, ALU.mult)
                ins.then_inc(ready, 1)

            conv_at = [0, 0]

            def prepare(n, i):
                half = n[1] % 2
                if i == AT_G_STATS:
                    dve.wait_ge(sem("g_ready"), at(n, 1, 1))
                    link(dve.tensor_tensor(g_act[:], tiles(M1), gcn_b[:].unsqueeze(1).broadcast_to([P, Q0, D]), ALU.add))
                    link(dve.tensor_scalar(g_act[:], g_act[:], 0.0, None, ALU.max))
                    stats(ln0_st, ln0_mv, g_act, Q0, sem("h_stats"))
                if i == AT_G_NORM:
                    dve.wait_ge(sem("h_rstd"), at(n, 1, 1))
                    normalise(lambda q: h_norm[:, q, :], g_act, ln0_mv, ln0_rs, Q0, sem("h_norm_ready"))
                if AT_CONV <= i < AT_CONV + TAPS:
                    tap = i - AT_CONV
                    for k in range(KD):
                        src, w = xc[:, k, tap:tap + T0], conv_w[:, k, tap:tap + 1]
                        if tap == 0:
                            dve.wait_ge(sem("xc_ready"), at(n, KD, k + 1))
                            ins = dve.tensor_scalar(conv[:, k, :], src, w, None, ALU.mult)
                        else:
                            link.wait(conv_at[k])
                            ins = dve.scalar_tensor_tensor(out=conv[:, k, :], in0=src, scalar=w, in1=conv[:, k, :],
                                                           op0=ALU.mult, op1=ALU.add)
                        if tap < TAPS - 1:
                            conv_at[k] = link.mark(ins)
                        else:
                            ins.then_inc(sem("conv_ready"), 1)
                if i == AT_BC_SPLIT:
                    dve.wait_ge(sem("bc1_ready"), at(n, 1, 1))
                    dve.tensor_tensor(bc_rest[:], ps[0:96, M0, :], bc1[:], ALU.subtract).then_inc(sem("bc_taken"), 1)
                if i == AT_BC_SPLIT + 1:
                    dve.wait_ge(sem("bc_taken"), at(n, 1, 1))
                    link.mark(dve.tensor_copy(bc2[:], bc_rest[:]))
                    link(dve.tensor_copy(bc_parts[32:64, half, :], bc_rest[32:64, :]))
                    link(dve.tensor_tensor(bc_rest[64:96, :], bc_rest[64:96, :], bc2[64:96, :], ALU.subtract))
                    dve.tensor_copy(bc_parts[64:96, half, :], bc_rest[64:96, :]).then_inc(sem("bc_split"), 1)
                if i == AT_DT:
                    dve.wait_ge(sem("sp_ready"), at(n, 1, 1))
                    dve.scalar_tensor_tensor(out=dt[:, half], in0=sp_v[:], scalar=0.0, in1=sp_e[:], op0=ALU.max,
                                             op1=ALU.add).then_inc(sem("dt_done"), 1)
                if i == AT_DT + 1:
                    dve.wait_ge(sem("dt_done"), at(n, 1, 1))
                    dve.wait_ge(sem("u_ready"), at(n, KD, KD))
                    link(dve.tensor_tensor(du[:, half], dt[:, half], u[:, half], ALU.mult))

            def finish0(c, i):
                half = c[1] % 2
                if i == AT_GATE:
                    for k in range(KD):
                        dve.wait_ge(sem("y_summed"), at(c, PAIRS, N_PAIR + PAIRS - KD + k + 1))
                        link(dve.scalar_tensor_tensor(out=yg[:, k, :], in0=u[:, half, k, :], scalar=d_skip[:, k:k + 1],
                                                      in1=ps[:, Y + k, :], op0=ALU.mult, op1=ALU.add))
                        dve.tensor_tensor(yg[:, k, :], yg[:, k, :], sz[:, half, k, :], ALU.mult).then_inc(sem("gated"), 1)
                rows = at(c, Q0, 0)
                if i == AT_X1_STATS:
                    dve.wait_ge(sem("out_ready"), at(c, 1, 1))
                    dve.tensor_tensor(xo[:], tiles(M1), xa[:, bass.ds(rows, Q0), :], ALU.add).then_inc(sem("out_taken"), 1)
                    dve.wait_ge(sem("out_taken"), at(c, 1, 3))
                    stats(ln1_st, ln1_mv, xo, Q0, sem("x1_stats"))
                if i == AT_X1:
                    dve.wait_ge(sem("x1_rstd"), at(c, 1, 1))
                    normalise(lambda q: xb[:, bass.ds(rows + q, 1), :].rearrange("p a d -> p (a d)"),
                              xo, ln1_mv, ln1_rs, Q0, sem("x1_ready"))

            def chunk0(c):
                half = c[1] % 2

                def step_dbu(i):
                    n, k = divmod(i, KD)
                    if k == 0:
                        dve.wait_ge(sem("b_bcast"), at(c, S_N, n + 1))
                    if i >= N_DBU:
                        dve.wait_ge(sem("scanned"), at(c, STEPS, N_DA + i - N_DBU + 1))
                    dve.tensor_tensor(dbu[:, i % N_DBU, :], du[:, half, k, :], ps[:, BB + n % 2, :],
                                      ALU.mult).then_inc(sem("dbu_ready"), 1)

                def step_keep(i):
                    dve.wait_ge(sem("scanned"), at(c, STEPS, N_DA + i + 1))
                    return link.mark(dve.tensor_copy(h_last[:, i:i + 1], hs[:, i % N_H, T0 - 1:T0]))

                kept = [0] * STEPS
                step_dbu(0)
                for i in range(STEPS):
                    if i + 1 < STEPS:
                        step_dbu(i + 1)
                    dve.wait_ge(sem("dbu_ready"), at(c, STEPS, DBU_CREDIT + i + 1))
                    dve.wait_ge(sem("da_ready"), at(c, STEPS, i + 1))
                    dve.wait_ge(sem("hc_ready"), at(c, STEPS, HC_CREDIT - N_H + i + 1))
                    if i >= N_H:
                        link.wait(kept[i - N_H])
                    dve.tensor_tensor_scan(hs[:, i % N_H, :], da[:, i % N_DA, :], dbu[:, i % N_DBU, :],
                                           h_last[:, i:i + 1], ALU.mult, ALU.add).then_inc(sem("scanned"), 1)
                    if i >= 1:
                        kept[i - 1] = step_keep(i - 1)
                    if has_next(c):
                        prepare(neighbour(c, 1), i)
                    if has_previous(c):
                        finish0(neighbour(c, -1), i)
                kept[STEPS - 1] = step_keep(STEPS - 1)
                link.wait()

            for i in range(STEPS):
                prepare((0, 0), i)
            link.straight()
            chunk0(FIRST)
            link.straight()
            with dve.Fori(0, LOOPS0) as pair:
                link.body(pair, RATE0)
                for c in in_loop(pair):
                    chunk0(c)
            link.leave(LOOPS0)
            for c in AFTER:
                chunk0(c)
            for i in range(STEPS):
                finish0(AFTER[-1], i)
            link.straight()

            dve.sem_inc(sem("x_taken"), 1)
            dve.wait_ge(sem("x1_ready"), C0)
            dve.wait_ge(sem("wa_raw"), 1)
            dve.tensor_copy(w1_cat[:, D:], ps[:, RAW, 0:2 * HEADS]).then_inc(sem("w1_cat_ready"), 1)
            dve.wait_ge(sem("h_taken"), NT // 2)
            e_dst, e_src = e_all[:, :, 0:HEADS], e_all[:, :, HEADS:]
            dve.tensor_reduce(d_max[:], e_dst.rearrange("p t h -> p h t"), AX_X, ALU.max).then_inc(sem("d_max_ready"), 1)
            dve.wait_ge(sem("d_all_ready"), 1)
            d_wide = d_all[:].unsqueeze(1).broadcast_to([P, NT, HEADS])
            link.mark(dve.tensor_tensor(e_src, e_src, d_wide, ALU.add))
            link(dve.tensor_tensor(e_dst, e_dst, d_wide, ALU.subtract))
            dve.tensor_scalar(e_neg[:], e_dst, LEAKY - 1, E_MAX, ALU.mult, ALU.min).then_inc(sem("e_ready"), 1)
            dve.wait_ge(sem("bc_ready"), 1)
            link.mark(dve.tensor_scalar(r_nat[:, 0:NT, :], r_nat[:, 0:NT, :], float(R_MAX), None, ALU.min))
            link.mark(dve.tensor_tensor(dv, bv[:], cv[:], ALU.mult))
            dve.tensor_scalar(neg_c[:], cv[:], -1.0, None, ALU.mult).then_inc(sem("neg_c_ready"), 1)
            link.wait()
            dve.tensor_copy(r_now, r_nat[:, 0:Q1, :]).then_inc(sem("r_now_ready"), 1)
            own = slice(DVE_HEADS * F, D)
            wide = lambda v, n: v.unsqueeze(3).broadcast_to([P, NT, n, F])
            link(dve.tensor_tensor(dh[:].rearrange("p t (h f) -> p t h f", f=F),
                                   bh[:, :, own].rearrange("p t (h f) -> p t h f", f=F),
                                   wide(dv[:, :, DVE_HEADS:], HEADS - DVE_HEADS), ALU.mult))
            bh4 = bh[:].rearrange("p t (h f) -> p t h f", f=F)
            link(dve.tensor_tensor(bh4, bh4, wide(bv[:], HEADS), ALU.mult))
            dve.wait_ge(sem("stat_zero"), 5)
            masked = stat_m[:, :, MASKED:MASKED + HEADS * PARTS].rearrange("p t (h a) -> p t h a", a=PARTS)
            for part in range(PARTS):
                for rest, into in ((bv[:], stat_s[:, :, :, part]), (dv, masked[:, :, :, part])):
                    link(dve.tensor_copy(into, rest))
                    if part < PARTS - 1:
                        link(dve.tensor_tensor(rest, rest, into, ALU.subtract))
                link.mark(dve.tensor_scalar(stat_s[:, :, :, PARTS + part], masked[:, :, :, part], -1.0, None, ALU.mult))
            link.wait()
            dve.sem_inc(sem("bh_ready"), 1)
            dve.sem_inc(sem("w_ready"), 1)
            link.straight()

            def attend(c):
                rows = bass.ds(c * Q1, Q1)
                dve.wait_ge(sem("den_turned"), c + 1)
                sums = tiles8(NAT).rearrange("p q (h f) -> p q h f", f=F)
                link.mark(dve.tensor_copy(deg[:, rows], sums[:, :, 0, DEG]))
                link.mark(dve.tensor_reduce(den_p[:], sums[:, :, :, 0:PARTS], AX_X, ALU.add))
                link.mark(dve.tensor_reduce(den_q[:], sums[:, :, :, PARTS:2 * PARTS], AX_X, ALU.add))
                for b in range(2):
                    half = slice(b * Q1 // 2, (b + 1) * Q1 // 2)
                    ins = dve.tensor_reduce(den_m[:, half, :], sums[:, half, b, MASKED:MASKED + HEADS * PARTS]
                                            .rearrange("p q (h a) -> p q h a", a=PARTS), AX_X, ALU.add)
                ins.then_inc(sem("den_used"), 1)
                dve.wait_ge(sem("den_used"), c + 1)
                link(dve.tensor_tensor(den_q[:], den_q[:], den_m[:], ALU.add))
                link(dve.tensor_tensor(den_p[:], den_p[:], r_nat[:, rows, :], ALU.mult))
                link(dve.tensor_tensor(den_p[:], den_p[:], den_q[:], ALU.add))
                link(dve.reciprocal(den_p[:], den_p[:]))
                dve.wait_ge(sem("num_turned"), c + 1)
                dve.tensor_tensor(xo1[:].rearrange("p q (h f) -> p (q h) f", f=F),
                                  tiles8(RAW).rearrange("p q (h f) -> p (q h) f", f=F),
                                  den_p[:].rearrange("p q h -> p (q h)").unsqueeze(2).broadcast_to([P, Q1 * HEADS, F]),
                                  ALU.mult).then_inc(sem("x_taken"), 1)
                dve.wait_ge(sem("x_taken"), c + 2)
                link(dve.tensor_tensor(xo1[:], xo1[:], xb[:, rows, :], ALU.add))
                stats(ln_st, ln_mv, xo1, Q1, sem("x2_stats"))

            def finish1(c):
                dve.wait_ge(sem("x2_rstd"), c + 1)
                normalise(lambda q: xa[:, bass.ds(c * Q1 + q, 1), :].rearrange("p a d -> p (a d)"),
                          xo1, ln_mv, ln_rs, Q1, sem("x2_ready"))

            def chunk1(c, first):
                if not first:
                    link.body(c - 1, RATE1)
                dve.wait_ge(sem("r_raw"), c * HEADS + (R_ORDER.index(0) + 1))
                dve.wait_ge(sem("w_ready"), c * NT + 1)
                link(dve.tensor_copy(r_rows[:, 0, :], two(NAT)))
                dve.wait_ge(sem("r_taken"), c * 3 + 3)
                for j in range(NT):
                    adj = ring[:, j % RING, :]
                    sl = j % N_S
                    dve.wait_ge(sem(f"adj_in{j % RING}"), c * (16 * NT // RING) + 16 * (LOADS // RING + j // RING + 1))
                    dve.wait_ge(sem("den_summed"), c * NT + (j + 1))
                    dve.sem_inc(sem("dve_settled"), 1)
                    if not act_masks(j):
                        link.mark(dve.tensor_scalar(m1[:, sl, :], adj, 0.0, None, ALU.is_gt, saturate=False))
                    for h in range(DVE_HEADS):
                        ins = dve.tensor_scalar(s8[:, sl, h, :], r_rows[:, h, :], cv[:, j, h:h + 1], None,
                                                ALU.is_gt, saturate=False)
                        link.mark(ins)
                    dve.wait_ge(sem("num_summed"), c * NT + (NUM_CREDIT - N_W + j + 1))
                    for h in range(DVE_HEADS):
                        ins = dve.scalar_tensor_tensor(out=w_ring[:, j % N_W, h, :], in0=r_rows[:, h, :],
                                                       scalar=cv[:, j, h:h + 1], in1=adj, op0=ALU.max, op1=ALU.mult)
                    ins.then_inc(sem("w_ready"), 1)
                    link.wait()
                    if act_masks(j):
                        dve.wait_ge(sem("mask_ready"), c * (NT // 2) + (j // 2 + 1))
                    s8w = s8[:, sl, 0:DVE_HEADS, :].bitcast(U32)
                    dve.tensor_tensor(s8w, s8w, m1[:, sl, :].bitcast(U32).unsqueeze(1)
                                      .broadcast_to([P, DVE_HEADS, T1 // 4]), ALU.bitwise_and).then_inc(sem("masked"), 1)
                    if j == ATTEND_AT and not first:
                        attend(c - 1)
                    if j == FINISH_AT and not first:
                        finish1(c - 1)
                    if j == PREFILL_AT - 2:
                        dve.wait_ge(sem("r_raw"), c * HEADS + HEADS)
                        dve.tensor_copy(r_now, r_nat[:, bass.ds(c * Q1 + Q1, Q1), :]).then_inc(sem("r_now_ready"), 1)

            chunk1(0, True)
            link.straight()
            with dve.Fori(1, C1) as c:
                chunk1(c, False)
            link.leave(C1 - 1)
            attend(C1 - 1)
            finish1(C1 - 1)
            link.straight()

            def split_sup(g, ready):
                tile4 = slice(4 * g, 4 * g + 4)
                link(dve.tensor_copy(sup_h[:, tile4, :], sup[:, tile4, :]))
                dve.tensor_tensor(sup_l[:, tile4, :], sup[:, tile4, :], sup_h[:, tile4, :].bitcast(F32),
                                  ALU.subtract).then_inc(ready, 1)

            def split_low(layer, c, j):
                if not pool_splits(j):
                    dve.wait_ge(sem("high_ready"), c * NT + ((layer - 2) * LOADS + j + 1))
                    dve.tensor_tensor(adj_l[:, j % N_SPLIT, :], ring[:, j % RING, :], adj_h[:, j % N_SPLIT, :].bitcast(F32),
                                      ALU.subtract).then_inc(sem("low_ready"), 1)

            def layer_loop(layer, finish, rate):
                for j in range(NT):
                    split_low(layer, 0, j)
                with dve.Fori(1, C1) as c:
                    link.body(c - 1, rate)
                    for j in range(NT):
                        split_low(layer, c, j)
                        finish(c - 1, j)
                link.leave(C1 - 1)
                for j in range(NT):
                    finish(C1 - 1, j)
                link.straight()

            dve.sem_inc(sem("turn_taken"), 1)
            dve.wait_ge(sem("x2_ready"), C1)
            dve.wait_ge(sem("dis_ready"), 1)
            for g in range(NT // 4):
                dve.wait_ge(sem("sup_raw"), g + 1)
                dve.tensor_tensor(sup[:, 4 * g:4 * g + 4, :], tiles(TURN + g % 2),
                                  dis[:, 4 * g:4 * g + 4].unsqueeze(2).broadcast_to([P, 4, D]),
                                  ALU.mult).then_inc(sem("sup_taken"), 1)
                dve.wait_ge(sem("sup_taken"), g + 1)
                split_sup(g, sem("sup_ready"))
            dve.sem_inc(sem("low_ready"), RING - RING // 4)
            dve.sem_inc(sem("mx_summed"), 2)
            link.straight()

            def finish2(c, j):
                rows = bass.ds(c * Q1, Q1)
                if j == AT2_ADD:
                    dve.wait_ge(sem("s2_turned"), c + 1)
                    dve.tensor_tensor(xo2[:], tiles8(TURN), sup[:, rows, :], ALU.add).then_inc(sem("turn_taken"), 1)
                    dve.wait_ge(sem("turn_taken"), c + 2)
                    link(dve.tensor_tensor(xo2[:], xo2[:], dis[:, rows].unsqueeze(2).broadcast_to([P, Q1, D]), ALU.mult))
                    flat = lambda v: v.rearrange("p q d -> p (q d)")
                    link(dve.scalar_tensor_tensor(out=flat(xo2[:]), in0=flat(xo2[:]), scalar=0.0, in1=flat(xa[:, rows, :]),
                                                  op0=ALU.max, op1=ALU.add))
                if j == AT2_STATS:
                    stats(ln_st, ln_mv, xo2, Q1, sem("x3_stats"))
                if j == AT2_NORM:
                    dve.wait_ge(sem("x3_rstd"), c + 1)
                    normalise(lambda q: xb[:, bass.ds(c * Q1 + q, 1), :].rearrange("p a d -> p (a d)"),
                              xo2, ln_mv, ln_rs, Q1, sem("x3_ready"))
                if j == AT2_SQUARES:
                    dve.wait_ge(sem("x3_ready"), c + 1)
                    link(dve.tensor_tensor(rl[:], xb[:, rows, :], xb[:, rows, :], ALU.mult))
                    link(dve.tensor_reduce(sums[:, rows], rl[:], AX_X, ALU.add))

            layer_loop(2, finish2, RATE2)

            dve.sem_inc(sem("rl_used"), 1)
            per_row = lambda v: v.unsqueeze(2).broadcast_to([P, 4, D])
            link.mark(dve.memset(arg[:], 0.0))
            for g in range(NT // 4):
                dve.wait_ge(sem("mx_ready"), g + 1)
                dve.tensor_reduce(sums[:, NT + 4 * g:NT + 4 * g + 4], sq[:, g % 2, 0:4, :], AX_X,
                                  ALU.add).then_inc(sem("mx_summed"), 1)
            dve.wait_ge(sem("dots_raw"), NT // 4)
            link.mark(dve.tensor_copy(dots[:], ps[:, ACC, 0:NT]))
            dve.wait_ge(sem("mx_summed"), NT // 4 + 2)
            dve.wait_ge(sem("sums_ready"), 1)
            dve.tensor_scalar(sums[:], sums[:], MIN_SQ, None, ALU.max).then_inc(sem("sums_floor"), 1)
            dve.wait_ge(sem("norms_ready"), 1)
            xn, mxn, bn = norms[:, 0:NT], norms[:, NT:2 * NT], norms[:, 2 * NT:]
            link.mark(dve.reciprocal(recips[:], norms[:]))
            dve.tensor_scalar(clipped[:], xn, ATANH_MAX, None, ALU.min).then_inc(sem("clipped_ready"), 1)
            link.wait()
            link.mark(dve.tensor_copy(arg[:, NT:], bn))
            link(dve.tensor_tensor(tmp[:, 0:NT], mxn, recips[:, 0:NT], ALU.mult))
            dve.wait_ge(sem("atanh_ln"), 1)
            link(dve.tensor_tensor(arg[:, 0:NT], ln_plus[:, 0:NT], ln_minus[:, 0:NT], ALU.subtract))
            dve.scalar_tensor_tensor(out=arg[:, 0:NT], in0=arg[:, 0:NT], scalar=0.5, in1=tmp[:, 0:NT],
                                     op0=ALU.mult, op1=ALU.mult).then_inc(sem("tanh_in"), 1)
            dve.wait_ge(sem("tanh_exp"), 1)
            link.mark(dve.tensor_scalar(tanh[:], tanh_e[:], -1.0, 1.0, ALU.mult, ALU.add))
            link(dve.tensor_scalar(tmp[:], tanh_e[:], 1.0, None, ALU.add))
            link(dve.reciprocal(tmp[:], tmp[:]))
            link.mark(dve.tensor_tensor(tanh[:], tanh[:], tmp[:], ALU.mult))
            link.mark(dve.tensor_tensor(gap[:], tanh_e[:], tmp[:], ALU.mult))
            link.wait()
            link.mark(dve.tensor_scalar(tanh[:], tanh[:], MAX_NORM, None, ALU.min))
            link(dve.scalar_tensor_tensor(out=gap[:], in0=gap[:], scalar=4.0, in1=tmp[:], op0=ALU.mult, op1=ALU.mult))
            link.mark(dve.tensor_scalar(gap[:], gap[:], LEAST_GAP, None, ALU.max))
            link.mark(dve.tensor_tensor(sq_norm[:], tanh[:], tanh[:], ALU.mult))
            link(dve.tensor_tensor(tmp[:], tanh[:], recips[:, NT:], ALU.mult))
            alpha, cb = tmp[:, 0:NT], tmp[:, NT:]
            x_sq, y_sq = sq_norm[:, 0:NT], sq_norm[:, NT:]
            link.mark(dve.tensor_scalar(hyp_bias[:], bias3[:], cb, None, ALU.mult))
            link(dve.tensor_scalar(dots[:], dots[:], cb, 2.0, ALU.mult, ALU.mult))
            link(dve.tensor_tensor(dots[:], dots[:], alpha, ALU.mult))
            link(dve.tensor_scalar(dots[:], dots[:], 1.0, None, ALU.add))
            link(dve.scalar_tensor_tensor(out=r_den[:], in0=x_sq, scalar=y_sq, in1=dots[:], op0=ALU.mult, op1=ALU.add))
            link(dve.tensor_scalar(r_den[:], r_den[:], 1e-15, None, ALU.max))
            link(dve.reciprocal(r_den[:], r_den[:]))
            link.mark(dve.scalar_tensor_tensor(out=cx[:], in0=dots[:], scalar=y_sq, in1=r_den[:], op0=ALU.add, op1=ALU.mult))
            link(dve.tensor_tensor(cy[:], gap[:, 0:NT], r_den[:], ALU.mult))
            link(dve.tensor_scalar(gap2[:], cy[:], gap[:, NT:], None, ALU.mult))
            link(dve.tensor_scalar(norm2[:], gap2[:], -1.0, 1.0, ALU.mult, ALU.add))
            link.mark(dve.tensor_scalar(gap2[:], gap2[:], LEAST_GAP, None, ALU.max))
            link.mark(dve.tensor_tensor(cx[:], cx[:], alpha, ALU.mult))
            link.wait()
            dve.tensor_scalar(norm2[:], norm2[:], FLAT_SQ, None, ALU.max).then_inc(sem("norm2_sq"), 1)
            dve.wait_ge(sem("norm2_ready"), 1)
            dve.tensor_scalar(clip2[:], norm2[:], MAX_NORM, None, ALU.min).then_inc(sem("clip2_ready"), 1)
            dve.wait_ge(sem("atanh2_ln"), 1)
            link(dve.scalar_tensor_tensor(out=ln_plus2[:], in0=ln_gap2[:], scalar=-0.5, in1=ln_plus2[:],
                                          op0=ALU.mult, op1=ALU.add))
            link(dve.tensor_tensor(ln_plus2[:], ln_plus2[:], by_norm2[:], ALU.mult))
            link.mark(dve.tensor_tensor(cx[:], cx[:], ln_plus2[:], ALU.mult))
            link(dve.tensor_tensor(cy[:], cy[:], ln_plus2[:], ALU.mult))
            for g in range(NT // 4):
                tile4 = slice(4 * g, 4 * g + 4)
                link.mark(dve.tensor_tensor(sup[:, tile4, :], sup[:, tile4, :], per_row(cx[:, tile4]), ALU.mult))
                link(dve.tensor_tensor(bias_part[:], hyp_bias[:].unsqueeze(1).broadcast_to([P, 4, D]),
                                       per_row(cy[:, tile4]), ALU.mult))
                link(dve.tensor_tensor(sup[:, tile4, :], sup[:, tile4, :], bias_part[:], ALU.add))
                split_sup(g, sem("xt_ready"))
            link.straight()

            def finish3(c, j):
                rows = bass.ds(c * Q1, Q1)
                if j == AT3_SUMS:
                    dve.wait_ge(sem("sq_ready"), c + 1)
                    link(dve.tensor_reduce(f_sq[:], sq[:], AX_X, ALU.add))
                    dve.tensor_scalar(f_sq[:], f_sq[:], MIN_SQ, None, ALU.max).then_inc(sem("f_sq_ready"), 1)
                if j == AT3_ARG:
                    dve.wait_ge(sem("f_norm_ready"), c + 1)
                    link.mark(dve.tensor_scalar(f_k[:], f_norm[:, 0, :], ATANH_OF_MAX, None, ALU.min))
                    link(dve.reciprocal(f_recip[:], f_norm[:]))
                    link(dve.tensor_tensor(f_k[:], f_k[:], f_recip[:, 0, :], ALU.mult))
                    dve.tensor_tensor(f_arg[:], f_k[:], f_norm[:, 1, :], ALU.mult).then_inc(sem("f_arg_ready"), 1)
                if j == AT3_ADD:
                    dve.wait_ge(sem("f_exp"), c + 1)
                    link.mark(dve.tensor_scalar(f_k[:], f_tanh[:], 1.0, None, ALU.add))
                    link(dve.tensor_scalar(f_tanh[:], f_tanh[:], -1.0, 1.0, ALU.mult, ALU.add))
                    link(dve.reciprocal(f_k[:], f_k[:]))
                    link(dve.tensor_tensor(f_tanh[:], f_tanh[:], f_k[:], ALU.mult))
                    link(dve.scalar_tensor_tensor(out=f_tanh[:], in0=f_tanh[:], scalar=MAX_NORM, in1=f_recip[:, 1, :],
                                                  op0=ALU.min, op1=ALU.mult))
                    link(dve.tensor_tensor(xo3[:], rl[:], f_tanh[:].unsqueeze(2).broadcast_to([P, Q1, D]), ALU.mult))
                    dve.tensor_tensor(xo3[:], xo3[:], xb[:, rows, :], ALU.add).then_inc(sem("rl_used"), 1)
                    dve.wait_ge(sem("rl_used"), c + 2)
                if j == AT3_STATS:
                    stats(ln_st, ln_mv, xo3, Q1, sem("x4_stats"))
                if j == AT3_NORM:
                    dve.wait_ge(sem("x4_rstd"), c + 1)
                    normalise(lambda q: xa[:, bass.ds(c * Q1 + q, 1), :].rearrange("p a d -> p (a d)"),
                              xo3, ln_mv, ln_rs, Q1, sem("x4_ready"))

            layer_loop(3, finish3, RATE3)

        @block.tensor
        def _(pe):
            pe.sem_inc(sem("y_summed"), N_PAIR)

            def aggregate(c, j):
                r = j // 2
                if j % 2 == 0:
                    pe.wait_ge(sem(f"adj_in{r % RING}"), at(c, 16 * NT // 2 // RING, 16 * (r // RING + 1)))
                ins = pe.matmul(ps[:, AX, :], xa[:, j, :], ring[:, r % RING, j % 2 * T0:(j % 2 + 1) * T0],
                                start=j == 0, stop=j == NT - 1)
                if j % 2 == 1:
                    ins.then_inc(sem("adj_free"), 1)

            def prepare(n, i):
                half = n[1] % 2
                if i == AT_GCN:
                    pe.wait_ge(sem("ax_taken"), at(n, 1, 1))
                    for q in range(Q0):
                        ins = pe.matmul(tiles(M1)[:, q, :], ax_t[:, q * P:(q + 1) * P], gcn_w[:], start=True, stop=True)
                    ins.then_inc(sem("g_ready"), 1)
                if i == AT_TURN:
                    pe.wait_ge(sem("h_norm_ready"), at(n, 1, 1))
                    for q in range(Q0):
                        ins = pe.transpose(tiles(M0)[:, q, :], h_norm[:, q, :], ident[:])
                    ins.then_inc(sem("h_turned"), 1)
                if i in (AT_XC, AT_Z):
                    for k in range(KD):
                        m = k if i == AT_XC else KD + k
                        if i == AT_XC:
                            pe.wait_ge(sem("h_t_ready"), at(n, 1, 1))
                            pe.wait_ge(sem("out_taken"), at(n, 1, 1))
                        else:
                            pe.wait_ge(sem("xc_ready"), at(n, KD, k + 1))
                        pe.matmul(ps[:, M0 + k, :], w_in[:, m * P:(m + 1) * P], ax_t[:], start=True,
                                  stop=True).then_inc(sem("xz_ready"), 1)
                if i == AT_BC:
                    pe.wait_ge(sem("z_ready"), at(n, KD, KD))
                    pe.wait_ge(sem("u_ready"), at(n, KD, KD))
                    for k in range(KD):
                        ins = pe.matmul(ps[0:RANK, M1, :], w_r[:, k, :], u[:, half, k, :], start=k == 0, stop=k == KD - 1)
                    ins.then_inc(sem("rank_ready"), 1)
                    for k in range(KD):
                        ins = pe.matmul(ps[0:96, M0, :], w_bc[:, k, :], u[:, half, k, :], start=k == 0, stop=k == KD - 1)
                    ins.then_inc(sem("bc_raw"), 1)
                if i == AT_DT_RAW:
                    pe.wait_ge(sem("rank_taken"), at(n, 1, 1))
                    pe.wait_ge(sem("bc_taken"), at(n, 1, 1))
                    for k in range(KD):
                        pe.matmul(ps[:, M0 + k, :], w_dt[:, k * P:(k + 1) * P], rank_t[:], start=True,
                                  stop=True).then_inc(sem("dt_raw"), 1)

            def finish0(c):
                pe.wait_ge(sem("gated"), at(c, KD, KD))
                for q in range(Q0):
                    for k in range(KD):
                        ins = pe.matmul(tiles(M1)[:, q, :], yg[:, k, q * P:(q + 1) * P], w_out[:, k, :],
                                        start=k == 0, stop=k == KD - 1)
                ins.then_inc(sem("out_ready"), 1)

            def b_row(c, n):
                pe.wait_ge(sem("dbu_ready"), at(c, STEPS, KD * n + KD))
                pe.matmul(ps[:, BB + n % 2, :], pick[:, n % S_N, :], bc_parts[:, (c[1] + n // S_N) % 2, :], start=True,
                          stop=True).then_inc(sem("b_bcast"), 1)

            def c_row(c, n):
                pe.wait_ge(sem("c_rows"), at(c, S_N, n + 1))
                pe.matmul(ps[:, CB, :], pick[:, S_N + n % S_N, :], bc_parts[:, (c[1] + n // S_N) % 2, :], start=True,
                          stop=True).then_inc(sem("c_bcast"), 1)

            def sum_y(c, i):
                n, k = divmod(i, KD)
                m = n // 2 * KD + k
                if n % 2 == 1:
                    pe.wait_ge(sem("pair_ready"), at(c, PAIRS, PAIR_CREDIT + m + 1))
                    ins = pe.matmul(ps[:, Y + k, :], ident[:], hc[:, m % N_PAIR, :], start=n == 1, stop=n == S_N - 1)
                    ins.then_inc(sem("y_summed"), 1)

            def chunk0(c):
                for i in range(STEPS):
                    n, k = divmod(i, KD)
                    if n + 1 < S_N or has_next(c):
                        if k == 0:
                            b_row(c, n + 1)
                        else:
                            c_row(c, n + 1)
                    if has_next(c) and has_next(neighbour(c, 1)):
                        if i == 0:
                            pe.wait_ge(sem("ax_taken"), at(c, 1, 2))
                        aggregate(neighbour(c, 2), i)
                    if has_next(c):
                        prepare(neighbour(c, 1), i)
                    if i == STEPS - 3 and has_next(c):
                        pe.wait_ge(sem("bc_split"), at(c, 1, 2))
                    if i == AT_OUT and has_previous(c):
                        finish0(neighbour(c, -1))
                    if i >= Y_LAG:
                        sum_y(c, i - Y_LAG)
                    elif has_previous(c):
                        sum_y(neighbour(c, -1), STEPS - Y_LAG + i)

            for j in range(NT):
                if j % (NT // X_PARTS) == 0:
                    pe.wait_ge(sem(f"x_in{j * X_PARTS // NT}"), 16)
                aggregate((0, 0), j)
            pe.wait_ge(sem("setup"), setup_all)
            pe.wait_ge(sem("consts"), 1)
            pe.wait_ge(sem("ax_taken"), 1)
            for i in range(STEPS):
                prepare((0, 0), i)
                aggregate((0, 1), i)
            pe.wait_ge(sem("bc_split"), 1)
            b_row((0, 0), 0)
            c_row((0, 0), 0)
            chunk0(FIRST)
            with pe.Fori(0, LOOPS0) as pair:
                for c in in_loop(pair):
                    chunk0(c)
            for c in AFTER:
                chunk0(c)
            for i in range(STEPS - Y_LAG, STEPS):
                sum_y(AFTER[-1], i)
            finish0(AFTER[-1])

            for g in range(NT // 4):
                pe.wait_ge(sem("x1_ready"), g * 4 // Q0 + 1)
                if g >= 2:
                    pe.wait_ge(sem("x1_t_ready"), g - 1)
                for q in range(4):
                    ins = pe.transpose(ps[:, NAT + g % 2, q * P:(q + 1) * P], xb[:, 4 * g + q, :], ident[:])
                ins.then_inc(sem("x1_turned"), 1)
            pe.matmul(ps[:, RAW, 0:2 * HEADS], w1_t[:], a_bd[:], start=True, stop=True).then_inc(sem("wa_raw"), 1)
            pe.wait_ge(sem("w1_cat_ready"), 1)
            pe.wait_ge(sem("x1_t_ready"), NT // 4)
            cols = D + 2 * HEADS
            for g in range(NT // 2):
                if g >= 2:
                    pe.wait_ge(sem("h_taken"), g - 1)
                for q in range(2):
                    j = 2 * g + q
                    ins = pe.matmul(ps[:, NAT + g % 2, q * cols:(q + 1) * cols], x_t[:, j * P:(j + 1) * P],
                                    w1_cat[:], start=True, stop=True)
                ins.then_inc(sem("h_raw"), 1)
            pe.wait_ge(sem("h_taken"), NT // 2)
            pe.sem_inc(sem("den_summed"), N_S)
            pe.sem_inc(sem("num_summed"), NUM_CREDIT)

            def fill(h):
                for q in range(Q1):
                    ins = pe.matmul(tiles8(RAW if h % 2 else NAT)[:, q, :], r_now[:, q, h:h + 1].broadcast_to([P, P]),
                                    ident[:], start=True, stop=True)
                ins.then_inc(sem("r_raw"), 1)

            def turn1(c):
                for q in range(Q1):
                    ins = pe.transpose(tiles8(NAT)[:, q, :], den_raw[:, q * P:(q + 1) * P], ident[:])
                ins.then_inc(sem("den_turned"), 1)
                for q in range(Q1):
                    ins = pe.transpose(tiles8(RAW)[:, q, :], num_raw[:, q * P:(q + 1) * P], ident[:])
                ins.then_inc(sem("num_turned"), 1)

            def chunk1(c, first):
                if not first:
                    pe.wait_ge(sem("sums_taken"), c * 2)
                for j in range(NT):
                    start, end = j == 0, j == NT - 1
                    pe.wait_ge(sem(f"adj_in{j % RING}"), c * (16 * NT // RING) + 16 * (LOADS // RING + j // RING + 1))
                    for b in range(2):
                        adj = ring[:, j % RING, b * BANK:(b + 1) * BANK]
                        for h in range(DVE_HEADS, HEADS):
                            pe.matmul(ps[F * h:F * (h + 1), NUM + b, :], dh[:, j, F * (h - DVE_HEADS):F * (h - DVE_HEADS + 1)],
                                      adj, start=start, stop=False)
                        pe.matmul(ps[0:F, DEN + b, :], deg_col[:], adj, start=start, stop=False)
                    if j == NT - 2:
                        pe.wait_ge(sem("r_taken"), c * 3 + 4)
                        fill(0)
                    if end:
                        pe.wait_ge(sem("r_taken"), c * 3 + 5)
                        fill(1)
                    pe.wait_ge(sem("w_ready"), c * NT + (j + 2))
                    pe.wait_ge(sem("v_ready"), c * NT + (j + 1))
                    for b in range(2):
                        cols = slice(b * BANK, (b + 1) * BANK)
                        for h in range(HEADS):
                            moving = w_ring[:, j % N_W, h, cols] if h < DVE_HEADS else v_ring[:, j % N_V, h - DVE_HEADS, cols]
                            ins = pe.matmul(ps[F * h:F * (h + 1), NUM + b, :], bh[:, j, F * h:F * (h + 1)],
                                            moving, start=start and h < DVE_HEADS, stop=end)
                    ins.then_inc(sem("num_summed"), 1)
                    pe.wait_ge(sem("masked"), c * NT + (j + 1))
                    pe.wait_ge(sem("sign_ready"), c * NT + (j + 2))
                    pe.sem_inc(sem("pe_settled"), 1)
                    for b in range(2):
                        cols = slice(b * BANK, (b + 1) * BANK)
                        order = (0, 1, 2, 3) if b == 0 else (1, 2, 3, 0)
                        for h in order:
                            pe.matmul(ps[F * h:F * (h + 1), DEN + b, :], stat_s[:, j, h, :], s8[:, j % N_S, h, cols],
                                      start=start and h > 0, stop=end and h != b)
                        ins = pe.matmul(ps[F * b:F * (b + 1), DEN + b, :], stat_m[:, j, :], m1[:, j % N_S, cols],
                                        start=False, stop=end)
                    ins.then_inc(sem("den_summed"), 1)
                    if j == TURN_AT and not first:
                        turn1(c - 1)
                    if j == PREFILL_AT:
                        pe.wait_ge(sem("r_now_ready"), c + 2)
                        if not first:
                            pe.wait_ge(sem("den_used"), c)
                            pe.wait_ge(sem("x_taken"), c + 1)
                        fill(2)
                        fill(3)

            pe.wait_ge(sem("r_now_ready"), 1)
            fill(2)
            fill(3)
            pe.wait_ge(sem("r_taken"), 1)
            fill(0)
            pe.wait_ge(sem("r_taken"), 2)
            fill(1)
            pe.wait_ge(sem("bh_ready"), 1)
            chunk1(0, True)
            with pe.Fori(1, C1) as c:
                chunk1(c, False)
            pe.wait_ge(sem("sums_taken"), 2 * C1)
            pe.wait_ge(sem("r_taken"), 3 * C1 + 2)
            turn1(C1 - 1)

            def prepare(layer, x, ready, w, raw, taken):
                def turn(g):
                    pe.wait_ge(sem(ready), g * 4 // Q1 + 1)
                    if g >= 2:
                        pe.wait_ge(sem(f"x_t_ready_{layer}"), g - 1)
                    for q in range(4):
                        ins = pe.transpose(ps[:, PREP + g % 2, q * P:(q + 1) * P], x[:, 4 * g + q, :], ident[:])
                    ins.then_inc(sem(f"x_turned_{layer}"), 1)

                def product(g):
                    pe.wait_ge(sem(f"x_t_ready_{layer}"), g + 1)
                    if g >= 2:
                        pe.wait_ge(sem(taken), g - 1)
                    for q in range(4):
                        ins = pe.matmul(tiles(TURN + g % 2)[:, q, :], x2_t[:, (4 * g + q) * P:(4 * g + q + 1) * P],
                                        w[:], start=True, stop=True)
                    ins.then_inc(sem(raw), 1)

                turn(0)
                for g in range(NT // 4):
                    if g + 1 < NT // 4:
                        turn(g + 1)
                    product(g)
                    if layer == 3:
                        for j in range(4 * g, 4 * g + 4):
                            ins = pe.matmul(ps[:, ACC, j:j + 1], x2_t[:, j * P:(j + 1) * P], w3b[:], start=True, stop=True)
                        ins.then_inc(sem("dots_raw"), 1)

            def aggregate_all(layer, c, first, ready, turned, free):
                for j in range(NT):
                    start, end = j == 0, j == NT - 1
                    if j % 4 == 0:
                        pe.wait_ge(sem(ready), j // 4 + 1)
                    if start and not first:
                        pe.wait_ge(sem(f"acc_taken_{layer}"), c)
                    pe.wait_ge(sem("high_ready"), c * NT + ((layer - 2) * LOADS + j + 1))
                    cols = [slice(b * BANK, (b + 1) * BANK) for b in range(2)]
                    for stat in (sup_h, sup_l):
                        for b in range(2):
                            pe.matmul(ps[:, ACC + b, :], stat[:, j, :], adj_h[:, j % N_SPLIT, cols[b]],
                                      start=start and stat is sup_h, stop=False)
                    name, value = low_count(layer, c, j)
                    pe.wait_ge(sem(name), value)
                    for b in range(2):
                        ins = pe.matmul(ps[:, ACC + b, :], sup_h[:, j, :], adj_l[:, j % N_SPLIT, cols[b]],
                                        start=False, stop=end)
                    ins.then_inc(sem("split_used"), 1)
                    if j == TURN2_AT and not first:
                        turn_out(layer, c - 1, turned, free)

            def turn_out(layer, c, turned, free):
                pe.wait_ge(sem(free), c + 1)
                pe.wait_ge(sem(f"acc_taken_{layer}"), c + 1)
                for q in range(Q1):
                    ins = pe.transpose(tiles8(TURN)[:, q, :], acc[:, q * P:(q + 1) * P], ident[:])
                ins.then_inc(sem(turned), 1)

            def layer_loop(layer, *names):
                aggregate_all(layer, 0, True, *names)
                with pe.Fori(1, C1) as c:
                    aggregate_all(layer, c, False, *names)
                turn_out(layer, C1 - 1, *names[1:])

            pe.wait_ge(sem("den_used"), C1)
            pe.wait_ge(sem("x_taken"), C1 + 1)
            prepare(2, xa, "x2_ready", w2_t, "sup_raw", "sup_taken")

            pe.sem_inc(sem("split_used"), N_SPLIT)
            layer_loop(2, "sup_ready", "s2_turned", "turn_taken")

            pe.wait_ge(sem("turn_taken"), C1 + 1)
            pe.matmul(ps[:, ACC + 1, 0:1], w3[:], bias3_col[:], start=True, stop=True).then_inc(sem("w3b_raw"), 1)
            pe.wait_ge(sem("w3b_ready"), 1)
            prepare(3, xb, "x3_ready", w3_t, "mx_raw", "mx_ready")

            layer_loop(3, "xt_ready", "s_turned", "turn3_taken")


_VECTORS = {"gcn_b": "L0_gnn_gcn_b", "ln_g": "L0_gnn_ln_g", "ln_b": "L0_gnn_ln_b", "gcn_w": "L0_gnn_gcn_w",
            "w_in": "L0_gnn_w_in", "conv_w": "L0_gnn_conv_w", "conv_b": "L0_gnn_conv_b", "w_dt": "L0_gnn_w_dt",
            "b_dt": "L0_gnn_b_dt", "a_log": "L0_gnn_A_log", "d_skip": "L0_gnn_D_skip", "w_out": "L0_gnn_w_out"}


def kernel(**inputs):
    import numpy as np
    import concourse.bacc as bacc
    from concourse.bass_utils import run_bass_kernel_spmd

    arrays = {k: inputs[name] for k, name in _VECTORS.items()}
    for k in ("conv_b", "b_dt", "d_skip"):
        arrays[k] = arrays[k].reshape(KD, P).T
    arrays["x"] = inputs["x"]
    arrays["adj_t"] = inputs["adj"].T
    w_xp = inputs["L0_gnn_w_xp"]
    arrays["w_r"] = w_xp[:, 0:RANK]
    arrays["w_bc"] = np.concatenate([w_xp[:, RANK:]] * PARTS, axis=1)
    arrays["w1"] = inputs["L1_gnn_W"]
    arrays["w1_t"] = inputs["L1_gnn_W"].T
    arrays["w2_t"] = inputs["L2_gnn_W"].T
    arrays["w3"] = inputs["L3_gnn_weight"]
    arrays["w3_t"] = inputs["L3_gnn_weight"].T
    arrays["bias3"] = inputs["L3_gnn_bias"]
    a_bd = np.zeros((D, 2 * HEADS), np.float32)
    for h in range(HEADS):
        rows = slice(F * h, F * (h + 1))
        a_bd[rows, h] = inputs["L1_gnn_a_dst"][h]
        a_bd[rows, HEADS + h] = inputs["L1_gnn_a_src"][h]
    arrays["a_bd"] = a_bd
    arrays["ident"] = np.eye(P, dtype=np.float32)
    arrays["row_is"] = np.tile(np.eye(32, dtype=np.float32), (PARTS, 1))
    arrays = {k: np.ascontiguousarray(a) for k, a in arrays.items()}
    nc = bacc.Bacc("TRN2", target_bir_lowering=False, num_devices=1)
    t = {k: nc.dram_tensor(f"in_{k}", a.shape, mybir.dt.from_np(a.dtype), kind="ExternalInput").ap()
         for k, a in arrays.items()}
    out = nc.dram_tensor("out_x", (N, D), F32, kind="ExternalOutput").ap()
    build_program(nc, t, out)
    r = run_bass_kernel_spmd(nc, [{f"in_{k}": a for k, a in arrays.items()}], core_ids=[0])
    return r.results[0]["out_x"]
```
